# Optimizing a Trainium2 kernel written in Bass

```python
import numpy as np
import jax
import jax.numpy as jnp

def _softmax(x, axis=-1):
    return jax.nn.softmax(x, axis=axis)

def _gelu(x):
    return jax.nn.gelu(x, approximate=True)

def _silu(x):
    return jax.nn.silu(x)

def _sigmoid(x):
    return jax.nn.sigmoid(x)

def _layernorm(x, axis=-1, eps=1e-05):
    m = jnp.mean(x, axis=axis, keepdims=True)
    v = jnp.var(x, axis=axis, keepdims=True)
    return (x - m) / jnp.sqrt(v + eps)

def _scatter_add(tgt, idx, src, axis=0):
    return tgt.at[idx].add(src)

def _segment_sum(src, seg, n):
    return jax.ops.segment_sum(src, seg, n)
kernel_name = 'mk_sandwich_d2_jaxref_r8_66e998'

def setup_inputs(seed: int=0):
    np.random.seed(seed)
    _w = jnp.asarray

    def _L0_attn_setup():
        import jax, jax.numpy as jnp
        import numpy as np
        import math
        EMBED_DIM = 256
        NUM_Q_HEADS = 32
        NUM_KV_HEADS = 8
        HEAD_DIM = EMBED_DIM // NUM_Q_HEADS
        GROUP = NUM_Q_HEADS // NUM_KV_HEADS
        THETA = 10000.0

        def _rope_tables(T, D):
            dim_half = D // 2
            inv_freq = 1.0 / THETA ** (jnp.arange(dim_half, dtype=jnp.float32) / dim_half)
            freqs = jnp.arange(T, dtype=jnp.float32)[:, None] * inv_freq[None, :]
            return (jnp.cos(freqs), jnp.sin(freqs))

        def _apply_rope(x, cos, sin):
            B, H, T, D = x.shape
            xp = x.reshape(B, H, T, D // 2, 2)
            xr, xi = (xp[..., 0], xp[..., 1])
            c = cos[None, None, :, :]
            s = sin[None, None, :, :]
            or_ = xr * c - xi * s
            oi_ = xr * s + xi * c
            return jnp.stack([or_, oi_], axis=-1).reshape(B, H, T, D)
        key = jax.random.key(seed)
        ks = jax.random.split(key, 5)
        B, T, C = (2, 256, EMBED_DIM)
        kvC = NUM_KV_HEADS * HEAD_DIM
        x = jax.random.normal(ks[0], (B, T, C), dtype=jnp.float32)
        Wq = jax.random.normal(ks[1], (C, C), dtype=jnp.float32) * 0.02
        Wk = jax.random.normal(ks[2], (kvC, C), dtype=jnp.float32) * 0.02
        Wv = jax.random.normal(ks[3], (kvC, C), dtype=jnp.float32) * 0.02
        Wo = jax.random.normal(ks[4], (C, C), dtype=jnp.float32) * 0.02
        return {'x': x, 'Wq': Wq, 'Wk': Wk, 'Wv': Wv, 'Wo': Wo}
    _L0_attn_in = _L0_attn_setup()

    def _L0_ffn_setup():
        import jax, jax.numpy as jnp
        import numpy as np
        HIDDEN = 256
        INTER = 704
        B, S = (2, 256)

        def _ternary(key, shape):
            return jax.random.randint(key, shape, -1, 2).astype(jnp.float32)
        key = jax.random.key(seed)
        ks = jax.random.split(key, 7)
        x = jax.random.normal(ks[0], (B, S, HIDDEN), dtype=jnp.float32)
        gate_w = _ternary(ks[1], (INTER, HIDDEN))
        up_w = _ternary(ks[2], (INTER, HIDDEN))
        down_w = _ternary(ks[3], (HIDDEN, INTER))
        gate_s = jax.random.uniform(ks[4], (INTER,), minval=0.01, maxval=0.1, dtype=jnp.float32)
        up_s = jax.random.uniform(ks[5], (INTER,), minval=0.01, maxval=0.1, dtype=jnp.float32)
        down_s = jax.random.uniform(ks[6], (HIDDEN,), minval=0.01, maxval=0.1, dtype=jnp.float32)
        return {'x': x, 'gate_w': gate_w, 'up_w': up_w, 'down_w': down_w, 'gate_s': gate_s, 'up_s': up_s, 'down_s': down_s}
    _L0_ffn_in = _L0_ffn_setup()

    def _L1_attn_setup():
        import jax, jax.numpy as jnp
        import numpy as np
        B, T, C = (4, 256, 256)
        D_ATT, D_FFN = (256, 1024)
        EPS = 1e-05

        def layer_norm(x, w, b):
            mu = jnp.mean(x, axis=-1, keepdims=True)
            var = jnp.var(x, axis=-1, keepdims=True)
            return (x - mu) * jax.lax.rsqrt(var + EPS) * w + b

        def time_shift(x):
            return jnp.pad(x, ((0, 0), (1, 0), (0, 0)))[:, :-1]

        def wkv(time_decay, time_first, k, v):
            decay = -jnp.exp(time_decay)
            kT = jnp.swapaxes(k, 0, 1)
            vT = jnp.swapaxes(v, 0, 1)

            def step(carry, kv_t):
                aa, bb, pp = carry
                kt, vt = kv_t
                ww = time_first + kt
                p = jnp.maximum(pp, ww)
                e1 = jnp.exp(pp - p)
                e2 = jnp.exp(ww - p)
                out = (e1 * aa + e2 * vt) / (e1 * bb + e2)
                ww2 = pp + decay
                p2 = jnp.maximum(ww2, kt)
                e1b = jnp.exp(ww2 - p2)
                e2b = jnp.exp(kt - p2)
                return ((e1b * aa + e2b * vt, e1b * bb + e2b, p2), out)
            z = jnp.zeros((k.shape[0], k.shape[2]), k.dtype)
            init = (z, z, jnp.full_like(z, -1e+38))
            _, outT = jax.lax.scan(step, init, (kT, vT))
            return jnp.swapaxes(outT, 0, 1)
        key = jax.random.key(seed)
        ks = jax.random.split(key, 20)
        n = lambda k, s, sc=0.02: jax.random.normal(k, s, dtype=jnp.float32) * sc
        u = lambda k, s: jax.random.uniform(k, s, dtype=jnp.float32)
        return {'x': jax.random.normal(ks[0], (B, T, C), dtype=jnp.float32), 'ln1_w': jnp.ones((C,), jnp.float32), 'ln1_b': jnp.zeros((C,), jnp.float32), 'ln2_w': jnp.ones((C,), jnp.float32), 'ln2_b': jnp.zeros((C,), jnp.float32), 'tm_k': u(ks[1], (1, 1, C)), 'tm_v': u(ks[2], (1, 1, C)), 'tm_r': u(ks[3], (1, 1, C)), 'time_decay': n(ks[4], (D_ATT,), 1.0), 'time_first': n(ks[5], (D_ATT,), 0.3) + float(np.log(0.3)), 'Wk': n(ks[6], (D_ATT, C)), 'Wv': n(ks[7], (D_ATT, C)), 'Wr': n(ks[8], (D_ATT, C)), 'Wo': n(ks[9], (C, D_ATT)), 'cm_k': u(ks[10], (1, 1, C)), 'cm_r': u(ks[11], (1, 1, C)), 'Wck': n(ks[12], (D_FFN, C)), 'Wcv': n(ks[13], (C, D_FFN)), 'Wcr': n(ks[14], (C, C))}
    _L1_attn_in = _L1_attn_setup()

    def _L1_ffn_setup():
        import jax, jax.numpy as jnp
        import numpy as np
        E = 32
        K = 6
        H = 256
        I = 128
        T = 256
        CAP = 96
        SCALE = 1.5
        SWIGLU_LIMIT = 10.0
        key = jax.random.key(seed)
        ks = jax.random.split(key, 9)

        def s(k, shape, fan):
            return jax.random.normal(k, shape, jnp.float32) * fan ** (-0.5)
        return {'x': jax.random.normal(ks[0], (1, T, H), jnp.float32), 'gate_w': s(ks[1], (E, H), H), 'bias': jax.random.normal(ks[2], (E,), jnp.float32) * 0.01, 'w_gate': s(ks[3], (E, I, H), H), 'w_up': s(ks[4], (E, I, H), H), 'w_down': s(ks[5], (E, H, I), I), 'sg': s(ks[6], (I, H), H), 'su': s(ks[7], (I, H), H), 'sd': s(ks[8], (H, I), I)}
    _L1_ffn_in = _L1_ffn_setup()
    _d = {'L0_attn_x': _L0_attn_in['x'], 'L0_attn_Wq': _L0_attn_in['Wq'], 'L0_attn_Wk': _L0_attn_in['Wk'], 'L0_attn_Wv': _L0_attn_in['Wv'], 'L0_attn_Wo': _L0_attn_in['Wo'], 'L0_ffn_gate_w': _L0_ffn_in['gate_w'], 'L0_ffn_up_w': _L0_ffn_in['up_w'], 'L0_ffn_down_w': _L0_ffn_in['down_w'], 'L0_ffn_gate_s': _L0_ffn_in['gate_s'], 'L0_ffn_up_s': _L0_ffn_in['up_s'], 'L0_ffn_down_s': _L0_ffn_in['down_s'], 'L1_attn_ln1_w': _L1_attn_in['ln1_w'], 'L1_attn_ln1_b': _L1_attn_in['ln1_b'], 'L1_attn_ln2_w': _L1_attn_in['ln2_w'], 'L1_attn_ln2_b': _L1_attn_in['ln2_b'], 'L1_attn_tm_k': _L1_attn_in['tm_k'], 'L1_attn_tm_v': _L1_attn_in['tm_v'], 'L1_attn_tm_r': _L1_attn_in['tm_r'], 'L1_attn_time_decay': _L1_attn_in['time_decay'], 'L1_attn_time_first': _L1_attn_in['time_first'], 'L1_attn_Wk': _L1_attn_in['Wk'], 'L1_attn_Wv': _L1_attn_in['Wv'], 'L1_attn_Wr': _L1_attn_in['Wr'], 'L1_attn_Wo': _L1_attn_in['Wo'], 'L1_attn_cm_k': _L1_attn_in['cm_k'], 'L1_attn_cm_r': _L1_attn_in['cm_r'], 'L1_attn_Wck': _L1_attn_in['Wck'], 'L1_attn_Wcv': _L1_attn_in['Wcv'], 'L1_attn_Wcr': _L1_attn_in['Wcr'], 'L1_ffn_gate_w': _L1_ffn_in['gate_w'], 'L1_ffn_bias': _L1_ffn_in['bias'], 'L1_ffn_w_gate': _L1_ffn_in['w_gate'], 'L1_ffn_w_up': _L1_ffn_in['w_up'], 'L1_ffn_w_down': _L1_ffn_in['w_down'], 'L1_ffn_sg': _L1_ffn_in['sg'], 'L1_ffn_su': _L1_ffn_in['su'], 'L1_ffn_sd': _L1_ffn_in['sd']}
    _x0 = _d['L0_attn_x']
    _d['L0_attn_x'] = jax.random.normal(jax.random.fold_in(jax.random.key(seed), 1), (4, 512, 256), dtype=_x0.dtype)
    del _x0
    return _d

def reference(L0_attn_x, L0_attn_Wq, L0_attn_Wk, L0_attn_Wv, L0_attn_Wo, L0_ffn_gate_w, L0_ffn_up_w, L0_ffn_down_w, L0_ffn_gate_s, L0_ffn_up_s, L0_ffn_down_s, L1_attn_ln1_w, L1_attn_ln1_b, L1_attn_ln2_w, L1_attn_ln2_b, L1_attn_tm_k, L1_attn_tm_v, L1_attn_tm_r, L1_attn_time_decay, L1_attn_time_first, L1_attn_Wk, L1_attn_Wv, L1_attn_Wr, L1_attn_Wo, L1_attn_cm_k, L1_attn_cm_r, L1_attn_Wck, L1_attn_Wcv, L1_attn_Wcr, L1_ffn_gate_w, L1_ffn_bias, L1_ffn_w_gate, L1_ffn_w_up, L1_ffn_w_down, L1_ffn_sg, L1_ffn_su, L1_ffn_sd):

    def _L0_attn_ref(x, Wq, Wk, Wv, Wo):
        import jax, jax.numpy as jnp
        import numpy as np
        import math
        EMBED_DIM = 256
        NUM_Q_HEADS = 32
        NUM_KV_HEADS = 8
        HEAD_DIM = EMBED_DIM // NUM_Q_HEADS
        GROUP = NUM_Q_HEADS // NUM_KV_HEADS
        THETA = 10000.0

        def _rope_tables(T, D):
            dim_half = D // 2
            inv_freq = 1.0 / THETA ** (jnp.arange(dim_half, dtype=jnp.float32) / dim_half)
            freqs = jnp.arange(T, dtype=jnp.float32)[:, None] * inv_freq[None, :]
            return (jnp.cos(freqs), jnp.sin(freqs))

        def _apply_rope(x, cos, sin):
            B, H, T, D = x.shape
            xp = x.reshape(B, H, T, D // 2, 2)
            xr, xi = (xp[..., 0], xp[..., 1])
            c = cos[None, None, :, :]
            s = sin[None, None, :, :]
            or_ = xr * c - xi * s
            oi_ = xr * s + xi * c
            return jnp.stack([or_, oi_], axis=-1).reshape(B, H, T, D)
        B, T, C = x.shape
        Hq, Hkv, D, G = (NUM_Q_HEADS, NUM_KV_HEADS, HEAD_DIM, GROUP)
        scale = 1.0 / math.sqrt(D)
        q = (x @ Wq.T).reshape(B, T, Hq, D).transpose(0, 2, 1, 3)
        k = (x @ Wk.T).reshape(B, T, Hkv, D).transpose(0, 2, 1, 3)
        v = (x @ Wv.T).reshape(B, T, Hkv, D).transpose(0, 2, 1, 3)
        cos, sin = _rope_tables(T, D)
        q = _apply_rope(q, cos, sin)
        k = _apply_rope(k, cos, sin)
        qg = q.reshape(B, Hkv, G, T, D)
        att = jnp.einsum('bhgtd,bhsd->bhgts', qg, k) * scale
        causal = jnp.tril(jnp.ones((T, T), dtype=bool))
        att = jnp.where(causal[None, None, None, :, :], att, -jnp.inf)
        att = jax.nn.softmax(att, axis=-1)
        out = jnp.einsum('bhgts,bhsd->bhgtd', att, v)
        out = out.reshape(B, Hq, T, D).transpose(0, 2, 1, 3).reshape(B, T, C)
        return out @ Wo.T

    def _L0_ffn_ref(x, gate_w, up_w, down_w, gate_s, up_s, down_s):
        import jax, jax.numpy as jnp
        import numpy as np
        HIDDEN = 256
        INTER = 704
        B, S = (2, 256)

        def _ternary(key, shape):
            return jax.random.randint(key, shape, -1, 2).astype(jnp.float32)
        b, s, h = x.shape
        xf = x.reshape(b * s, h)
        g = jnp.einsum('th,ih->ti', xf, gate_w) * gate_s
        u = jnp.einsum('th,ih->ti', xf, up_w) * up_s
        hdn = jax.nn.silu(g) * u
        out = jnp.einsum('ti,hi->th', hdn, down_w) * down_s
        return out.reshape(b, s, -1)

    def _L1_attn_ref(x, ln1_w, ln1_b, ln2_w, ln2_b, tm_k, tm_v, tm_r, time_decay, time_first, Wk, Wv, Wr, Wo, cm_k, cm_r, Wck, Wcv, Wcr):
        import jax, jax.numpy as jnp
        import numpy as np
        B, T, C = (4, 256, 256)
        D_ATT, D_FFN = (256, 1024)
        EPS = 1e-05

        def layer_norm(x, w, b):
            mu = jnp.mean(x, axis=-1, keepdims=True)
            var = jnp.var(x, axis=-1, keepdims=True)
            return (x - mu) * jax.lax.rsqrt(var + EPS) * w + b

        def time_shift(x):
            return jnp.pad(x, ((0, 0), (1, 0), (0, 0)))[:, :-1]

        def wkv(time_decay, time_first, k, v):
            decay = -jnp.exp(time_decay)
            kT = jnp.swapaxes(k, 0, 1)
            vT = jnp.swapaxes(v, 0, 1)

            def step(carry, kv_t):
                aa, bb, pp = carry
                kt, vt = kv_t
                ww = time_first + kt
                p = jnp.maximum(pp, ww)
                e1 = jnp.exp(pp - p)
                e2 = jnp.exp(ww - p)
                out = (e1 * aa + e2 * vt) / (e1 * bb + e2)
                ww2 = pp + decay
                p2 = jnp.maximum(ww2, kt)
                e1b = jnp.exp(ww2 - p2)
                e2b = jnp.exp(kt - p2)
                return ((e1b * aa + e2b * vt, e1b * bb + e2b, p2), out)
            z = jnp.zeros((k.shape[0], k.shape[2]), k.dtype)
            init = (z, z, jnp.full_like(z, -1e+38))
            _, outT = jax.lax.scan(step, init, (kT, vT))
            return jnp.swapaxes(outT, 0, 1)
        h = layer_norm(x, ln1_w, ln1_b)
        hh = time_shift(h)
        xk = h * tm_k + hh * (1 - tm_k)
        xv = h * tm_v + hh * (1 - tm_v)
        xr = h * tm_r + hh * (1 - tm_r)
        k = jnp.einsum('btc,dc->btd', xk, Wk)
        v = jnp.einsum('btc,dc->btd', xv, Wv)
        sr = jax.nn.sigmoid(jnp.einsum('btc,dc->btd', xr, Wr))
        rwkv = sr * wkv(time_decay, time_first, k, v)
        x = x + jnp.einsum('btd,cd->btc', rwkv, Wo)
        g = layer_norm(x, ln2_w, ln2_b)
        gg = time_shift(g)
        xk2 = g * cm_k + gg * (1 - cm_k)
        xr2 = g * cm_r + gg * (1 - cm_r)
        kf = jnp.square(jax.nn.relu(jnp.einsum('btc,fc->btf', xk2, Wck)))
        kv = jnp.einsum('btf,cf->btc', kf, Wcv)
        x = x + jax.nn.sigmoid(jnp.einsum('btc,dc->btd', xr2, Wcr)) * kv
        return x

    def _L1_ffn_ref(x, gate_w, bias, w_gate, w_up, w_down, sg, su, sd):
        import jax, jax.numpy as jnp
        import numpy as np
        E = 32
        K = 6
        H = 256
        I = 128
        T = 256
        CAP = 96
        SCALE = 1.5
        SWIGLU_LIMIT = 10.0
        B, S, Hd = x.shape
        h = x.reshape(-1, Hd)
        logits = h @ gate_w.T
        scores = jnp.sqrt(jax.nn.softplus(logits))
        _, topk_idx = jax.lax.top_k(scores + bias[None, :], K)
        topk_w = jnp.take_along_axis(scores, topk_idx, axis=1)
        topk_w = topk_w / jnp.sum(topk_w, axis=-1, keepdims=True)
        topk_w = topk_w * SCALE
        eid = topk_idx.reshape(-1)
        onehot = jax.nn.one_hot(eid, E, dtype=jnp.int32)
        pos = jnp.cumsum(onehot, axis=0) - 1
        pos = jnp.take_along_axis(pos, eid[:, None], axis=1)[:, 0]
        valid = pos < CAP
        pos = jnp.where(valid, pos, CAP)
        h_rep = jnp.repeat(h, K, axis=0)
        xb = jnp.zeros((E, CAP + 1, Hd), x.dtype).at[eid, pos].set(h_rep)
        g = jnp.einsum('ech,eih->eci', xb, w_gate)
        u = jnp.einsum('ech,eih->eci', xb, w_up)
        inter = jax.nn.silu(g) * u
        yb = jnp.einsum('eci,ehi->ech', inter, w_down)
        w_slot = jnp.where(valid, topk_w.reshape(-1), 0.0)
        y = yb[eid, pos] * w_slot[:, None]
        routed = y.reshape(-1, K, Hd).sum(axis=1)
        si = jax.nn.silu(h @ sg.T) * (h @ su.T)
        si = jnp.clip(si, -SWIGLU_LIMIT, SWIGLU_LIMIT)
        shared = si @ sd.T
        return (routed + shared).reshape(B, S, Hd)
    x = L0_attn_x
    x = x + _layernorm(_L0_attn_ref(_layernorm(x, axis=-1), L0_attn_Wq, L0_attn_Wk, L0_attn_Wv, L0_attn_Wo), axis=-1)
    x = x + _layernorm(_L0_ffn_ref(_layernorm(x, axis=-1), L0_ffn_gate_w, L0_ffn_up_w, L0_ffn_down_w, L0_ffn_gate_s, L0_ffn_up_s, L0_ffn_down_s), axis=-1)
    x = x + _layernorm(_L1_attn_ref(_layernorm(x, axis=-1), L1_attn_ln1_w, L1_attn_ln1_b, L1_attn_ln2_w, L1_attn_ln2_b, L1_attn_tm_k, L1_attn_tm_v, L1_attn_tm_r, L1_attn_time_decay, L1_attn_time_first, L1_attn_Wk, L1_attn_Wv, L1_attn_Wr, L1_attn_Wo, L1_attn_cm_k, L1_attn_cm_r, L1_attn_Wck, L1_attn_Wcv, L1_attn_Wcr), axis=-1)
    x = x + _layernorm(_L1_ffn_ref(_layernorm(x, axis=-1), L1_ffn_gate_w, L1_ffn_bias, L1_ffn_w_gate, L1_ffn_w_up, L1_ffn_w_down, L1_ffn_sg, L1_ffn_su, L1_ffn_sd), axis=-1)
    return x

_drawn_inputs = setup_inputs


def setup_inputs(seed=0):
    import zlib

    import numpy as np

    out = dict(_drawn_inputs(seed))
    spreads = {'L1_attn_ln1_w': (1.0, 0.6),
     'L1_attn_ln1_b': (0.0, 0.8),
     'L1_attn_ln2_w': (1.0, 0.6),
     'L1_attn_ln2_b': (0.0, 0.8)}
    factors = {'L1_attn_tm_k': 8.0,
     'L1_attn_tm_v': 8.0,
     'L1_attn_tm_r': 8.0,
     'L1_attn_time_decay': 7.069,
     'L1_attn_time_first': 8.0,
     'L1_attn_Wk': 8.0,
     'L1_attn_Wv': 2.677,
     'L1_attn_Wr': 8.0,
     'L1_attn_Wo': 2.669,
     'L1_attn_cm_k': 6.274,
     'L1_attn_cm_r': 8.0,
     'L1_attn_Wck': 3.149,
     'L1_attn_Wcv': 2.792,
     'L1_attn_Wcr': 8.0}
    for name, (base, spread) in spreads.items():
        noise = np.random.default_rng([zlib.crc32(name.encode()), seed]).standard_normal(out[name].shape)
        drawn = base * np.exp(spread * noise) if base else spread * noise
        out[name] = jnp.asarray(drawn.astype(out[name].dtype))
    for name, factor in factors.items():
        out[name] = (out[name] * factor).astype(out[name].dtype)
    return out
```

```python
from contextlib import ExitStack

import numpy as np

import concourse.bass as bass
from concourse import mybir

ALU = mybir.AluOpType
ACT = mybir.ActivationFunctionType
AX = mybir.AxisListType
F32 = mybir.dt.float32
BF16 = mybir.dt.bfloat16
U32 = mybir.dt.uint32

P = 128
B, T, C = 4, 512, 256
NT = T // P
NC = C // P
HQ, HKV, D = 32, 8, 8
GROUP = HQ // HKV
INTER = 704
NI = (INTER + P - 1) // P
ILAST = INTER - (NI - 1) * P
FFN = 1024
NF = FFN // P
E, TOPK, CAP, EI = 32, 6, 96, 128
SLOTS = E * CAP
TILES = B * NT
EPS = 1e-5
SCALE = D ** -0.5
NEG = -1e30
BIG = 3e38
N_LOADS = 25
OOB = float(1 << 20)

Q_PARTS = (0, 0, 0, 1, 1, 2)
K_PARTS = (0, 1, 2, 0, 1, 0)
ROWS = len(Q_PARTS) * D
STACK = ROWS + 2

REGION = T + 384 + 256 + 128
OFFSETS = {0: 0, 1: 512, 3: 896, 2: 1024}
OWN = 1024



def linked(eng, sem):
    done = [0]

    def link(ins):
        done[0] += 1
        ins.then_inc(sem, 1)
        eng.wait_ge(sem, done[0])
    return link


def flat(t):
    return t.rearrange("p a n -> p (a n)")


def as_tokens(t):
    return flat(t).rearrange("p (j c) -> p j c", c=C)


class Scratch:

    def __init__(self, tensor):
        self.t, self.at = tensor, 0

    def cut(self, shape, dt=F32):
        n = int(np.prod(shape[1:])) // (1 if dt == F32 else 2)
        v = self.t[:, self.at:self.at + n]
        self.at += n
        if dt != F32:
            v = v.bitcast(dt)
        dims = " ".join("abcd"[:len(shape) - 1])
        return v.rearrange(f"p ({dims}) -> p {dims}", **dict(zip("abcd", shape[1:]))) if len(shape) > 2 else v


def batch_phase(nc, a, d):
    with ExitStack() as ctx:
        def sb(name, shape, dt=F32):
            return ctx.enter_context(nc.sbuf_tensor(name, shape, dt))

        sems = []

        def sem(name):
            sems.append(ctx.enter_context(nc.semaphore(name)))
            return sems[-1]

        WQK = HKV * D
        wq = sb("wq", [P, NC, 2 * C + 2 * WQK])
        wv0 = sb("wv0", [P, NC, HKV * D])
        wo0 = sb("wo0", [P, NC, C])
        wgate = sb("wgate", [P, NC, INTER])
        wup = sb("wup", [P, NC, INTER])
        wdown = sb("wdown", [P, NI, C])
        gs = sb("gs", [P, NI])
        us = sb("us", [P, NI])
        ghalf = sb("ghalf", [P, NI])
        gus = sb("gus", [P, NI])
        ds = sb("ds", [P, C])
        wk1 = sb("wk1", [P, NC, C])
        wv1 = sb("wv1", [P, NC, C])
        wr1 = sb("wr1", [P, NC, C])
        wo1 = sb("wo1", [P, NC, C])
        wck = sb("wck", [P, NC, FFN])
        wcv = sb("wcv", [P, NF, C])
        wcr = sb("wcr", [P, NC, C])
        wrt = sb("wrt", [P, NC, E])
        wsg = sb("wsg", [P, NC, EI])
        wsu = sb("wsu", [P, NC, EI])
        wsd = sb("wsd", [P, C])
        NVEC = 11
        vecs = sb("vecs", [P, NVEC, NC])
        LN1W, LN1B, LN2W, LN2B, TMK, TMV, TMR, TDEC, TFIRST, CMK, CMR = range(NVEC)
        decay = sb("decay", [P, NC])
        rope = sb("rope", [P, 2, T])
        ident = sb("ident", [P, P])
        identb = sb("identb", [P, P], BF16)
        causal = sb("causal", [P, P], BF16)
        mhalf = sb("mhalf", [P, NT])

        NPB = 6
        probs = sb("probs", [P, NPB, REGION])
        early = Scratch(flat(probs[:]))
        x = early.cut([P, NT, C])
        hA = early.cut([P, NT, C])
        hAT = early.cut([P, NC, T])
        qparts = early.cut([P, 3, NC, T], BF16)
        kparts = early.cut([P, 3, T], BF16)[0:WQK]
        kr1 = early.cut([P, T])[0:WQK]
        kr2 = early.cut([P, T])[0:WQK]
        qst = sb("qst", [P, HQ // 2, T], BF16)
        kst = sb("kst", [P, 2, HKV, T], BF16)
        vaug = sb("vaug", [P, NT, HKV, 32])
        negmax = sb("negmax", [P, NT, HQ])
        nmparts = sb("nmparts", [P, 2, P], BF16)
        hout = sb("hout", [P, 2, T])
        r1 = sb("r1", [P, NC, T])
        r2 = sb("r2", [P, NC, T])
        attT, rdenb = r1, r2
        den = sb("den", [P, P])[:]
        stA = sb("stA", [P, NT, 6])
        mvA = sb("mvA", [P, NT, 2])
        veA = sb("veA", [P, NT])
        rsA = sb("rsA", [P, NT])

        x2 = sb("x2", [P, NT, C])
        x3 = sb("x3", [P, NT, C])
        z = sb("z", [P, NT, C])
        hB = sb("hB", [P, NT, C])
        hBT = sb("hBT", [P, NC, T + 1])
        th = sb("th", [P, NC, T])
        big = sb("big", [P, NF, T])
        ones = flat(big[:])[0:2, 0:HKV * T // 2].bitcast(BF16)
        wkv = [big[:, 2 * i:2 * i + 2, :] for i in range(4)] + [sb(f"wkv{i}", [P, NC, T])[:] for i in (4, 5)]
        pp = sb("pp", [P, NC, T + 1])
        aa = sb("aa", [P, NC, T + 1])
        bb = sb("bb", [P, NC, T + 1])
        stB = sb("stB", [P, NT, 6])
        mvB = sb("mvB", [P, NT, 2])
        veB = sb("veB", [P, NT])
        rsB = sb("rsB", [P, NT])
        lg = sb("lg", [P, NT, E])

        psum = ctx.enter_context(nc.psum_tensor("psum", [P, 8, 512], F32))
        pflat = flat(psum[:])

        with ExitStack() as once:
            w_in = once.enter_context(nc.semaphore("w_in"))
            ones_set = once.enter_context(nc.semaphore("ones_set"))
            stacks_set = once.enter_context(nc.semaphore("stacks_set"))
            ones_in = once.enter_context(nc.semaphore("ones_in"))
            exp_set = once.enter_context(nc.semaphore("exp_set"))
            zeros_out = once.enter_context(nc.semaphore("zeros_out"))
            block = once.enter_context(nc.Block())

            @block.sync
            def _(sp):
                n = 0
                for tile, name in ((wq, "wq"), (wv0, "wv0"), (wo0, "wo0"), (wgate, "wgate"), (wup, "wup"),
                                   (wk1, "wk1"), (wv1, "wv1"), (wr1, "wr1"), (wo1, "wo1"), (wck, "wck"), (wcv, "wcv"),
                                   (wcr, "wcr"), (wrt, "wrt"), (wsg, "wsg"), (wsu, "wsu")):
                    sp.dma_start(tile[:], a[name].rearrange("(k p) n -> p k n", p=P)).then_inc(w_in, 16)
                    n += 1
                full = (NI - 1) * P
                sp.dma_start(wdown[:, 0:NI - 1, :], a["wdown"][0:full].rearrange("(k p) n -> p k n", p=P)).then_inc(w_in, 16)
                sp.dma_start(wdown[0:ILAST, NI - 1, :], a["wdown"][full:INTER]).then_inc(w_in, 16)
                for tile, name in ((gs, "gs"), (us, "us")):
                    sp.dma_start(tile[:], a[name]).then_inc(w_in, 16)
                sp.dma_start(wsd[:], a["wsd"]).then_inc(w_in, 16)
                sp.dma_start(ds[:], a["ds"].partition_broadcast(P)).then_inc(w_in, 16)
                sp.dma_start(rope[:], a["rope"]).then_inc(w_in, 16)
                sp.dma_start(vecs[:], a["vecs"]).then_inc(w_in, 16)
                sp.dma_start(ident[:], a["ident"]).then_inc(w_in, 16)
                sp.dma_start(r1[:, 0, 0:P], a["causal"]).then_inc(w_in, 16)
                n += 10
                assert n == N_LOADS
                sp.wait_ge(w_in, 16 * n)
                sp.wait_ge(ones_set, 1)
                sp.wait_ge(stacks_set, 2)
                for par in range(2):
                    row = 64 * par + ROWS
                    sp.dma_start(flat(kst[row:row + 2, par, :, :]), ones).then_inc(ones_in, 16)
                sp.wait_ge(ones_in, 32)

            @block.gpsimd
            def _(pool):
                pool.memset(ones, 1.0).then_inc(ones_set, 1)
                pool.memset(mhalf[:], -0.5)
                pool.memset(hBT[:, :, 0:1], 0.0)
                pool.memset(pp[:, :, 0:1], -1e38)
                pool.memset(aa[:, :, 0:1], 0.0)
                pool.memset(bb[:, :, 0:1], 0.0)
                pool.memset(vaug[:], 1.0)
                pool.memset(flat(x2[:])[:, 0:C], 0.0).then_inc(ones_set, 1)
                pool.wait_ge(ones_set, 2)
                for k in range(SLOTS // P):
                    pool.dma_start(d["slots"][k * P:(k + 1) * P, :], flat(x2[:])[:, 0:C]).then_inc(zeros_out, 16)
                pool.wait_ge(zeros_out, 16 * (SLOTS // P))

            @block.vector
            def _(dve):
                dve.memset(kst[:].bitcast(F32), 0.0).then_inc(stacks_set, 1)
                dve.memset(qst[:].bitcast(F32), 0.0).then_inc(stacks_set, 1)
                dve.wait_ge(w_in, 16 * N_LOADS)
                dve.tensor_copy(identb[:], ident[:])
                dve.tensor_copy(causal[:], r1[:, 0, 0:P])
                dve.tensor_scalar(ghalf[:], gs[:], 0.5, None, ALU.mult)
                dve.scalar_tensor_tensor(gus[:], gs[:], 0.5, us[:], ALU.mult, ALU.mult)
                dve.wait_ge(exp_set, 1)
                dve.tensor_scalar(decay[:], decay[:], -1.0, None, ALU.mult)

            @block.scalar
            def _(act):
                act.wait_ge(w_in, 16 * N_LOADS)
                act.activation(decay[:], vecs[:, TDEC, :], ACT.Exp).then_inc(exp_set, 1)

        A_link, B_link = sem("A_link"), sem("B_link")
        A_in = sem("A_in")
        A_again = sem("A_again")
        A_var, A_rs = sem("A_var"), sem("A_rs")
        A_h = sem("A_h")
        A_mm = sem("A_mm")
        A_hT = sem("A_hT")
        A_qk = sem("A_qk")
        A_vaug = sem("A_vaug")
        A_rest = sem("A_rest")
        A_cast = sem("A_cast")
        A_parts = sem("A_parts")
        parts_out = sem("parts_out")
        stack_in = sem("stack_in")
        mx_mm, mx_rd = sem("mx_mm"), sem("mx_rd")
        nm_t, nm_s = sem("nm_t"), sem("nm_s")
        nm_out, nm_in = sem("nm_out"), sem("nm_in")
        sc_mm, sc_exp, sc_msk = sem("sc_mm"), sem("sc_exp"), sem("sc_msk")
        pv_mm, pv_rd = sem("pv_mm"), sem("pv_rd")
        ho_out = [sem(f"ho_out{i}") for i in range(2)]
        att_in = sem("att_in")
        den_in, A_rden = sem("den_in"), sem("A_rden")
        rden_out, rden_in = sem("rden_out"), sem("rden_in")
        A_att = sem("A_att")

        NFILLS = 48
        B_var, B_rs = sem("B_var"), sem("B_rs")
        B_h = sem("B_h")
        B_mm = sem("B_mm")
        B_gate, B_hid = sem("B_gate"), sem("B_hid")
        B_down, B_wo, B_cv = sem("B_down"), sem("B_wo"), sem("B_cv")
        B_sg, B_su = sem("B_sg"), sem("B_su")
        B_sc = sem("B_sc")
        B_hT = sem("B_hT")
        B_xs = sem("B_xs")
        B_arg = sem("B_arg")
        B_rwkv = sem("B_rwkv")
        B_kf = sem("B_kf")
        B_si = sem("B_si")
        B_x6 = sem("B_x6")
        B_lg = sem("B_lg")
        B_sh = sem("B_sh")
        B_out = sem("B_out")

        def bank(n):
            return psum[:, 6 + n % 2, :]

        S_GATE, S_K, S_V, S_R, S_EXP, S_KF, S_CR, S_SG = 0, 6, 8, 10, 12, 16, 24, 26
        F_T1, F_GU, F_DOWN, F_T2, F_K, F_V, F_R, F_WO, F_T3, F_CK, F_CR, F_CV, F_T4, F_SG, F_SU, F_LG, F_SD = \
            0, 2, 14, 16, 18, 20, 22, 24, 26, 28, 36, 38, 40, 42, 43, 44, 46

        read_off = {}
        for k in range(2):
            for n, (f, at) in enumerate(((F_T1, 0), (F_T2, 2), (F_T3, 4), (F_T4, 6))):
                read_off[f + k] = (B_hT, at + k + 1)
            for f, at in ((F_K, S_K), (F_V, S_V), (F_R, S_R), (F_CR, S_CR)):
                read_off[f + k] = (B_sc, at + k + 1)
            for f, by in ((F_DOWN, B_down), (F_WO, B_wo), (F_CV, B_cv), (F_LG, B_lg), (F_SD, B_sh)):
                read_off[f + k] = (by, k + 1)
        for m in range(NI):
            read_off[F_GU + 2 * m] = (B_gate, m + 1)
            read_off[F_GU + 2 * m + 1] = (B_hid, m + 1)
        for f in range(NF):
            read_off[F_CK + f] = (B_sc, S_KF + f + 1)
        read_off[F_SG], read_off[F_SU] = (B_sg, 1), (B_su, 1)

        def norm_stats(dve, link, src, st, mv, ve, var):
            for j in range(NT):
                ins = dve.bn_stats(st[:, j, :], src[:, j, :])
            link(ins)
            for j in range(NT):
                ins = dve.bn_aggr(mv[:, j, :], st[:, j, :])
            link(ins)
            dve.tensor_scalar(ve[:], mv[:, :, 1], EPS, None, ALU.add).then_inc(var, 1)

        def norm_apply(dve, out, src, mv, rs):
            for j in range(NT):
                ins = dve.tensor_scalar(out[:, j, :], src[:, j, :], mv[:, j, 0:1], rs[:, j:j + 1],
                                        ALU.subtract, ALU.mult)
            return ins

        def iteration(bA, bB):
            doA, doB = bA is not None, bB is not None
            STEPS, PAIRS = NT * HQ // 2, HQ // 2
            TURN = STEPS // NI
            LAGS = {"t2": 3, "k": 6, "v": 7, "r": 8, "args": (11, 12, 13, 14)}
            with nc.Block() as block:
                @block.sync
                def _(sp):
                    if doA:
                        sp.dma_start(x, a["x"][bass.ds(bA, 1)].rearrange("o (j p) c -> p (o j) c", p=P)).then_inc(A_in, 16)
                        sp.wait_ge(A_parts, 1)
                        sp.dma_start(d["qparts"].rearrange("s (k p) t -> p (s k) t", p=P),
                                     qparts.rearrange("p s k t -> p (s k) t")).then_inc(parts_out, 16)
                        sp.wait_ge(A_parts, 2)
                        sp.dma_start(d["kparts"].rearrange("s p t -> p s t"), kparts).then_inc(parts_out, 16)
                        sp.wait_ge(parts_out, 32)
                        for par in range(2):
                            for r in range(len(Q_PARTS)):
                                rows = slice(64 * par + D * r, 64 * par + D * r + D)
                                src = d["qparts"][Q_PARTS[r]].rearrange("(j two d) t -> two d j t", two=2, d=D)[par]
                                sp.dma_start(qst[rows, :, :], src).then_inc(stack_in, 16)
                                src = d["kparts"][K_PARTS[r]].rearrange("(g d) t -> d g t", d=D)
                                sp.dma_start(kst[rows, par, :, :], src).then_inc(stack_in, 16)
                        sp.wait_ge(nm_s, 1)
                        sp.dma_start(d["negmax"].rearrange("s i h t -> (i h) s t"), nmparts[:]).then_inc(nm_out, 16)
                        sp.wait_ge(nm_out, 16)
                        for par in range(2):
                            for s in range(2):
                                row = 64 * par + ROWS + s
                                src = d["negmax"][s].rearrange("i (j two) t -> two j i t", two=2)[par:par + 1]
                                sp.dma_start(qst[row:row + 1, :, :].rearrange("p j (i t) -> p j i t", t=P), src)\
                                    .then_inc(nm_in, 16)
                        for g in range(HKV):
                            sp.wait_ge(pv_rd, g + 1)
                            sp.dma_start(d["heads"][g], hout[:, g % 2, :]).then_inc(ho_out[g % 2], 16)
                        sp.wait_ge(pv_mm, HKV)
                        sp.dma_start(x, a["x"][bass.ds(bA, 1)].rearrange("o (j p) c -> p (o j) c", p=P)).then_inc(A_again, 16)
                        for i in range(2):
                            sp.wait_ge(ho_out[i], 16 * HKV // 2)
                        sums = d["heads"].rearrange("g (q r) t -> g q r t", r=32)
                        for g in range(HKV):
                            sp.dma_start(den[16 * g:16 * g + 16, :],
                                         sums[g, :, D, :].rearrange("q (b t) -> q b t", b=4)).then_inc(den_in, 16)
                        for g in range(HKV):
                            rows = slice(32 * (g % 4), 32 * (g % 4) + 32)
                            sp.dma_start(attT[rows, g // 4, :], sums[g, :, 0:D, :]).then_inc(att_in, 16)
                        sp.wait_ge(A_rden, 1)
                        sp.dma_start(d["rden"].rearrange("h (b t) -> (h b) t", b=4), den).then_inc(rden_out, 16)
                        sp.wait_ge(rden_out, 16)
                        for k in range(NC):
                            sp.dma_start(rdenb[:, k, :],
                                         d["rden"].rearrange("(h o) t -> h o t", o=1)[16 * k:16 * k + 16].broadcast_to([16, D, T]))\
                                .then_inc(rden_in, 16)
                    if doB:
                        sp.wait_ge(B_x6, 1)
                        sp.dma_start(d["x6"][bass.ds(bB * NT, NT)].rearrange("j p c -> p j c"), x3[:]).then_inc(B_out, 16)
                        sp.wait_ge(B_h, 4)
                        sp.dma_start(d["h4"][bass.ds(bB * NT, NT)].rearrange("j p c -> p j c"), hB[:]).then_inc(B_out, 16)
                        sp.wait_ge(B_lg, 2)
                        sp.dma_start(d["logits"][bass.ds(bB * NT, NT)].rearrange("j p c -> p j c"), lg[:]).then_inc(B_out, 16)
                        sp.wait_ge(B_sh, 2)
                        sp.dma_start(d["shared"][bass.ds(bB * NT, NT)].rearrange("j p c -> p j c"), as_tokens(wkv[4])).then_inc(B_out, 16)
                        sp.wait_ge(B_out, 64)

                @block.tensor
                def _(pe):
                    def fill(n):
                        if n >= 2:
                            pe.wait_ge(*read_off[n - 2])
                        return bank(n)

                    def transposed(n, m):
                        pe.wait_ge(B_h, m)
                        for k in range(NC):
                            to = fill(n + k)
                            for j in range(NT):
                                ins = pe.transpose(to[:, j * P:(j + 1) * P], hB[:, j, k * P:(k + 1) * P], ident[:])
                            ins.then_inc(B_mm, 1)

                    def channels(n, w, rows, cols, src, kt=NC):
                        to = fill(n)
                        for k in range(kt):
                            ins = pe.matmul(to[0:rows, :], w[:, k, cols:cols + rows], src[:, k, :],
                                            start=(k == 0), stop=(k == kt - 1))
                        ins.then_inc(B_mm, 1)

                    def tokens(n, src, w, kt, width=C, last=P):
                        for half in range(2):
                            to = fill(n + half)
                            for j in range(2):
                                at = (2 * half + j) * P
                                for k in range(kt):
                                    rows = last if k == kt - 1 else P
                                    ins = pe.matmul(to[:, j * width:(j + 1) * width], src[0:rows, k, at:at + P],
                                                    w[0:rows, k, :], start=(k == 0), stop=(k == kt - 1))
                            ins.then_inc(B_mm, 1)

                    def project_heads():
                        pe.wait_ge(A_h, 1)
                        for k in range(NC):
                            for j in range(NT):
                                ins = pe.transpose(psum[:, k, j * P:(j + 1) * P], hA[:, j, k * P:(k + 1) * P], ident[:])
                            ins.then_inc(A_mm, 1)
                        pe.wait_ge(A_hT, 2)

                        def project(to, w0, m):
                            for k in range(NC):
                                ins = pe.matmul(psum[0:m, to, :], wq[:, k, w0:w0 + m], hAT[:, k, :],
                                                start=(k == 0), stop=(k == NC - 1))
                            return ins
                        for i in range(NC):
                            ins = project(2 + i, i * P, P)
                        ins.then_inc(A_mm, 1)
                        for i in range(NC):
                            ins = project(i, C + i * P, P)
                        ins.then_inc(A_mm, 1)
                        project(4, 2 * C, WQK).then_inc(A_mm, 1)
                        project(5, 2 * C + WQK, WQK).then_inc(A_mm, 1)
                        pe.wait_ge(A_qk, 1)
                        for j in range(NT):
                            for k in range(NC):
                                ins = pe.matmul(psum[:, 2, j * WQK:(j + 1) * WQK], hAT[:, k, j * P:(j + 1) * P],
                                                wv0[:, k, :], start=(k == 0), stop=(k == NC - 1))
                        ins.then_inc(A_mm, 1)

                    def scores_for_max(s):
                        if s == 0:
                            pe.wait_ge(A_qk, 4)
                            pe.wait_ge(A_vaug, 1)
                            pe.wait_ge(stack_in, 16 * 24)
                        j, i = s // NT, s % NT
                        if s >= 3:
                            pe.wait_ge(mx_rd, s - 2)
                        for par in range(2):
                            to = 2 * (s % 3) + par
                            pe.matmul(psum[:, to, 0:(i + 1) * P], qst[:, j, i * P:(i + 1) * P],
                                      kst[:, par, j // 2, 0:(i + 1) * P], start=True, stop=True)
                            ins = pe.matmul(psum[:, to, i * P:(i + 1) * P], identb[:], causal[:], start=False, stop=True,
                                            skip_group_check=True)
                        ins.then_inc(mx_mm, 1)

                    def scores(m):
                        for par in range(2):
                            if m:
                                pe.wait_ge(sc_exp, 3 * (m - 1) + par + 1)
                            for i in (0, 1, 3):
                                at = 1024 * par + OFFSETS[i]
                                ins = pe.matmul(pflat[:, at:at + T - i * P], kst[:, par, m // 2, i * P:(i + 1) * P],
                                                qst[:, m, i * P:T], start=True, stop=True)
                            ins.then_inc(sc_mm, 1)
                        if m:
                            pe.wait_ge(sc_exp, 3 * m)
                        for par in range(2):
                            ins = pe.matmul(psum[:, 4, 2 * P * par:2 * P * (par + 1)], kst[:, par, m // 2, 2 * P:3 * P],
                                            qst[:, m, 2 * P:T], start=True, stop=True)
                        ins.then_inc(sc_mm, 1)

                    def values(g):
                        pe.wait_ge(sc_msk, 8 * (g + 1))
                        if g:
                            pe.wait_ge(pv_rd, g)
                        for i in range(NT):
                            for q in range(GROUP):
                                h = g * GROUP + q
                                at = OFFSETS[i]
                                ins = pe.matmul(psum[32 * q:32 * q + 32, 5, i * P:T], vaug[:, i, g, :],
                                                probs[:, h % NPB, at:at + T - i * P], start=(i == 0), stop=True,
                                                skip_group_check=True)
                        ins.then_inc(pv_mm, 1)

                    hT = hBT[:, :, 1:T + 1]
                    if doA:
                        project_heads()
                    if doB:
                        transposed(F_T1, 1)
                        pe.wait_ge(B_hT, 2)
                    for s in range(STEPS):
                        if doA:
                            scores_for_max(s)
                        if doB and s % TURN == TURN - 1 and s // TURN < NI:
                            m = s // TURN
                            rows = P if m < NI - 1 else ILAST
                            channels(F_GU + 2 * m, wgate, rows, m * P, hT)
                            channels(F_GU + 2 * m + 1, wup, rows, m * P, hT)
                    if doA:
                        pe.wait_ge(mx_rd, STEPS)
                        pe.transpose(psum[:, 4, 0:P], negmax[:].rearrange("p i h -> p (i h)"), ident[:]).then_inc(nm_t, 1)
                    if doB:
                        pe.wait_ge(B_hid, NI)
                        tokens(F_DOWN, big, wdown, NI, last=ILAST)
                    if doA:
                        pe.wait_ge(nm_in, 64)
                    for m in range(PAIRS):
                        if doA:
                            scores(m)
                            if m % 2 == 0 and m:
                                values(m // 2 - 1)
                        if doB:
                            if m == LAGS["t2"]:
                                transposed(F_T2, 2)
                            for i, (n, w, at) in enumerate(((F_K, wk1, "k"), (F_V, wv1, "v"), (F_R, wr1, "r"))):
                                if m == LAGS[at]:
                                    pe.wait_ge(B_xs, i + 1)
                                    for k in range(NC):
                                        channels(n + k, w, P, k * P, wkv[1 + i])
                    if doA:
                        values(HKV - 1)
                    if doB:
                        pe.wait_ge(B_rwkv, 1)
                        tokens(F_WO, wkv[0], wo1, NC)
                        transposed(F_T3, 3)
                        pe.wait_ge(B_xs, 4)
                        for f in range(NF):
                            channels(F_CK + f, wck, P, f * P, wkv[4])
                        pe.wait_ge(B_xs, 5)
                        tokens(F_CR, wkv[5], wcr, NC)
                    if doA:
                        pe.wait_ge(A_att, 1)
                        for j in range(NT):
                            for k in range(NC):
                                ins = pe.matmul(psum[:, j // 2, (j % 2) * C:(j % 2 + 1) * C], attT[:, k, j * P:(j + 1) * P],
                                                wo0[:, k, :], start=(k == 0), stop=(k == NC - 1))
                        ins.then_inc(A_mm, 1)
                    if doB:
                        pe.wait_ge(B_kf, NF)
                        tokens(F_CV, big, wcv, NF)
                        transposed(F_T4, 4)
                        pe.wait_ge(B_hT, 8)
                        channels(F_SG, wsg, P, 0, hT)
                        channels(F_SU, wsu, P, 0, hT)
                        tokens(F_LG, hT, wrt, NC, width=E)
                        pe.wait_ge(B_si, 1)
                        tokens(F_SD, wkv[3][:, 0:1, :], wsd[:].rearrange("p (o c) -> p o c", o=1), 1)

                @block.scalar
                def _(act):
                    def transposed(n, w=None, b=None):
                        for k in range(NC):
                            act.wait_ge(B_mm, n + k + 1)
                            if w is None:
                                act.activation(hBT[:, k, 1:T + 1], bank(n + k), ACT.Copy).then_inc(B_hT, 1)
                            else:
                                act.activation(hBT[:, k, 1:T + 1], bank(n + k), ACT.Identity, scale=vecs[:, w, k:k + 1],
                                               bias=vecs[:, b, k:k + 1]).then_inc(B_hT, 1)

                    def read(n, out, func=ACT.Copy, scale=1.0, rows=P):
                        act.wait_ge(B_mm, n + 1)
                        act.activation(out, bank(n)[0:rows, :], func, scale=scale).then_inc(B_sc, 1)

                    def read_values(g):
                        act.wait_ge(pv_mm, g + 1)
                        if g >= 2:
                            act.wait_ge(ho_out[g % 2], 16 * (g // 2))
                        act.activation(hout[:, g % 2, :], psum[:, 5, :], ACT.Copy).then_inc(pv_rd, 1)

                    def pair_exps(m):
                        at = 2 * m % NPB
                        if 2 * m >= NPB:
                            act.wait_ge(pv_mm, (2 * m - NPB) // GROUP + 1)
                        for par in range(2):
                            act.wait_ge(sc_mm, 3 * m + par + 1)
                            act.activation(probs[:, at + par, 0:OWN], pflat[:, 1024 * par:1024 * par + OWN], ACT.Exp,
                                           scale=SCALE).then_inc(sc_exp, 1)
                        act.wait_ge(sc_mm, 3 * m + 3)
                        act.activation(probs[:, at:at + 2, OWN:REGION], psum[:, 4, :].rearrange("p (h t) -> p h t", h=2),
                                       ACT.Exp, scale=SCALE).then_inc(sc_exp, 1)

                    if doA:
                        for k in range(NC):
                            act.wait_ge(A_mm, k + 1)
                            act.activation(hAT[:, k, :], psum[:, k, :], ACT.Copy).then_inc(A_hT, 1)
                    if doB:
                        transposed(F_T1)
                    if doA:
                        act.wait_ge(A_rest, 1)
                        act.activation(qparts[:, 0], r1[:], ACT.Copy).then_inc(A_cast, 1)
                        act.wait_ge(A_rest, 2)
                        act.activation(kparts[:, 0], kr1, ACT.Copy).then_inc(A_cast, 1)
                        act.wait_ge(A_mm, 7)
                        act.activation(vaug[:, :, :, 0:D], psum[:, 2, 0:NT * WQK].rearrange("p (j g d) -> p j g d", g=HKV, d=D),
                                       ACT.Copy).then_inc(A_vaug, 1)
                        act.wait_ge(A_rest, 3)
                        act.activation(qparts[:, 1], r2[:], ACT.Copy).then_inc(A_cast, 1)
                        act.wait_ge(A_rest, 4)
                        act.activation(kparts[:, 1], kr2, ACT.Copy).then_inc(A_cast, 1)
                    if doB:
                        for m in range(NI):
                            rows = P if m < NI - 1 else ILAST
                            if m >= 2:
                                act.wait_ge(B_gate, m - 1)
                            read(F_GU + 2 * m, th[0:rows, m % 2, :], ACT.Tanh, ghalf[0:rows, m:m + 1], rows)
                    for m in range(PAIRS):
                        if doA:
                            pair_exps(m)
                            if m % 2 and m > 1:
                                read_values(m // 2 - 1)
                        if doB:
                            if m == LAGS["t2"]:
                                transposed(F_T2, LN1W, LN1B)
                            if m == LAGS["k"]:
                                for k in range(NC):
                                    read(F_K + k, wkv[4][:, k, :])
                            if m == LAGS["v"]:
                                for k in range(NC):
                                    read(F_V + k, wkv[5][:, k, :])
                            if m == LAGS["r"]:
                                for k in range(NC):
                                    read(F_R + k, th[:, k, :], ACT.Tanh, 0.5)
                            if m in LAGS["args"]:
                                i = LAGS["args"].index(m)
                                t = (0, 1, 3, 2)[i]
                                act.wait_ge(B_arg, i + 1)
                                act.activation(wkv[t], wkv[t], ACT.Exp).then_inc(B_sc, 1)
                    if doA:
                        read_values(HKV - 1)
                    if doB:
                        transposed(F_T3, LN2W, LN2B)
                        for f in range(NF):
                            read(F_CK + f, big[:, f, :], ACT.Relu)
                        for k in range(2):
                            read(F_CR + k, th[:, k, :], ACT.Tanh, 0.5)
                        transposed(F_T4)
                        read(F_SG, th[:, 0, :], ACT.Tanh, 0.5)
                        for k in range(2):
                            act.wait_ge(B_mm, F_SD + k + 1)
                            act.activation(wkv[4][:, k, :], bank(F_SD + k), ACT.Copy).then_inc(B_sh, 1)

                @block.gpsimd
                def _(pool):
                    def deviations(var, n, rs_sem, ve, rs):
                        pool.wait_ge(var, n)
                        pool.tensor_tensor(rs[:], ve[:], mhalf[:], ALU.pow).then_inc(rs_sem, 1)

                    def devA(n):
                        if doA:
                            deviations(A_var, n, A_rs, veA, rsA)

                    def devB(*ns):
                        for n in ns if doB else ():
                            deviations(B_var, n, B_rs, veB, rsB)

                    def mask(m):
                        pool.wait_ge(sc_exp, 3 * m + 3)
                        for h in (2 * m % NPB, 2 * m % NPB + 1):
                            for blocks in (probs[:, h, 0:1024].rearrange("p (a t) -> p a t", t=512)[:, :, 0:P],
                                           probs[:, h, 896:1152].rearrange("p (a t) -> p a t", t=P)):
                                pool.affine_select(out=blocks, in_=blocks, compare_op=ALU.is_ge, fill=0.0, base=0,
                                                   pattern=[[0, 2], [1, P]], channel_multiplier=-1).then_inc(sc_msk, 1)

                    devA(1)
                    devB(1, 2)
                    for m in range(PAIRS):
                        if m < 2:
                            devB(3 + m)
                        if doA:
                            mask(m)
                    devB(5)
                    if doB:
                        for f in range(NF):
                            pool.wait_ge(B_sc, S_KF + f + 1)
                            pool.tensor_tensor(big[:, f, :], big[:, f, :], big[:, f, :], ALU.mult).then_inc(B_kf, 1)
                    devA(2)
                    devB(6, 7)

                @block.vector
                def _(dve):
                    linkA, link = linked(dve, A_link), linked(dve, B_link)
                    norms = [0]

                    def norm(out, src):
                        norms[0] += 1
                        norm_stats(dve, link, src, stB, mvB, veB, B_var)
                        dve.wait_ge(B_rs, norms[0])
                        return norm_apply(dve, out, src, mvB, rsB)

                    def two(t, half):
                        return t[:, 2 * half:2 * half + 2, :]

                    def banks(n):
                        return bank(n).rearrange("p (j c) -> p j c", c=C)

                    def rotate():
                        cos = rope[:, 0:1, :].broadcast_to([P, NC, T])
                        sin = rope[:, 1:2, :].broadcast_to([P, NC, T])
                        dve.wait_ge(A_mm, 3)
                        dve.tensor_tensor(r1[:], psum[:, 2:4, :], cos, ALU.mult).then_inc(A_qk, 1)
                        dve.wait_ge(A_mm, 4)
                        dve.tensor_tensor(r2[:], psum[:, 0:2, :], sin, ALU.mult).then_inc(A_qk, 1)
                        dve.wait_ge(A_qk, 2)
                        dve.tensor_tensor(r1[:], r1[:], r2[:], ALU.add).then_inc(A_rest, 1)
                        dve.wait_ge(A_mm, 5)
                        dve.tensor_tensor(kr1, psum[0:WQK, 4, :], rope[0:WQK, 0, :], ALU.mult).then_inc(A_qk, 1)
                        dve.wait_ge(A_mm, 6)
                        dve.tensor_tensor(kr2, psum[0:WQK, 5, :], rope[0:WQK, 1, :], ALU.mult).then_inc(A_qk, 1)
                        dve.wait_ge(A_qk, 4)
                        dve.tensor_tensor(kr1, kr1, kr2, ALU.add).then_inc(A_rest, 1)
                        dve.wait_ge(A_cast, 1)
                        dve.tensor_tensor(r2[:], r1[:], qparts[:, 0], ALU.subtract).then_inc(A_rest, 1)
                        dve.wait_ge(A_cast, 2)
                        dve.wait_ge(A_rest, 2)
                        dve.tensor_tensor(kr2, kr1, kparts[:, 0], ALU.subtract).then_inc(A_rest, 1)
                        dve.wait_ge(A_cast, 3)
                        dve.wait_ge(A_rest, 3)
                        dve.tensor_tensor(qparts[:, 2], r2[:], qparts[:, 1], ALU.subtract).then_inc(A_parts, 1)
                        dve.wait_ge(A_cast, 4)
                        dve.wait_ge(A_rest, 4)
                        dve.tensor_tensor(kparts[:, 2], kr2, kparts[:, 1], ALU.subtract).then_inc(A_parts, 1)

                    def maximum(s):
                        j, i = s // NT, s % NT
                        dve.wait_ge(mx_mm, s + 1)
                        to = 2 * (s % 3)
                        dve.tensor_reduce(negmax[:, i, 2 * j:2 * j + 2], psum[:, to:to + 2, 0:(i + 1) * P], AX.X,
                                          ALU.max, negate=True).then_inc(mx_rd, 1)

                    def hidden(m):
                        rows = P if m < NI - 1 else ILAST
                        g, u = F_GU + 2 * m, F_GU + 2 * m + 1
                        dve.wait_ge(B_sc, S_GATE + m + 1)
                        dve.scalar_tensor_tensor(big[0:rows, m, :], th[0:rows, m % 2, :], 1.0, bank(g)[0:rows, :],
                                                 ALU.add, ALU.mult).then_inc(B_gate, 1)
                        dve.wait_ge(B_gate, m + 1)
                        dve.wait_ge(B_mm, u + 1)
                        dve.scalar_tensor_tensor(big[0:rows, m, :], bank(u)[0:rows, :], gus[0:rows, m:m + 1],
                                                 big[0:rows, m, :], ALU.mult, ALU.mult).then_inc(B_hid, 1)

                    def mixtures(diff, outs):
                        link(dve.tensor_tensor(diff, hBT[:, :, 1:T + 1], hBT[:, :, 0:T], ALU.subtract))
                        for out, vec in outs:
                            for k in range(NC):
                                ins = dve.scalar_tensor_tensor(out[:, k, :], diff[:, k, :], vecs[:, vec, k:k + 1],
                                                               hBT[:, k, 0:T], ALU.mult, ALU.add)
                            ins.then_inc(B_xs, 1)

                    def swiglu_out():
                        for half in range(2):
                            n = F_DOWN + half
                            dve.wait_ge(B_mm, n + 1)
                            dve.tensor_tensor(two(hB, half), banks(n), ds[:].rearrange("p (o c) -> p o c", o=1)
                                              .broadcast_to([P, 2, C]), ALU.mult).then_inc(B_down, 1)
                        dve.wait_ge(B_down, 2)
                        link(norm(hB, hB))
                        link(dve.tensor_tensor(x3[:], x2[:], hB[:], ALU.add))

                    def time_mixing():
                        dve.wait_ge(B_hT, 4)
                        mixtures(wkv[0], ((wkv[1], TMK), (wkv[2], TMV), (wkv[3], TMR)))
                        dve.wait_ge(B_sc, S_R)
                        k_, v_ = wkv[4], wkv[5]
                        for k in range(NC):
                            ins = dve.tensor_tensor_scan(pp[:, k, 1:T + 1], decay[:, k:k + 1].broadcast_to([P, T]), k_[:, k, :],
                                                         -1e38, ALU.add, ALU.max)
                        link(ins)
                        old, new = pp[:, :, 0:T], pp[:, :, 1:T + 1]
                        for k in range(NC):
                            ins = dve.scalar_tensor_tensor(wkv[0][:, k, :], old[:, k, :], decay[:, k:k + 1], new[:, k, :],
                                                           ALU.add, ALU.subtract)
                        ins.then_inc(B_arg, 1)
                        dve.wait_ge(B_mm, F_R + 2)
                        dve.tensor_tensor(wkv[1], k_, new, ALU.subtract).then_inc(B_arg, 1)
                        for k in range(NC):
                            ins = dve.scalar_tensor_tensor(wkv[2][:, k, :], k_[:, k, :], vecs[:, TFIRST, k:k + 1], old[:, k, :],
                                                           ALU.add, ALU.max)
                        link(ins)
                        dve.tensor_tensor(wkv[3], old, wkv[2], ALU.subtract).then_inc(B_arg, 1)
                        dve.wait_ge(B_arg, 3)
                        for k in range(NC):
                            ins = dve.scalar_tensor_tensor(wkv[2][:, k, :], k_[:, k, :], vecs[:, TFIRST, k:k + 1],
                                                           wkv[2][:, k, :], ALU.add, ALU.subtract)
                        ins.then_inc(B_arg, 1)
                        dve.wait_ge(B_arg, 4)
                        dve.wait_ge(B_sc, S_EXP + 2)
                        link(dve.tensor_tensor(k_, wkv[1], v_, ALU.mult))
                        for k in range(NC):
                            dve.tensor_tensor_scan(aa[:, k, 1:T + 1], wkv[0][:, k, :], k_[:, k, :], 0.0, ALU.mult, ALU.add)
                            ins = dve.tensor_tensor_scan(bb[:, k, 1:T + 1], wkv[0][:, k, :], wkv[1][:, k, :], 0.0,
                                                         ALU.mult, ALU.add)
                        link(ins)
                        dve.wait_ge(B_sc, S_EXP + 4)
                        dve.tensor_tensor(wkv[0], wkv[3], aa[:, :, 0:T], ALU.mult)
                        dve.tensor_tensor(k_, wkv[3], bb[:, :, 0:T], ALU.mult)
                        link(dve.tensor_tensor(v_, wkv[2], v_, ALU.mult))
                        dve.tensor_tensor(wkv[0], wkv[0], v_, ALU.add)
                        link(dve.tensor_tensor(k_, k_, wkv[2], ALU.add))
                        link(dve.reciprocal(k_, k_))
                        link(dve.scalar_tensor_tensor(wkv[0], wkv[0], 0.5, k_, ALU.mult, ALU.mult))
                        dve.scalar_tensor_tensor(wkv[0], th[:], 1.0, wkv[0], ALU.add, ALU.mult).then_inc(B_rwkv, 1)
                        for half in range(2):
                            n = F_WO + half
                            dve.wait_ge(B_mm, n + 1)
                            dve.tensor_tensor(two(z, half), two(z, half), banks(n), ALU.add).then_inc(B_wo, 1)
                        dve.wait_ge(B_wo, 2)

                    def mixing_out():
                        for half in range(2):
                            n = F_CV + half
                            dve.wait_ge(B_sc, S_CR + half + 1)
                            dve.wait_ge(B_mm, n + 1)
                            dve.scalar_tensor_tensor(two(hB, half), as_tokens(th[:])[:, 2 * half:2 * half + 2, :], 1.0,
                                                     banks(n), ALU.add, ALU.mult).then_inc(B_cv, 1)
                        dve.wait_ge(B_cv, 2)
                        link(dve.scalar_tensor_tensor(z[:], hB[:], 0.5, z[:], ALU.mult, ALU.add))
                        link(norm(hB, z))
                        dve.tensor_tensor(x3[:], x3[:], hB[:], ALU.add).then_inc(B_x6, 1)
                        dve.wait_ge(B_x6, 1)

                    def shared_hidden():
                        dve.wait_ge(B_sc, S_SG + 1)
                        si = wkv[3][:, 0, :]
                        dve.scalar_tensor_tensor(si, th[:, 0, :], 1.0, bank(F_SG), ALU.add, ALU.mult).then_inc(B_sg, 1)
                        dve.wait_ge(B_sg, 1)
                        dve.wait_ge(B_mm, F_SU + 1)
                        dve.scalar_tensor_tensor(si, si, 0.5, bank(F_SU), ALU.mult, ALU.mult).then_inc(B_su, 1)
                        dve.wait_ge(B_su, 1)
                        dve.tensor_scalar(si, si, 10.0, -10.0, ALU.min, ALU.max).then_inc(B_si, 1)
                        for half in range(2):
                            n = F_LG + half
                            dve.wait_ge(B_mm, n + 1)
                            dve.tensor_copy(two(lg, half), bank(n)[:, 0:2 * E].rearrange("p (j c) -> p j c", c=E))\
                                .then_inc(B_lg, 1)

                    if doA:
                        dve.wait_ge(A_in, 16)
                        norm_stats(dve, linkA, x, stA, mvA, veA, A_var)
                        dve.wait_ge(A_rs, 1)
                        norm_apply(dve, hA, x, mvA, rsA).then_inc(A_h, 1)
                    if doB:
                        norm(hB, x2).then_inc(B_h, 1)
                    if doA:
                        rotate()
                    for s in range(STEPS):
                        if doA:
                            maximum(s)
                        if doB and s >= 3 and (s - 3) % TURN == TURN - 1 and (s - 3) // TURN < NI:
                            hidden((s - 3) // TURN)
                    if doA:
                        dve.wait_ge(nm_t, 1)
                        linkA(dve.tensor_copy(nmparts[:, 0, :], psum[:, 4, 0:P]))
                        dve.tensor_tensor(nmparts[:, 1, :], psum[:, 4, 0:P], nmparts[:, 0, :], ALU.subtract).then_inc(nm_s, 1)
                    if doB:
                        swiglu_out()
                        link(norm(z, x3))
                        norm(hB, z).then_inc(B_h, 1)
                        time_mixing()
                        norm(hB, z).then_inc(B_h, 1)
                        dve.wait_ge(B_hT, 6)
                        mixtures(aa[:, :, 1:T + 1], ((wkv[4], CMK), (wkv[5], CMR)))
                    if doA:
                        dve.wait_ge(den_in, 16 * HKV)
                        dve.reciprocal(den, den).then_inc(A_rden, 1)
                        dve.wait_ge(att_in, 16 * HKV)
                        dve.wait_ge(rden_in, 16 * NC)
                        dve.tensor_tensor(attT[:], attT[:], rdenb[:], ALU.mult).then_inc(A_att, 1)
                        dve.wait_ge(A_mm, 8)
                        out = psum[:, 0:2, :].rearrange("p a (j c) -> p (a j) c", c=C)
                        norm_stats(dve, linkA, out, stA, mvA, veA, A_var)
                        dve.wait_ge(A_rs, 2)
                        linkA(norm_apply(dve, hA, out, mvA, rsA))
                        dve.wait_ge(A_again, 16)
                        linkA(dve.tensor_tensor(x2[:], x, hA, ALU.add))
                    if doB:
                        mixing_out()
                        norm(hB, x3).then_inc(B_h, 1)
                        shared_hidden()
            nc.multi_engine_barrier(mybir.ALL_ENGINES, sems_to_clear=range(sems[0].num, sems[-1].num + 1))

        iteration(0, None)
        with nc.Fori(0, B - 1) as b:
            iteration(b + 1, b)
        iteration(None, B - 1)


def route(nc, a, d, idx, w6):
    with ExitStack() as ctx:
        def sb(name, shape, dt=F32):
            return ctx.enter_context(nc.sbuf_tensor(name, shape, dt))

        def sem(name):
            return ctx.enter_context(nc.semaphore(name))

        TE, ET = [P, TILES, E], [P, E, TILES]
        lg = sb("lg_all", TE)
        t0, t1, t2, t3, score = (sb(n, TE) for n in ("t0", "t1", "t2", "t3", "score"))
        sel = sb("sel", [P, TILES, E + 2])
        rep = sb("rep", [P, TILES, E + 2])
        top = sb("top", [P, TILES, 8])
        mask = sb("mask", TE)
        weight = sb("weight", TE)
        total = sb("total", [P, TILES])
        mask_e = sb("mask_e", ET)
        count = sb("count", ET)
        mask_b = sb("mask_b", ET, BF16)
        prior_b = sb("prior_b", ET, BF16)
        valid = sb("valid", ET)
        slot_e = sb("slot_e", ET)
        slot = sb("slot", TE)
        slot8 = sb("slot8", [P, TILES, 8])
        s8 = sb("s8", [P, TILES, 8])
        biasr = sb("biasr", [P, E])
        slotb = sb("slotb", ET)
        keep = sb("keep", ET)
        tri = sb("tri", [P, 2, P])
        trib = sb("trib", [P, 2, P], BF16)
        h4 = sb("h4", [P, TILES, C])
        ps = ctx.enter_context(nc.psum_tensor("ps_pos", [P, 512], F32))

        r_in, h_in = sem("r_in"), sem("h_in")
        r_v, r_s = sem("r_v"), sem("r_s")
        r_ready, r_pos = sem("r_ready"), sem("r_pos")
        r_idx, r_put = sem("r_idx"), sem("r_put")
        block = ctx.enter_context(nc.Block())

        @block.sync
        def _(sp):
            sp.dma_start(lg[:], d["logits"].rearrange("i p e -> p i e")).then_inc(r_in, 16)
            sp.dma_start(biasr[:], a["bias"].partition_broadcast(P)).then_inc(r_in, 16)
            sp.dma_start(slotb[:], a["slotb"]).then_inc(r_in, 16)
            sp.dma_start(keep[:], a["keep"]).then_inc(r_in, 16)
            sp.dma_start(tri[:], a["tri"]).then_inc(r_in, 16)
            sp.dma_start(h4[:], d["h4"].rearrange("i p c -> p i c")).then_inc(h_in, 16)

        @block.scalar
        def _(act):
            act.wait_ge(r_v, 1)
            act.activation(t1[:], t0[:], ACT.Exp, scale=-1.0).then_inc(r_s, 1)
            act.wait_ge(r_v, 2)
            act.activation(t0[:], t2[:], ACT.Ln).then_inc(r_s, 1)
            act.wait_ge(r_ready, 1)
            act.activation(score[:], t0[:], ACT.Sqrt).then_inc(r_s, 1)

        @block.tensor
        def _(pe):
            pe.wait_ge(r_ready, 2)
            pe.matmul(ps[:], trib[:, 0, :], flat(mask_b[:]), start=True, stop=False)
            pe.matmul(ps[:], trib[:, 1, :], flat(prior_b[:]), start=False, stop=True).then_inc(r_pos, 1)

        @block.gpsimd
        def _(pool):
            pool.wait_ge(r_idx, 1)
            pool.wait_ge(h_in, 16)
            for i in range(TILES):
                for k in range(TOPK):
                    pool.indirect_dma_start(
                        out=d["slots"], out_offset=bass.IndirectOffsetOnAxis(ap=idx[:, i * 8 + k:i * 8 + k + 1], axis=0),
                        in_=h4[:, i, :], in_offset=None, bounds_check=SLOTS - 1, oob_is_err=False).then_inc(r_put, 16)
            pool.wait_ge(r_put, 16 * TILES * TOPK)

        @block.vector
        def _(dve):
            link = linked(dve, r_v)
            dve.wait_ge(r_in, 16 * 5)
            link(dve.scalar_tensor_tensor(t0[:], lg[:], -1.0, lg[:], ALU.mult, ALU.max))
            dve.wait_ge(r_s, 1)
            link(dve.tensor_scalar(t2[:], t1[:], 1.0, None, ALU.add))
            link(dve.tensor_scalar(t3[:], t2[:], -1.0, None, ALU.add))
            link(dve.tensor_scalar(mask[:], t3[:], 0.0, None, ALU.is_equal))
            link(dve.tensor_scalar(t3[:], t3[:], 1e-30, None, ALU.max))
            link(dve.reciprocal(t3[:], t3[:]))
            dve.wait_ge(r_s, 2)
            link(dve.tensor_tensor(t0[:], t0[:], t1[:], ALU.mult))
            link(dve.tensor_tensor(t0[:], t0[:], t3[:], ALU.mult))
            link(dve.tensor_tensor(t1[:], t1[:], mask[:], ALU.mult))
            link(dve.tensor_tensor(t0[:], t0[:], t1[:], ALU.add))
            dve.scalar_tensor_tensor(t0[:], lg[:], 0.0, t0[:], ALU.max, ALU.add).then_inc(r_ready, 1)
            dve.tensor_copy(trib[:], tri[:])
            link(dve.memset(sel[:, :, E:E + 2], BIG))
            dve.wait_ge(r_s, 3)
            link(dve.tensor_tensor(sel[:, :, 0:E], score[:], biasr[:].rearrange("p (o e) -> p o e", o=1)
                                   .broadcast_to(TE), ALU.add))
            for i in range(TILES):
                ins = dve.max(top[:, i, :], sel[:, i, :])
            link(ins)
            for i in range(TILES):
                ins = dve.match_replace(out=rep[:, i, :], in_to_replace=top[:, i, :], in_values=sel[:, i, :], imm_value=-BIG)
            link(ins)
            link(dve.tensor_scalar(mask[:], rep[:, :, 0:E], -0.5 * BIG, None, ALU.is_le))
            dve.tensor_copy(mask_b[:], mask[:].rearrange("p i e -> p e i"))
            link(dve.tensor_copy(mask_e[:], mask[:].rearrange("p i e -> p e i")))
            link(dve.tensor_tensor_scan(flat(count[:]), flat(keep[:]), flat(mask_e[:]), 0.0, ALU.mult, ALU.add))
            dve.tensor_tensor(prior_b[:], count[:], mask_e[:], ALU.subtract).then_inc(r_ready, 1)
            link(dve.tensor_tensor(weight[:], mask[:], score[:], ALU.mult))
            link(dve.tensor_reduce(total[:], weight[:], AX.X, ALU.add))
            link(dve.reciprocal(total[:], total[:]))
            link(dve.scalar_tensor_tensor(weight[:], weight[:], 1.5, total[:].rearrange("p (i o) -> p i o", o=1)
                                          .broadcast_to(TE), ALU.mult, ALU.mult))
            dve.wait_ge(r_pos, 1)
            link(dve.scalar_tensor_tensor(flat(valid[:]), ps[:], float(CAP), flat(mask_e[:]), ALU.is_lt, ALU.mult))
            link(dve.tensor_tensor(flat(slot_e[:]), ps[:], flat(slotb[:]), ALU.add))
            dve.tensor_tensor(slot[:], slot_e[:].rearrange("p e i -> p i e"), valid[:].rearrange("p e i -> p i e"), ALU.mult)
            link(dve.tensor_tensor(weight[:], weight[:], valid[:].rearrange("p e i -> p i e"), ALU.mult))
            for i in range(TILES):
                ins = dve.max(slot8[:, i, :], slot[:, i, :])
            link(ins)
            link(dve.tensor_scalar(s8[:], slot8[:], 0.0, OOB, ALU.is_equal, ALU.mult))
            link(dve.scalar_tensor_tensor(s8[:], slot8[:], -1.0, s8[:], ALU.add, ALU.add))
            dve.tensor_copy(idx[:], s8[:].rearrange("p i k -> p (i k)")).then_inc(r_idx, 1)
            for k in range(TOPK):
                link(dve.tensor_tensor(t1[:], slot[:], slot8[:, :, k:k + 1].broadcast_to(TE), ALU.is_equal))
                link(dve.tensor_tensor(t1[:], t1[:], weight[:], ALU.mult))
                link(dve.tensor_reduce(w6[:, :, k], t1[:], AX.X, ALU.add))


def experts(nc, a, d):
    with ExitStack() as ctx:
        def sb(name, shape, dt=F32):
            return ctx.enter_context(nc.sbuf_tensor(name, shape, dt))

        def both(name):
            return [ctx.enter_context(nc.semaphore(f"{name}{q}")) for q in range(2)]

        xs = sb("xs", [CAP, 2, C])
        wgu = sb("wgu", [P, 2, NC, 2 * EI])
        wd = sb("wd", [P, 2, C])
        xT = sb("xT", [P, 2, NC, CAP])
        the = sb("the", [CAP, 2, EI])
        hid = sb("hid", [CAP, 2, EI])
        hidT = sb("hidT", [P, 2, CAP])
        ye = sb("ye", [CAP, 2, C])
        ident = sb("ident_e", [P, P])
        ps = ctx.enter_context(nc.psum_tensor("ps_e", [P, 8, 512], F32))
        id_in = ctx.enter_context(nc.semaphore("id_in"))
        e_in, e_xt, e_xTs, e_gu, e_th, e_g, e_hid, e_ht, e_hTs, e_y, e_ys, e_out = (both(n) for n in (
            "e_in", "e_xt", "e_xTs", "e_gu", "e_th", "e_g", "e_hid", "e_ht", "e_hTs", "e_y", "e_ys", "e_out"))
        block = ctx.enter_context(nc.Block())

        @block.sync
        def _(sp):
            sp.dma_start(ident[:], a["ident"]).then_inc(id_in, 16)
            with sp.Fori(0, E // 2) as p:
                for q in range(2):
                    e = p * 2 + q
                    sp.wait_ge(e_y[q], p + 1)
                    sp.dma_start(xs[:, q, :], d["slots"].rearrange("(e s) c -> e s c", s=CAP)[bass.ds(e, 1)]
                                 .rearrange("o s c -> (o s) c")).then_inc(e_in[q], 16)
                    sp.dma_start(wgu[:, q], a["wgu"][bass.ds(e, 1)].rearrange("o (k p) n -> p (o k) n", p=P)).then_inc(e_in[q], 16)
                    sp.dma_start(wd[:, q], a["wd"][bass.ds(e, 1)].rearrange("o p n -> (o p) n")).then_inc(e_in[q], 16)

        @block.tensor
        def _(pe):
            pe.wait_ge(id_in, 16)
            for q in range(2):
                pe.sem_inc(e_y[q], 1)
            with pe.Fori(0, E // 2) as p:
                for q in range(2):
                    pe.wait_ge(e_in[q], p * 48 + 48)
                    for k in range(NC):
                        ins = pe.transpose(ps[:, q, k * CAP:(k + 1) * CAP], xs[:, q, k * P:(k + 1) * P], ident[0:CAP, 0:CAP])
                    ins.then_inc(e_xt[q], 1)
                for q in range(2):
                    pe.wait_ge(e_xTs[q], p + 1)
                    for k in range(NC):
                        ins = pe.matmul(ps[0:CAP, 2 + q, 0:2 * EI], xT[:, q, k, :], wgu[:, q, k, :], start=(k == 0), stop=(k == NC - 1))
                    ins.then_inc(e_gu[q], 1)
                for q in range(2):
                    pe.wait_ge(e_hid[q], p + 1)
                    pe.transpose(ps[:, 4 + q, 0:CAP], hid[:, q, :], ident[0:CAP, 0:CAP]).then_inc(e_ht[q], 1)
                for q in range(2):
                    pe.wait_ge(e_hTs[q], p + 1)
                    pe.wait_ge(e_ys[q], p + 1)
                    pe.matmul(ps[0:CAP, 6 + q, 0:C], hidT[:, q, :], wd[:, q, :], start=True, stop=True).then_inc(e_y[q], 1)

        @block.scalar
        def _(act):
            for q in range(2):
                act.sem_inc(e_ys[q], 1)
                act.sem_inc(e_out[q], 16)
            with act.Fori(0, E // 2) as p:
                for q in range(2):
                    act.wait_ge(e_xt[q], p + 1)
                    act.activation(xT[:, q].rearrange("p k s -> p (k s)"), ps[:, q, 0:NC * CAP], ACT.Copy).then_inc(e_xTs[q], 1)
                for q in range(2):
                    act.wait_ge(e_gu[q], p + 1)
                    act.activation(the[:, q, :], ps[0:CAP, 2 + q, 0:EI], ACT.Tanh, scale=0.5).then_inc(e_th[q], 1)
                for q in range(2):
                    act.wait_ge(e_y[q], p + 2)
                    act.wait_ge(e_out[q], p * 16 + 16)
                    act.activation(ye[:, q, :], ps[0:CAP, 6 + q, 0:C], ACT.Copy).then_inc(e_ys[q], 1)
                for q in range(2):
                    act.wait_ge(e_ys[q], p + 2)
                    act.dma_start(d["expert"].rearrange("(e s) c -> e s c", s=CAP)[bass.ds(p * 2 + q, 1)]
                                  .rearrange("o s c -> (o s) c"), ye[:, q, :]).then_inc(e_out[q], 16)
            for q in range(2):
                act.wait_ge(e_out[q], 16 * (E // 2 + 1))

        @block.vector
        def _(dve):
            with dve.Fori(0, E // 2) as p:
                for q in range(2):
                    dve.wait_ge(e_th[q], p + 1)
                    dve.scalar_tensor_tensor(hid[:, q, :], the[:, q, :], 1.0, ps[0:CAP, 2 + q, 0:EI], ALU.add, ALU.mult).then_inc(e_g[q], 1)
                    dve.wait_ge(e_g[q], p + 1)
                    dve.scalar_tensor_tensor(hid[:, q, :], hid[:, q, :], 0.5, ps[0:CAP, 2 + q, EI:2 * EI], ALU.mult, ALU.mult)\
                        .then_inc(e_hid[q], 1)
                for q in range(2):
                    dve.wait_ge(e_ht[q], p + 1)
                    dve.tensor_copy(hidT[:, q, :], ps[:, 4 + q, 0:CAP]).then_inc(e_hTs[q], 1)


def combine(nc, d, out, idx, w6):
    with ExitStack() as ctx:
        def sb(name, shape, dt=F32):
            return ctx.enter_context(nc.sbuf_tensor(name, shape, dt))

        def both(name):
            return [ctx.enter_context(nc.semaphore(f"{name}{q}")) for q in range(2)]

        rows = sb("rows", [P, 2, TOPK, C])
        x6 = sb("x6t", [P, 2, C])
        acc = sb("acc", [P, 2, C])
        res = sb("res", [P, 2, C])
        st = sb("st", [P, 6])
        mv = sb("mv", [P, 2])
        ve = sb("ve", [P, 1])
        rs = sb("rs", [P, 1])
        mh = sb("mh", [P, 1])
        c_zero, c_rows, c_in, c_done, c_out = (both(n) for n in ("c_zero", "c_rows", "c_in", "c_done", "c_out"))
        c_mh = ctx.enter_context(nc.semaphore("c_mh"))
        c_v = ctx.enter_context(nc.semaphore("c_v"))
        c_rs = ctx.enter_context(nc.semaphore("c_rs"))
        V_STEPS = TOPK + 4
        block = ctx.enter_context(nc.Block())

        @block.sync
        def _(sp):
            for i in range(TILES):
                q, n = i % 2, i // 2
                if n:
                    sp.wait_ge(c_done[q], n)
                sp.dma_start(x6[:, q, :], d["x6"][i]).then_inc(c_in[q], 16)
                if n:
                    sp.wait_ge(c_out[q], 16 * n)
                sp.dma_start(acc[:, q, :], d["shared"][i]).then_inc(c_in[q], 16)

        @block.gpsimd
        def _(pool):
            pool.memset(mh[:], -0.5).then_inc(c_mh, 1)
            pool.wait_ge(c_mh, 1)

            def gather(i):
                q, n = i % 2, i // 2
                pool.wait_ge(c_zero[q], n + 1)
                for k in range(TOPK):
                    pool.indirect_dma_start(
                        out=rows[:, q, k, :], out_offset=None, in_=d["expert"],
                        in_offset=bass.IndirectOffsetOnAxis(ap=idx[:, i * 8 + k:i * 8 + k + 1], axis=0),
                        bounds_check=SLOTS - 1, oob_is_err=False).then_inc(c_rows[q], 16)

            gather(0)
            for i in range(TILES):
                if i + 1 < TILES:
                    gather(i + 1)
                pool.wait_ge(c_v, V_STEPS * i + V_STEPS - 1)
                pool.tensor_tensor(rs[:], ve[:], mh[:], ALU.pow).then_inc(c_rs, 1)

        @block.vector
        def _(dve):
            link = linked(dve, c_v)

            def clear(i):
                dve.memset(rows[:, i % 2], 0.0).then_inc(c_zero[i % 2], 1)
            clear(0)
            clear(1)
            for i in range(TILES):
                q, n = i % 2, i // 2
                dve.wait_ge(c_in[q], 32 * (n + 1))
                dve.wait_ge(c_rows[q], 16 * TOPK * (n + 1))
                for k in range(TOPK):
                    link(dve.scalar_tensor_tensor(acc[:, q, :], rows[:, q, k, :], w6[:, i, k:k + 1], acc[:, q, :],
                                                  ALU.mult, ALU.add))
                if i + 2 < TILES:
                    clear(i + 2)
                link(dve.bn_stats(st[:], acc[:, q, :]))
                link(dve.bn_aggr(mv[:], st[:]))
                link(dve.tensor_scalar(ve[:], mv[:, 1:2], EPS, None, ALU.add))
                dve.wait_ge(c_rs, i + 1)
                link(dve.tensor_scalar(acc[:, q, :], acc[:, q, :], mv[:, 0:1], rs[:], ALU.subtract, ALU.mult))
                if n:
                    dve.wait_ge(c_out[q], 16 * n)
                dve.tensor_tensor(res[:, q, :], x6[:, q, :], acc[:, q, :], ALU.add).then_inc(c_done[q], 1)

        @block.scalar
        def _(act):
            for i in range(TILES):
                q, n = i % 2, i // 2
                act.wait_ge(c_done[q], n + 1)
                act.dma_start(out[i], res[:, q, :]).then_inc(c_out[q], 16)
            for q in range(2):
                act.wait_ge(c_out[q], 16 * (TILES // 2))


def build(nc, a, out):
    def dram(name, shape, dt=F32):
        return nc.dram_tensor(name, shape, dt).ap()

    d = {
        "qparts": dram("qparts_d", [3, C, T], BF16), "kparts": dram("kparts_d", [3, HKV * D, T], BF16),
        "negmax": dram("negmax_d", [2, NT, HQ, P], BF16), "heads": dram("heads_d", [HKV, P, T]), "rden": dram("rden_d", [HQ, T]),
        "x6": dram("x6_d", [TILES, P, C]), "h4": dram("h4_d", [TILES, P, C]),
        "shared": dram("shared_d", [TILES, P, C]), "logits": dram("logits_d", [TILES, P, E]),
        "slots": dram("slots_d", [SLOTS, C]), "expert": dram("expert_d", [SLOTS, C]),
    }
    batch_phase(nc, a, d)
    with ExitStack() as ctx:
        idx = ctx.enter_context(nc.sbuf_tensor("idx", [P, TILES * 8], U32))
        w6 = ctx.enter_context(nc.sbuf_tensor("w6", [P, TILES, TOPK], F32))
        route(nc, a, d, idx, w6)
        experts(nc, a, d)
        combine(nc, d, out.rearrange("b (j p) c -> (b j) p c", p=P), idx, w6)


def kernel(**inputs):
    import concourse.bacc as bacc
    from concourse.bass_utils import run_bass_kernel_spmd

    g = {k: np.asarray(v) for k, v in inputs.items()}
    swap = np.arange(C) ^ 1

    def turned(w):
        return np.ascontiguousarray(np.swapaxes(w, -1, -2))

    def by_channel(v, n):
        full = np.zeros(n * P, v.dtype)
        full[:v.size] = v.reshape(-1)
        return full.reshape(n, P).T

    wq, wk = g["L0_attn_Wq"], g["L0_attn_Wk"]
    pair = (np.arange(P) % D) // 2
    inv = (np.float32(1.0) / np.float32(10000.0) ** (np.arange(D // 2, dtype=np.float32) / np.float32(D // 2))).astype(np.float32)
    angle = (np.arange(T, dtype=np.float32)[None, :] * inv[pair][:, None]).astype(np.float32)
    sign = np.where(np.arange(P) % 2 == 0, -1.0, 1.0)[:, None]
    rope = np.stack([np.cos(angle), np.sin(angle) * sign], axis=1).astype(np.float32)
    p, t = np.arange(P)[:, None], np.arange(P)[None, :]
    arrays = {
        "x": g["L0_attn_x"],
        "wq": np.concatenate([turned(wq), turned(wq[swap]), turned(wk), turned(wk[swap[:HKV * D]])], axis=1),
        "wv0": turned(g["L0_attn_Wv"]), "wo0": turned(g["L0_attn_Wo"]),
        "wgate": turned(g["L0_ffn_gate_w"]), "wup": turned(g["L0_ffn_up_w"]), "wdown": turned(g["L0_ffn_down_w"]),
        "gs": by_channel(g["L0_ffn_gate_s"], NI), "us": by_channel(g["L0_ffn_up_s"], NI), "ds": g["L0_ffn_down_s"],
        "wk1": turned(g["L1_attn_Wk"]), "wv1": turned(g["L1_attn_Wv"]), "wr1": turned(g["L1_attn_Wr"]),
        "wo1": turned(g["L1_attn_Wo"]), "wck": turned(g["L1_attn_Wck"]), "wcv": turned(g["L1_attn_Wcv"]),
        "wcr": turned(g["L1_attn_Wcr"]), "wrt": turned(g["L1_ffn_gate_w"]), "wsg": turned(g["L1_ffn_sg"]),
        "wsu": turned(g["L1_ffn_su"]), "wsd": turned(g["L1_ffn_sd"]), "bias": g["L1_ffn_bias"],
        "vecs": np.stack([by_channel(g["L1_attn_" + n], NC) for n in (
            "ln1_w", "ln1_b", "ln2_w", "ln2_b", "tm_k", "tm_v", "tm_r", "time_decay", "time_first", "cm_k", "cm_r")], axis=1),
        "wgu": np.concatenate([turned(g["L1_ffn_w_gate"]), turned(g["L1_ffn_w_up"])], axis=2),
        "wd": turned(g["L1_ffn_w_down"]),
        "rope": rope,
        "ident": np.eye(P, dtype=np.float32),
        "causal": np.where(t > p, NEG, 0.0).astype(np.float32),
        "tri": np.stack([(p < t), np.ones((P, P))], axis=1).astype(np.float32),
        "slotb": np.broadcast_to((np.arange(E) * CAP + 1.0)[None, :, None], (P, E, TILES)).astype(np.float32),
        "keep": np.broadcast_to((np.arange(TILES) > 0)[None, None, :], (P, E, TILES)).astype(np.float32),
    }
    arrays = {f"in_{k}": np.ascontiguousarray(v) for k, v in arrays.items()}
    nc = bacc.Bacc("TRN2", target_bir_lowering=False, num_devices=1)
    a = {k[3:]: nc.dram_tensor(k, v.shape, mybir.dt.from_np(v.dtype), kind="ExternalInput").ap() for k, v in arrays.items()}
    out = nc.dram_tensor("out", (B, T, C), F32, kind="ExternalOutput").ap()
    build(nc, a, out)
    r = run_bass_kernel_spmd(nc, [arrays], core_ids=[0])
    return r.results[0]["out"]
```

```python
from contextlib import ExitStack

import numpy as np

import concourse.bass as bass
from concourse import mybir

ALU = mybir.AluOpType
ACT = mybir.ActivationFunctionType
AX = mybir.AxisListType
F32 = mybir.dt.float32
BF16 = mybir.dt.bfloat16
U32 = mybir.dt.uint32

P = 128
B, T, C = 4, 512, 256
NT = T // P
NC = C // P
HQ, HKV, D = 32, 8, 8
GROUP = HQ // HKV
INTER = 704
NI = (INTER + P - 1) // P
ILAST = INTER - (NI - 1) * P
FFN = 1024
NF = FFN // P
E, TOPK, CAP, EI = 32, 6, 96, 128
SLOTS = E * CAP
TILES = B * NT
EPS = 1e-5
SCALE = D ** -0.5
NEG = -1e30
BIG = 3e38
N_LOADS = 11
OOB = float(1 << 20)
ROW = C + 1 + E
NACC = 2

Q_PARTS = (0, 0, 0, 1, 1, 2)
K_PARTS = (0, 1, 2, 0, 1, 0)
ROWS = len(Q_PARTS) * D
STACK = ROWS + 2

REGION = T + 384 + 256 + 128
OFFSETS = {0: 0, 1: 512, 3: 896, 2: 1024}
OWN = 1024



def linked(eng, sem):
    done = [0]

    def link(ins):
        done[0] += 1
        ins.then_inc(sem, 1)
        eng.wait_ge(sem, done[0])
    return link


def flat(t):
    return t.rearrange("p a n -> p (a n)")


def as_tokens(t):
    return flat(t).rearrange("p (j c) -> p j c", c=C)


class Scratch:

    def __init__(self, tensor):
        self.t, self.at = tensor, 0

    def cut(self, shape, dt=F32):
        n = int(np.prod(shape[1:])) // (1 if dt == F32 else 2)
        v = self.t[:, self.at:self.at + n]
        self.at += n
        if dt != F32:
            v = v.bitcast(dt)
        dims = " ".join("abcd"[:len(shape) - 1])
        return v.rearrange(f"p ({dims}) -> p {dims}", **dict(zip("abcd", shape[1:]))) if len(shape) > 2 else v


def batch_phase(nc, a, d, later):
    with ExitStack() as ctx:
        def sb(name, shape, dt=F32):
            return ctx.enter_context(nc.sbuf_tensor(name, shape, dt))

        sems = []

        def sem(name):
            sems.append(ctx.enter_context(nc.semaphore(name)))
            return sems[-1]

        WQK = HKV * D
        wq = sb("wq", [P, NC, 2 * C + 2 * WQK])
        wv0 = sb("wv0", [P, NC, HKV * D])
        wo0 = sb("wo0", [P, NC, C])
        wgate = sb("wgate", [P, NC, INTER])
        wup = sb("wup", [P, NC, INTER])
        wdown = sb("wdown", [P, NI, C])
        gs = sb("gs", [P, NI])
        us = sb("us", [P, NI])
        ghalf = sb("ghalf", [P, NI])
        gus = sb("gus", [P, NI])
        ds = sb("ds", [P, C])
        wk1 = sb("wk1", [P, NC, C])
        wv1 = sb("wv1", [P, NC, C])
        wr1 = sb("wr1", [P, NC, C])
        wo1 = sb("wo1", [P, NC, C])
        wck = sb("wck", [P, NC, FFN])
        wcv = sb("wcv", [P, NF, C])
        wcr = sb("wcr", [P, NC, C])
        wrt = sb("wrt", [P, NC, E])
        wsg = sb("wsg", [P, NC, EI])
        wsu = sb("wsu", [P, NC, EI])
        wsd = sb("wsd", [P, C])
        NVEC = 11
        vecs = sb("vecs", [P, NVEC, NC])
        LN1W, LN1B, LN2W, LN2B, TMK, TMV, TMR, TDEC, TFIRST, CMK, CMR = range(NVEC)
        decay = sb("decay", [P, NC])
        rope = sb("rope", [P, 2, T])
        ident = sb("ident", [P, P])
        identb = sb("identb", [P, P], BF16)
        causal = sb("causal", [P, P], BF16)
        mhalf = sb("mhalf", [P, NT])

        NPB = 6
        probs = sb("probs", [P, NPB, REGION])
        early = Scratch(flat(probs[:]))
        attT = early.cut([P, NC, T])
        hAT = early.cut([P, NC, T])
        qparts = early.cut([P, 3, NC, T], BF16)
        kparts = early.cut([P, 3, T], BF16)[0:WQK]
        kr1 = early.cut([P, T])[0:WQK]
        kr2 = early.cut([P, T])[0:WQK]
        qst = sb("qst", [P, HQ // 2, T], BF16)
        kst = sb("kst", [P, 2, HKV, T], BF16)
        vaug = sb("vaug", [P, NT, HKV, 32])
        negmax = sb("negmax", [P, NT, HQ])
        nmparts = sb("nmparts", [P, 2, P], BF16)
        hout = sb("hout", [P, 2, T])
        r1 = sb("r1", [P, NC, T])
        r2 = sb("r2", [P, NC, T])
        hA = sb("hA", [P, NT, C])
        rdenb = hout
        den = sb("den", [P, P])[:]
        stA = sb("stA", [P, NT, 6])
        mvA = sb("mvA", [P, NT, 2])
        veA = sb("veA", [P, NT])
        rsA = sb("rsA", [P, NT])
        stP = sb("stP", [P, NT, 6])
        mvP = sb("mvP", [P, NT, 2])
        veP = sb("veP", [P, NT])
        rsP = sb("rsP", [P, NT])

        x2 = sb("x2", [P, NT, C])
        x3 = sb("x3", [P, NT, C])
        z = sb("z", [P, NT, C])
        hB = sb("hB", [P, NT, C])
        hBT = sb("hBT", [P, NC, T + 1])
        th = flat(hB[:]).rearrange("p (k t) -> p k t", t=T)
        big = sb("big", [P, NF, T])
        ones = flat(big[:])[0:2, 0:HKV * T // 2].bitcast(BF16)
        ut = flat(z[:]).rearrange("p (k t) -> p k t", t=T)
        wkv = [big[:, 2 * i:2 * i + 2, :] for i in range(4)] + [sb(f"wkv{i}", [P, NC, T])[:] for i in (4, 5)]
        pp = sb("pp", [P, NC, T + 1])
        aa = sb("aa", [P, NC, T + 1])
        bb = sb("bb", [P, NC, T + 1])
        stB = sb("stB", [P, NT, 6])
        mvB = sb("mvB", [P, NT, 2])
        veB = sb("veB", [P, NT])
        rsB = sb("rsB", [P, NT])
        lg = sb("lg", [P, NT, E])

        routed = sb("routed", [P, NT, ROW])
        tok = sb("tok", [P, NT])
        seen = sb("seen", [P, E])
        biasr = sb("biasr", [P, E])
        slotb = sb("slotb", [P, E])
        trib = sb("trib", [P, 2, P], BF16)
        idx = sb("idx", [P, NT * 8], U32)
        mask_b = sb("mask_b", [P, NT, E], BF16)
        before = sb("before", [P, NT + 1, E], BF16)
        free4, free5 = Scratch(flat(wkv[4])), Scratch(flat(wkv[5]))
        TE = [P, NT, E]
        a0, a1, a2, a3, score, mask, valid = (free4.cut(TE) for _ in range(7))
        sel, rep, weight, total, slot, top, slot8, s8 = (free5.cut(shape) for shape in (
            [P, NT, E + 2], [P, NT, E + 2], TE, [P, NT], TE, [P, NT, 8], [P, NT, 8], [P, NT, 8]))

        psum = ctx.enter_context(nc.psum_tensor("psum", [P, 8, 512], F32))
        pflat = flat(psum[:])

        N_LATER = 19 + 1 + NACC
        with ExitStack() as once:
            w_in = sem("w_in")
            ones_set = sem("ones_set")
            stacks_set = sem("stacks_set")
            ones_in = sem("ones_in")
            exp_set = sem("exp_set")
            empty_set = sem("empty_set")
            block = once.enter_context(nc.Block())

            @block.sync
            def _(sp):
                loads = [(hA[:], a["x"][0].rearrange("(j p) c -> p j c", p=P)), (wq[:], a["wq"].rearrange("(k p) n -> p k n", p=P)), (rope[:], a["rope"]), (ident[:], a["ident"]),
                         (wv0[:], a["wv0"].rearrange("(k p) n -> p k n", p=P)),
                         (gs[:], a["gs"]), (us[:], a["us"]), (vecs[:], a["vecs"]), (r1[:, 0, 0:P], a["causal"]),
                         (r2[:, 0, 0:2 * P], a["tri"].rearrange("p a n -> p (a n)")), (tok[:], a["tok"])]
                assert len(loads) == N_LOADS
                for to, src in loads:
                    sp.dma_start(to, src).then_inc(w_in, 16)
                sp.wait_ge(ones_set, 1)
                sp.wait_ge(stacks_set, 2)
                for par in range(2):
                    row = 64 * par + ROWS
                    sp.dma_start(flat(kst[row:row + 2, par, :, :]), ones).then_inc(ones_in, 16)
                sp.wait_ge(ones_in, 32)

            @block.gpsimd
            def _(pool):
                pool.memset(ones, 1.0).then_inc(ones_set, 1)
                pool.memset(mhalf[:], -0.5)
                pool.memset(hBT[:, :, 0:1], 0.0)
                pool.memset(pp[:, :, 0:1], -1e38)
                pool.memset(aa[:, :, 0:1], 0.0)
                pool.memset(bb[:, :, 0:1], 0.0)
                pool.memset(vaug[:], 1.0)
                pool.memset(seen[:], 0.0)

            @block.vector
            def _(dve):
                dve.memset(kst[:].bitcast(F32), 0.0).then_inc(stacks_set, 1)
                dve.memset(qst[:].bitcast(F32), 0.0).then_inc(stacks_set, 1)
                dve.wait_ge(w_in, 16 * N_LOADS)
                dve.tensor_copy(identb[:], ident[:])
                dve.tensor_copy(causal[:], r1[:, 0, 0:P])
                dve.tensor_copy(flat(trib[:]), r2[:, 0, 0:2 * P])
                dve.memset(x2[:], 0.0).then_inc(stacks_set, 1)
                dve.wait_ge(stacks_set, 3)
                dve.tensor_scalar(flat(x2[:])[:, C:C + 1], tok[:, 0:1], float(TILES * P), None, ALU.add).then_inc(empty_set, 1)
                dve.tensor_scalar(ghalf[:], gs[:], 0.5, None, ALU.mult)
                dve.scalar_tensor_tensor(gus[:], gs[:], 0.5, us[:], ALU.mult, ALU.mult)
                dve.wait_ge(exp_set, 1)
                dve.tensor_scalar(decay[:], decay[:], -1.0, None, ALU.mult)

            @block.scalar
            def _(act):
                act.wait_ge(w_in, 16 * N_LOADS)
                act.activation(decay[:], vecs[:, TDEC, :], ACT.Exp).then_inc(exp_set, 1)

        def load_later(sp):
            full = (NI - 1) * P
            loads = [(tile[:], a[name].rearrange("(k p) n -> p k n", p=P)) for tile, name in (
                (wo0, "wo0"), (wgate, "wgate"), (wup, "wup"), (wk1, "wk1"), (wv1, "wv1"), (wr1, "wr1"), (wo1, "wo1"),
                (wck, "wck"), (wcv, "wcv"), (wcr, "wcr"), (wrt, "wrt"), (wsg, "wsg"), (wsu, "wsu"))]
            loads += [(wdown[:, 0:NI - 1, :], a["wdown"][0:full].rearrange("(k p) n -> p k n", p=P)),
                      (wdown[0:ILAST, NI - 1, :], a["wdown"][full:INTER]), (wsd[:], a["wsd"]),
                      (ds[:], a["ds"].partition_broadcast(P)), (biasr[:], a["bias"].partition_broadcast(P)),
                      (slotb[:], a["slotb"])]
            for to, src in loads:
                sp.dma_start(to, src).then_inc(later, 16)
            assert len(loads) + 1 + NACC == N_LATER

        def empty_tables(sp):
            def repeated(src, n):
                return src.rearrange("p (o c) -> p o c", o=1).broadcast_to([P, n, src.shape[1]])
            sp.dma_start(d["slots"].rearrange("(k p) c -> p k c", p=P), repeated(flat(x2[:])[:, 0:ROW], SLOTS // P))\
                .then_inc(later, 16)
            sp.dma_start(d["acc"][0][TILES * P:], x2[:, 2, :]).then_inc(later, 16)
            for i in range(1, NACC):
                sp.dma_start(d["acc"][i].rearrange("(k p) c -> p k c", p=P), repeated(x2[:, 2, :], TILES + 1)).then_inc(later, 16)

        A_link, B_link = sem("A_link"), sem("B_link")
        A_in = sem("A_in")
        A_again = sem("A_again")
        B_x3 = sem("B_x3")
        P_var, P_rs = sem("P_var"), sem("P_rs")
        A_var, A_rs = sem("A_var"), sem("A_rs")
        A_h = sem("A_h")
        A_mm = sem("A_mm")
        A_hT = sem("A_hT")
        A_qk = sem("A_qk")
        A_vaug = sem("A_vaug")
        A_rest = sem("A_rest")
        A_cast = sem("A_cast")
        A_parts = sem("A_parts")
        parts_out = sem("parts_out")
        stack_in = sem("stack_in")
        mx_mm, mx_rd = sem("mx_mm"), sem("mx_rd")
        nm_t, nm_s = sem("nm_t"), sem("nm_s")
        nm_out, nm_in = sem("nm_out"), sem("nm_in")
        sc_mm, sc_exp, sc_msk = sem("sc_mm"), sem("sc_exp"), sem("sc_msk")
        pv_mm, pv_rd = sem("pv_mm"), sem("pv_rd")
        ho_out = [sem(f"ho_out{i}") for i in range(2)]
        att_in = sem("att_in")
        den_in, A_rden = sem("den_in"), sem("A_rden")
        rden_out, rden_in = sem("rden_out"), sem("rden_in")
        A_att = sem("A_att")
        A_wo = sem("A_wo")

        NFILLS = 48
        B_var, B_rs = sem("B_var"), sem("B_rs")
        B_h = sem("B_h")
        B_mm = sem("B_mm")
        B_gate, B_hid = sem("B_gate"), sem("B_hid")
        B_down, B_wo, B_cv = sem("B_down"), sem("B_wo"), sem("B_cv")
        B_sg, B_su = sem("B_sg"), sem("B_su")
        B_sc = sem("B_sc")
        B_hT = sem("B_hT")
        B_xs = sem("B_xs")
        B_arg = sem("B_arg")
        B_kv, B_ev = sem("B_kv"), sem("B_ev")
        B_rwkv = sem("B_rwkv")
        B_kf = sem("B_kf")
        B_si = sem("B_si")
        B_x6 = sem("B_x6")
        B_lg = sem("B_lg")
        B_sh = sem("B_sh")
        B_out = sem("B_out")

        C_v = sem("C_v")
        C_s = sem("C_s")
        C_abs, C_log, C_plus = sem("C_abs"), sem("C_log"), sem("C_plus")
        C_mask, C_pos = sem("C_mask"), sem("C_pos")
        C_read = sem("C_read")
        C_idx, C_put = sem("C_idx"), sem("C_put")

        def bank(n):
            return psum[:, 6 + n % 2, :]

        S_GU, S_K, S_V, S_R, S_EXP, S_KF, S_CR, S_SG = 0, 12, 14, 16, 18, 22, 30, 32
        F_T1, F_GU, F_DOWN, F_T2, F_K, F_V, F_R, F_WO, F_T3, F_CK, F_CR, F_CV, F_T4, F_SG, F_SU, F_LG, F_SD = \
            0, 2, 14, 16, 18, 20, 22, 24, 26, 28, 36, 38, 40, 42, 43, 44, 46

        read_off = {}
        for k in range(2):
            for n, (f, at) in enumerate(((F_T1, 0), (F_T2, 2), (F_T3, 4), (F_T4, 6))):
                read_off[f + k] = (B_hT, at + k + 1)
            for f, at in ((F_K, S_K), (F_V, S_V), (F_R, S_R), (F_CR, S_CR)):
                read_off[f + k] = (B_sc, at + k + 1)
            for f, by in ((F_DOWN, B_down), (F_WO, B_wo), (F_CV, B_cv), (F_LG, B_lg), (F_SD, B_sh)):
                read_off[f + k] = (by, k + 1)
        for m in range(NI):
            read_off[F_GU + 2 * m] = (B_gate, m + 1)
            read_off[F_GU + 2 * m + 1] = (B_sc, S_GU + 2 * m + 2)
        for f in range(NF):
            read_off[F_CK + f] = (B_sc, S_KF + f + 1)
        read_off[F_SG], read_off[F_SU] = (B_sg, 1), (B_su, 1)

        def norm_stats(dve, link, src, st, mv, ve, var):
            for j in range(NT):
                ins = dve.bn_stats(st[:, j, :], src[:, j, :])
            link(ins)
            for j in range(NT):
                ins = dve.bn_aggr(mv[:, j, :], st[:, j, :])
            link(ins)
            dve.tensor_scalar(ve[:], mv[:, :, 1], EPS, None, ALU.add).then_inc(var, 1)

        def norm_apply(dve, out, src, mv, rs):
            for j in range(NT):
                ins = dve.tensor_scalar(out[:, j, :], src[:, j, :], mv[:, j, 0:1], rs[:, j:j + 1],
                                        ALU.subtract, ALU.mult)
            return ins

        def iteration(project=None, attend=None, bB=None, doC=False):
            doP, doA, doB = project is not None, attend is not None, bB is not None
            STEPS, PAIRS = NT * HQ // 2, HQ // 2
            N_DOWN = NT * NI
            DOWN_FROM, DOWN_AFTER = 28, 12
            V_LAG = 12
            RANKS = 12
            LAGS = {"t2": 4, "k": 6, "v": 7, "r": 8, "args": (9, 9, 11, 11)}
            with nc.Block() as block:
                @block.sync
                def _(sp):
                    if project == 0:
                        load_later(sp)
                    elif doP:
                        sp.dma_start(hA[:], a["x"][bass.ds(project, 1)].rearrange("o (j p) c -> p (o j) c", p=P)).then_inc(A_in, 16)
                    if attend == 0:
                        empty_tables(sp)
                    if doA:
                        sp.wait_ge(nm_s, 1)
                        sp.dma_start(d["negmax"].rearrange("s i h t -> (i h) s t"), nmparts[:]).then_inc(nm_out, 16)
                        sp.wait_ge(nm_out, 16)
                        for par in range(2):
                            for s in range(2):
                                row = 64 * par + ROWS + s
                                src = d["negmax"][s].rearrange("i (j two) t -> two j i t", two=2)[par:par + 1]
                                sp.dma_start(qst[row:row + 1, :, :].rearrange("p j (i t) -> p j i t", t=P), src)\
                                    .then_inc(nm_in, 16)
                        for g in range(HKV):
                            sp.wait_ge(pv_rd, g + 1)
                            sp.dma_start(d["heads"][g], hout[:, g % 2, :]).then_inc(ho_out[g % 2], 16)
                        if doB:
                            sp.wait_ge(B_x3, 1)
                        else:
                            sp.wait_ge(later, 16 * N_LATER)
                        sp.dma_start(x2[:], a["x"][bass.ds(attend, 1)].rearrange("o (j p) c -> p (o j) c", p=P)).then_inc(A_again, 16)
                        for i in range(2):
                            sp.wait_ge(ho_out[i], 16 * HKV // 2)
                        sums = d["heads"].rearrange("g (q r) t -> g q r t", r=32)
                        for g in range(HKV):
                            sp.dma_start(den[16 * g:16 * g + 16, :],
                                         sums[g, :, D, :].rearrange("q (b t) -> q b t", b=4)).then_inc(den_in, 16)
                        for g in range(HKV):
                            rows = slice(32 * (g % 4), 32 * (g % 4) + 32)
                            sp.dma_start(attT[rows, g // 4, :], sums[g, :, 0:D, :]).then_inc(att_in, 16)
                        sp.wait_ge(A_rden, 1)
                        sp.dma_start(d["rden"].rearrange("h (b t) -> (h b) t", b=4), den).then_inc(rden_out, 16)
                        sp.wait_ge(rden_out, 16)
                        for k in range(NC):
                            sp.dma_start(rdenb[:, k, :],
                                         d["rden"].rearrange("(h o) t -> h o t", o=1)[16 * k:16 * k + 16].broadcast_to([16, D, T]))\
                                .then_inc(rden_in, 16)
                    if doP:
                        sp.wait_ge(A_parts, 1)
                        sp.dma_start(d["qparts"].rearrange("s (k p) t -> p (s k) t", p=P),
                                     qparts.rearrange("p s k t -> p (s k) t")).then_inc(parts_out, 16)
                        sp.wait_ge(A_parts, 2)
                        sp.dma_start(d["kparts"].rearrange("s p t -> p s t"), kparts).then_inc(parts_out, 16)
                        sp.wait_ge(parts_out, 32)
                        for par in range(2):
                            for r in range(len(Q_PARTS)):
                                rows = slice(64 * par + D * r, 64 * par + D * r + D)
                                src = d["qparts"][Q_PARTS[r]].rearrange("(j two d) t -> two d j t", two=2, d=D)[par]
                                sp.dma_start(qst[rows, :, :], src).then_inc(stack_in, 16)
                                src = d["kparts"][K_PARTS[r]].rearrange("(g d) t -> d g t", d=D)
                                sp.dma_start(kst[rows, par, :, :], src).then_inc(stack_in, 16)
                        sp.wait_ge(stack_in, 16 * 24)
                    if doB:
                        sp.wait_ge(B_x6, 1)
                        sp.dma_start(d["x6"][bass.ds(bB * NT, NT)].rearrange("j p c -> p j c"), x3[:]).then_inc(B_out, 16)
                        sp.wait_ge(B_sh, 2)
                        sp.dma_start(d["acc"][0][0:TILES * P].rearrange("(j p) c -> j p c", p=P)[bass.ds(bB * NT, NT)]
                                     .rearrange("j p c -> p j c"), as_tokens(wkv[4])).then_inc(B_out, 16)
                        sp.wait_ge(B_out, 32)

                @block.tensor
                def _(pe):
                    def fill(n):
                        if n >= 2:
                            pe.wait_ge(*read_off[n - 2])
                        return bank(n)

                    def transposed(n, m, src=hB):
                        if m:
                            pe.wait_ge(B_h, m)
                        for k in range(NC):
                            to = fill(n + k)
                            for j in range(NT):
                                ins = pe.transpose(to[:, j * P:(j + 1) * P], src[:, j, k * P:(k + 1) * P], ident[:])
                            ins.then_inc(B_mm, 1)

                    def channels(n, w, rows, cols, src, kt=NC):
                        to = fill(n)
                        for k in range(kt):
                            ins = pe.matmul(to[0:rows, :], w[:, k, cols:cols + rows], src[:, k, :],
                                            start=(k == 0), stop=(k == kt - 1))
                        ins.then_inc(B_mm, 1)

                    def gate_up_product(m, part):
                        cols = P if m < NI - 1 else ILAST
                        up, k = divmod(part, 2)
                        n, w = F_GU + 2 * m + up, (wgate, wup)[up]
                        to = fill(n) if k == 0 else bank(n)
                        ins = pe.matmul(to[0:cols, :], w[:, k, m * P:m * P + cols], hT[:, k, :], start=(k == 0), stop=(k == 1))
                        if k == 1:
                            ins.then_inc(B_mm, 1)

                    def down_product(i):
                        j, k = divmod(i, NI)
                        n = F_DOWN + j // 2
                        if i == 0:
                            pe.wait_ge(B_hid, NI)
                        to = fill(n) if j % 2 == 0 and k == 0 else bank(n)
                        end = P if k < NI - 1 else ILAST
                        ins = pe.matmul(to[:, (j % 2) * C:(j % 2 + 1) * C], big[0:end, k, j * P:(j + 1) * P], wdown[0:end, k, :],
                                        start=(k == 0), stop=(k == NI - 1))
                        if j % 2 and k == NI - 1:
                            ins.then_inc(B_mm, 1)

                    def tokens(n, src, w, kt, width=C, last=P):
                        for half in range(2):
                            to = fill(n + half)
                            for j in range(2):
                                at = (2 * half + j) * P
                                for k in range(kt):
                                    rows = last if k == kt - 1 else P
                                    ins = pe.matmul(to[:, j * width:(j + 1) * width], src[0:rows, k, at:at + P],
                                                    w[0:rows, k, :], start=(k == 0), stop=(k == kt - 1))
                            ins.then_inc(B_mm, 1)

                    def project_to(to, w0, m):
                        for k in range(NC):
                            ins = pe.matmul(psum[0:m, to, :], wq[:, k, w0:w0 + m], hAT[:, k, :],
                                            start=(k == 0), stop=(k == NC - 1))
                        return ins

                    def project_queries():
                        pe.wait_ge(A_h, 1)
                        if doA:
                            pe.wait_ge(sc_exp, 3 * PAIRS)
                        for k in range(NC):
                            for j in range(NT):
                                ins = pe.transpose(psum[:, k, j * P:(j + 1) * P], hA[:, j, k * P:(k + 1) * P], ident[:])
                            ins.then_inc(A_mm, 1)
                        pe.wait_ge(A_hT, 2)
                        for i in range(NC):
                            ins = project_to(2 + i, i * P, P)
                        ins.then_inc(A_mm, 1)
                        for i in range(NC):
                            ins = project_to(i, C + i * P, P)
                        ins.then_inc(A_mm, 1)

                    def project_keys():
                        project_to(4, 2 * C, WQK).then_inc(A_mm, 1)
                        if doA:
                            pe.wait_ge(pv_rd, HKV)
                        project_to(5, 2 * C + WQK, WQK).then_inc(A_mm, 1)
                        pe.wait_ge(A_qk, 1)
                        for j in range(NT):
                            for k in range(NC):
                                ins = pe.matmul(psum[:, 2, j * WQK:(j + 1) * WQK], hAT[:, k, j * P:(j + 1) * P],
                                                wv0[:, k, :], start=(k == 0), stop=(k == NC - 1))
                        ins.then_inc(A_mm, 1)

                    def ranks():
                        pe.wait_ge(C_mask, 1)
                        pe.matmul(psum[:, 0, 2 * P:2 * P + (NT + 1) * E], trib[:, 1, :], flat(before[:]), start=True, stop=True)
                        pe.matmul(psum[:, 0, 2 * P:2 * P + NT * E], trib[:, 0, :], flat(mask_b[:]), start=False, stop=True,
                                  skip_group_check=True).then_inc(C_pos, 1)

                    def scores_for_max(s):
                        j, i = s // NT, s % NT
                        if s >= 3:
                            pe.wait_ge(mx_rd, s - 2)
                        if s == RANKS and doC:
                            ranks()
                        if s == RANKS + 3 and doC:
                            pe.wait_ge(C_read, 2)
                        for par in range(2):
                            to = 2 * (s % 3) + par
                            pe.matmul(psum[:, to, 0:(i + 1) * P], qst[:, j, i * P:(i + 1) * P],
                                      kst[:, par, j // 2, 0:(i + 1) * P], start=True, stop=True)
                            ins = pe.matmul(psum[:, to, i * P:(i + 1) * P], identb[:], causal[:], start=False, stop=True,
                                            skip_group_check=True)
                        ins.then_inc(mx_mm, 1)

                    def scores(m):
                        for par in range(2):
                            if m:
                                pe.wait_ge(sc_exp, 3 * (m - 1) + par + 1)
                            for i in (0, 1, 3):
                                at = 1024 * par + OFFSETS[i]
                                ins = pe.matmul(pflat[:, at:at + T - i * P], kst[:, par, m // 2, i * P:(i + 1) * P],
                                                qst[:, m, i * P:T], start=True, stop=True)
                            ins.then_inc(sc_mm, 1)
                        if m:
                            pe.wait_ge(sc_exp, 3 * m)
                        for par in range(2):
                            ins = pe.matmul(psum[:, 4, 2 * P * par:2 * P * (par + 1)], kst[:, par, m // 2, 2 * P:3 * P],
                                            qst[:, m, 2 * P:T], start=True, stop=True)
                        ins.then_inc(sc_mm, 1)

                    def values(g):
                        if g:
                            pe.wait_ge(pv_rd, g)
                        for i in range(NT):
                            if i in (0, 2):
                                pe.wait_ge(sc_msk, 8 * g + 6 + i)
                            for q in range(GROUP):
                                h = g * GROUP + q
                                at = OFFSETS[i]
                                ins = pe.matmul(psum[32 * q:32 * q + 32, 5, i * P:T], vaug[:, i, g, :],
                                                probs[:, h % NPB, at:at + T - i * P], start=(i == 0), stop=True,
                                                skip_group_check=True)
                        ins.then_inc(pv_mm, 1)

                    hT = hBT[:, :, 1:T + 1]
                    if doB:
                        transposed(F_T1, 0)
                        pe.wait_ge(B_hT, 2)
                    for s in range(STEPS):
                        if doA:
                            scores_for_max(s)
                        elif doC and s == RANKS:
                            ranks()
                        if doB and s < 4 * NI:
                            gate_up_product(s // 4, s % 4)
                        elif doB and s >= DOWN_FROM:
                            n = N_DOWN - DOWN_AFTER
                            for i in range(n):
                                if s == DOWN_FROM + i * (STEPS - DOWN_FROM) // n:
                                    down_product(i)
                    if doA:
                        pe.wait_ge(mx_rd, STEPS)
                        pe.transpose(psum[:, 4, 0:P], negmax[:].rearrange("p i h -> p (i h)"), ident[:]).then_inc(nm_t, 1)
                    if doB:
                        for i in range(N_DOWN - DOWN_AFTER, N_DOWN):
                            down_product(i)
                    if doA:
                        pe.wait_ge(nm_in, 64)
                    for m in range(PAIRS):
                        if doA:
                            scores(m)
                            if m % 2 == 0 and m:
                                values(m // 2 - 1)
                        if doB:
                            if m == LAGS["t2"]:
                                transposed(F_T2, 1)
                            for i, (n, w, at) in enumerate(((F_K, wk1, "k"), (F_V, wv1, "v"), (F_R, wr1, "r"))):
                                if m == LAGS[at]:
                                    pe.wait_ge(B_xs, i + 1)
                                    for k in range(NC):
                                        channels(n + k, w, P, k * P, wkv[1 + i])
                    if doA:
                        values(HKV - 1)
                    if doB:
                        pe.wait_ge(B_rwkv, 1)
                        tokens(F_WO, wkv[0], wo1, NC)
                    if doP:
                        project_queries()
                    if doB:
                        transposed(F_T3, 2)
                    if doP:
                        project_keys()
                    if doB:
                        pe.wait_ge(B_xs, 4)
                        for f in range(NF):
                            channels(F_CK + f, wck, P, f * P, wkv[4])
                        pe.wait_ge(B_xs, 5)
                        tokens(F_CR, wkv[5], wcr, NC)
                    if doB:
                        pe.wait_ge(B_kf, NF)
                        tokens(F_CV, big, wcv, NF)
                    if doA:
                        pe.wait_ge(A_att, 1)
                        if not doB:
                            pe.wait_ge(later, 16 * N_LATER)
                        if doP:
                            pe.wait_ge(A_qk, 2)
                        for j in range(NT):
                            for k in range(NC):
                                ins = pe.matmul(psum[:, j // 2, (j % 2) * C:(j % 2 + 1) * C], attT[:, k, j * P:(j + 1) * P],
                                                wo0[:, k, :], start=(k == 0), stop=(k == NC - 1))
                        ins.then_inc(A_wo, 1)
                    if doB:
                        transposed(F_T4, 3, routed)
                        pe.wait_ge(B_hT, 8)
                        channels(F_SG, wsg, P, 0, hT)
                        channels(F_SU, wsu, P, 0, hT)
                        tokens(F_LG, hT, wrt, NC, width=E)
                        pe.wait_ge(B_si, 1)
                        tokens(F_SD, wkv[3][:, 0:1, :], wsd[:].rearrange("p (o c) -> p o c", o=1), 1)

                @block.scalar
                def _(act):
                    def transposed(n, w=None, b=None):
                        for k in range(NC):
                            act.wait_ge(B_mm, n + k + 1)
                            if w is None:
                                act.activation(hBT[:, k, 1:T + 1], bank(n + k), ACT.Copy).then_inc(B_hT, 1)
                            else:
                                act.activation(hBT[:, k, 1:T + 1], bank(n + k), ACT.Identity, scale=vecs[:, w, k:k + 1],
                                               bias=vecs[:, b, k:k + 1]).then_inc(B_hT, 1)

                    def read(n, out, func=ACT.Copy, scale=1.0, rows=P):
                        act.wait_ge(B_mm, n + 1)
                        act.activation(out, bank(n)[0:rows, :], func, scale=scale).then_inc(B_sc, 1)

                    def read_values(g):
                        act.wait_ge(pv_mm, g + 1)
                        if g >= 2:
                            act.wait_ge(ho_out[g % 2], 16 * (g // 2))
                        act.activation(hout[:, g % 2, :], psum[:, 5, :], ACT.Copy).then_inc(pv_rd, 1)

                    def pair_exps(m):
                        at = 2 * m % NPB
                        if 2 * m >= NPB:
                            act.wait_ge(pv_mm, (2 * m - NPB) // GROUP + 1)
                        for par in range(2):
                            act.wait_ge(sc_mm, 3 * m + par + 1)
                            act.activation(probs[:, at + par, 0:OWN], pflat[:, 1024 * par:1024 * par + OWN], ACT.Exp,
                                           scale=SCALE).then_inc(sc_exp, 1)
                        act.wait_ge(sc_mm, 3 * m + 3)
                        act.activation(probs[:, at:at + 2, OWN:REGION], psum[:, 4, :].rearrange("p (h t) -> p h t", h=2),
                                       ACT.Exp, scale=SCALE).then_inc(sc_exp, 1)

                    def cast(n, out, src):
                        act.wait_ge(A_rest, n)
                        act.activation(out, src, ACT.Copy).then_inc(A_cast, 1)

                    if doB:
                        transposed(F_T1)
                    if doC:
                        act.wait_ge(C_abs, 1)
                        act.activation(a1, a0, ACT.Exp, scale=-1.0).then_inc(C_s, 1)
                        act.wait_ge(C_log, 1)
                        act.activation(a0, a2, ACT.Ln).then_inc(C_s, 1)
                    for m in range(NI):
                        if m == 1 and doC:
                            act.wait_ge(C_plus, 1)
                            act.activation(score, a0, ACT.Sqrt).then_inc(C_s, 1)
                        if doB:
                            rows = P if m < NI - 1 else ILAST
                            g, u = F_GU + 2 * m, F_GU + 2 * m + 1
                            if m >= 2:
                                act.wait_ge(B_gate, m - 1)
                            else:
                                act.wait_ge(B_hT, 2)
                            read(g, th[0:rows, m % 2, :], ACT.Tanh, ghalf[0:rows, m:m + 1], rows)
                            if m >= 2:
                                act.wait_ge(B_hid, m - 1)
                            read(u, ut[0:rows, m % 2, :], scale=gus[0:rows, m:m + 1], rows=rows)
                    for m in range(PAIRS):
                        if doA:
                            pair_exps(m)
                            if m % 2 and m > 1:
                                read_values(m // 2 - 1)
                        if doB:
                            if m == LAGS["t2"]:
                                transposed(F_T2, LN1W, LN1B)
                            if m == LAGS["k"]:
                                for k in range(NC):
                                    read(F_K + k, wkv[4][:, k, :])
                            if m == LAGS["v"]:
                                for k in range(NC):
                                    read(F_V + k, wkv[5][:, k, :])
                            if m == LAGS["r"]:
                                for k in range(NC):
                                    read(F_R + k, th[:, k, :], ACT.Tanh, 0.5)
                            for i, t in enumerate((0, 1, 3, 2)):
                                if m == LAGS["args"][i]:
                                    act.wait_ge(B_arg, i + 1)
                                    act.activation(wkv[t], wkv[t], ACT.Exp).then_inc(B_sc, 1)
                    if doA:
                        read_values(HKV - 1)
                    if doP:
                        for k in range(NC):
                            act.wait_ge(A_mm, k + 1)
                            act.activation(hAT[:, k, :], psum[:, k, :], ACT.Copy).then_inc(A_hT, 1)
                    if doB:
                        transposed(F_T3, LN2W, LN2B)
                    if doP:
                        cast(1, qparts[:, 0], r1[:])
                        cast(2, kparts[:, 0], kr1)
                        act.wait_ge(A_mm, 7)
                        act.activation(vaug[:, :, :, 0:D], psum[:, 2, 0:NT * WQK].rearrange("p (j g d) -> p j g d", g=HKV, d=D),
                                       ACT.Copy).then_inc(A_vaug, 1)
                    for f in range(NF):
                        if doB:
                            read(F_CK + f, big[:, f, :], ACT.Relu)
                        if doP and f in (1, 2):
                            cast(2 + f, (qparts[:, 1], kparts[:, 1])[f - 1], (r2[:], kr2)[f - 1])
                    if doB:
                        for k in range(2):
                            read(F_CR + k, th[:, k, :], ACT.Tanh, 0.5)
                        transposed(F_T4)
                        read(F_SG, th[:, 0, :], ACT.Tanh, 0.5)
                        for k in range(2):
                            act.wait_ge(B_mm, F_SD + k + 1)
                            act.activation(wkv[4][:, k, :], bank(F_SD + k), ACT.Copy).then_inc(B_sh, 1)

                @block.gpsimd
                def _(pool):
                    def deviations(var, n, rs_sem, ve, rs):
                        pool.wait_ge(var, n)
                        pool.tensor_tensor(rs[:], ve[:], mhalf[:], ALU.pow).then_inc(rs_sem, 1)

                    def devB(*ns):
                        for n in ns if doB else ():
                            deviations(B_var, n, B_rs, veB, rsB)

                    def mask(m):
                        for part in range(2):
                            for par in range(2):
                                h = 2 * m % NPB + par
                                if part == 0:
                                    pool.wait_ge(sc_exp, 3 * m + par + 1)
                                    blocks = probs[:, h, 0:1024].rearrange("p (a t) -> p a t", t=512)[:, :, 0:P]
                                else:
                                    pool.wait_ge(sc_exp, 3 * m + 3)
                                    blocks = probs[:, h, 896:1152].rearrange("p (a t) -> p a t", t=P)
                                pool.affine_select(out=blocks, in_=blocks, compare_op=ALU.is_ge, fill=0.0, base=0,
                                                   pattern=[[0, 2], [1, P]], channel_multiplier=-1).then_inc(sc_msk, 1)

                    def hidden(m):
                        rows = P if m < NI - 1 else ILAST
                        pool.wait_ge(B_gate, m + 1)
                        pool.wait_ge(B_sc, S_GU + 2 * m + 2)
                        pool.tensor_tensor(big[0:rows, m, :], big[0:rows, m, :], ut[0:rows, m % 2, :], ALU.mult).then_inc(B_hid, 1)

                    def put_rows(first, last):
                        if first == 0:
                            pool.wait_ge(C_idx, 1)
                        for n in range(first, last):
                            i, k = divmod(n, TOPK)
                            pool.indirect_dma_start(
                                out=d["slots"], out_offset=bass.IndirectOffsetOnAxis(ap=idx[:, i * 8 + k:i * 8 + k + 1], axis=0),
                                in_=routed[:, i, :], in_offset=None, bounds_check=SLOTS - 1, oob_is_err=False)\
                                .then_inc(C_put, 16)

                    for m in range(NI):
                        if doB:
                            hidden(m)
                        if doC and m >= 3:
                            put_rows(4 * (m - 3), 4 * (m - 2) if m < NI - 1 else NT * TOPK)
                    devB(1)
                    for m in range(PAIRS):
                        if m in (1, 3):
                            devB(2 + m // 2)
                        if m == V_LAG and doB:
                            pool.wait_ge(B_sc, S_EXP + 4)
                            pool.wait_ge(B_kv, 1)
                            pool.tensor_tensor(wkv[5], wkv[2], wkv[5], ALU.mult).then_inc(B_ev, 1)
                        if m == 4 and doP:
                            deviations(P_var, 1, P_rs, veP, rsP)
                        if doA:
                            mask(m)
                    devB(4)
                    if doB:
                        for f in range(NF):
                            pool.wait_ge(B_sc, S_KF + f + 1)
                            pool.tensor_tensor(big[:, f, :], big[:, f, :], big[:, f, :], ALU.mult).then_inc(B_kf, 1)
                    devB(5, 6)
                    if doA:
                        deviations(A_var, 1, A_rs, veA, rsA)
                        deviations(B_var, 7 if doB else 1, B_rs, veB, rsB)
                    if doC:
                        pool.wait_ge(C_put, 16 * NT * TOPK)
                        pool.dma_reset(range(C_put.num, C_put.num + 1))

                @block.vector
                def _(dve):
                    linkA, link, linkC = linked(dve, A_link), linked(dve, B_link), linked(dve, C_v)
                    norms = [0]

                    def norm(out, src):
                        norms[0] += 1
                        norm_stats(dve, link, src, stB, mvB, veB, B_var)
                        dve.wait_ge(B_rs, norms[0])
                        return norm_apply(dve, out, src, mvB, rsB)

                    def two(t, half):
                        return t[:, 2 * half:2 * half + 2, :]

                    def banks(n):
                        return bank(n).rearrange("p (j c) -> p j c", c=C)

                    def rotate_queries():
                        cos = rope[:, 0:1, :].broadcast_to([P, NC, T])
                        sin = rope[:, 1:2, :].broadcast_to([P, NC, T])
                        dve.wait_ge(A_mm, 3)
                        dve.tensor_tensor(r1[:], psum[:, 2:4, :], cos, ALU.mult).then_inc(A_qk, 1)
                        dve.wait_ge(A_mm, 4)
                        dve.tensor_tensor(r2[:], psum[:, 0:2, :], sin, ALU.mult).then_inc(A_qk, 1)
                        dve.wait_ge(A_qk, 2)
                        dve.tensor_tensor(r1[:], r1[:], r2[:], ALU.add).then_inc(A_rest, 1)

                    def rotate_keys():
                        dve.wait_ge(A_mm, 5)
                        dve.tensor_tensor(kr1, psum[0:WQK, 4, :], rope[0:WQK, 0, :], ALU.mult).then_inc(A_qk, 1)
                        dve.wait_ge(A_mm, 6)
                        dve.tensor_tensor(kr2, psum[0:WQK, 5, :], rope[0:WQK, 1, :], ALU.mult).then_inc(A_qk, 1)
                        dve.wait_ge(A_qk, 4)
                        dve.tensor_tensor(kr1, kr1, kr2, ALU.add).then_inc(A_rest, 1)

                    def split():
                        dve.wait_ge(A_cast, 1)
                        dve.tensor_tensor(r2[:], r1[:], qparts[:, 0], ALU.subtract).then_inc(A_rest, 1)
                        dve.wait_ge(A_cast, 2)
                        dve.wait_ge(A_rest, 2)
                        dve.tensor_tensor(kr2, kr1, kparts[:, 0], ALU.subtract).then_inc(A_rest, 1)
                        dve.wait_ge(A_cast, 3)
                        dve.wait_ge(A_rest, 3)
                        dve.tensor_tensor(qparts[:, 2], r2[:], qparts[:, 1], ALU.subtract).then_inc(A_parts, 1)
                        dve.wait_ge(A_cast, 4)
                        dve.wait_ge(A_rest, 4)
                        dve.tensor_tensor(kparts[:, 2], kr2, kparts[:, 1], ALU.subtract).then_inc(A_parts, 1)

                    def maximum(s):
                        j, i = s // NT, s % NT
                        dve.wait_ge(mx_mm, s + 1)
                        to = 2 * (s % 3)
                        dve.tensor_reduce(negmax[:, i, 2 * j:2 * j + 2], psum[:, to:to + 2, 0:(i + 1) * P], AX.X,
                                          ALU.max, negate=True).then_inc(mx_rd, 1)

                    def gate(m):
                        rows = P if m < NI - 1 else ILAST
                        dve.wait_ge(B_sc, S_GU + 2 * m + 1)
                        dve.scalar_tensor_tensor(big[0:rows, m, :], th[0:rows, m % 2, :], 1.0, bank(F_GU + 2 * m)[0:rows, :],
                                                 ALU.add, ALU.mult).then_inc(B_gate, 1)

                    def mixtures(diff, outs):
                        link(dve.tensor_tensor(diff, hBT[:, :, 1:T + 1], hBT[:, :, 0:T], ALU.subtract))
                        for out, vec in outs:
                            for k in range(NC):
                                ins = dve.scalar_tensor_tensor(out[:, k, :], diff[:, k, :], vecs[:, vec, k:k + 1],
                                                               hBT[:, k, 0:T], ALU.mult, ALU.add)
                            ins.then_inc(B_xs, 1)

                    def swiglu_out():
                        for half in range(2):
                            n = F_DOWN + half
                            dve.wait_ge(B_mm, n + 1)
                            dve.tensor_tensor(two(hB, half), banks(n), ds[:].rearrange("p (o c) -> p o c", o=1)
                                              .broadcast_to([P, 2, C]), ALU.mult).then_inc(B_down, 1)
                        dve.wait_ge(B_down, 2)
                        link(norm(hB, hB))
                        dve.tensor_tensor(x3[:], x2[:], hB[:], ALU.add).then_inc(B_x3, 1)
                        dve.wait_ge(B_x3, 1)

                    def time_mixing():
                        dve.wait_ge(B_hT, 4)
                        mixtures(wkv[0], ((wkv[1], TMK), (wkv[2], TMV), (wkv[3], TMR)))
                        k_, v_ = wkv[4], wkv[5]
                        dve.wait_ge(B_sc, S_K + 2)
                        for k in range(NC):
                            ins = dve.tensor_tensor_scan(pp[:, k, 1:T + 1], decay[:, k:k + 1].broadcast_to([P, T]), k_[:, k, :],
                                                         -1e38, ALU.add, ALU.max)
                        link(ins)
                        old, new = pp[:, :, 0:T], pp[:, :, 1:T + 1]
                        for k in range(NC):
                            ins = dve.scalar_tensor_tensor(wkv[0][:, k, :], old[:, k, :], decay[:, k:k + 1], new[:, k, :],
                                                           ALU.add, ALU.subtract)
                        ins.then_inc(B_arg, 1)
                        dve.tensor_tensor(wkv[1], k_, new, ALU.subtract).then_inc(B_arg, 1)
                        dve.wait_ge(B_mm, F_V + 2)
                        for k in range(NC):
                            ins = dve.scalar_tensor_tensor(wkv[2][:, k, :], k_[:, k, :], vecs[:, TFIRST, k:k + 1], old[:, k, :],
                                                           ALU.add, ALU.max)
                        link(ins)
                        dve.wait_ge(B_mm, F_R + 2)
                        dve.tensor_tensor(wkv[3], old, wkv[2], ALU.subtract).then_inc(B_arg, 1)
                        dve.wait_ge(B_arg, 3)
                        for k in range(NC):
                            ins = dve.scalar_tensor_tensor(wkv[2][:, k, :], k_[:, k, :], vecs[:, TFIRST, k:k + 1],
                                                           wkv[2][:, k, :], ALU.add, ALU.subtract)
                        ins.then_inc(B_arg, 1)
                        dve.wait_ge(B_arg, 4)
                        dve.wait_ge(B_sc, S_EXP + 2)
                        dve.tensor_tensor(k_, wkv[1], v_, ALU.mult).then_inc(B_kv, 1)
                        dve.wait_ge(B_kv, 1)
                        for k in range(NC):
                            dve.tensor_tensor_scan(aa[:, k, 1:T + 1], wkv[0][:, k, :], k_[:, k, :], 0.0, ALU.mult, ALU.add)
                            ins = dve.tensor_tensor_scan(bb[:, k, 1:T + 1], wkv[0][:, k, :], wkv[1][:, k, :], 0.0,
                                                         ALU.mult, ALU.add)
                        link(ins)
                        dve.wait_ge(B_sc, S_EXP + 4)
                        dve.tensor_tensor(wkv[0], wkv[3], aa[:, :, 0:T], ALU.mult)
                        link(dve.tensor_tensor(k_, wkv[3], bb[:, :, 0:T], ALU.mult))
                        dve.wait_ge(B_ev, 1)
                        dve.tensor_tensor(wkv[0], wkv[0], v_, ALU.add)
                        link(dve.tensor_tensor(k_, k_, wkv[2], ALU.add))
                        link(dve.reciprocal(k_, k_))
                        link(dve.scalar_tensor_tensor(k_, th[:], 1.0, k_, ALU.add, ALU.mult))
                        dve.scalar_tensor_tensor(wkv[0], wkv[0], 0.5, k_, ALU.mult, ALU.mult).then_inc(B_rwkv, 1)
                        for half in range(2):
                            n = F_WO + half
                            dve.wait_ge(B_mm, n + 1)
                            dve.tensor_tensor(two(z, half), two(z, half), banks(n), ALU.add).then_inc(B_wo, 1)
                        dve.wait_ge(B_wo, 2)

                    def mixing_out():
                        for half in range(2):
                            n = F_CV + half
                            dve.wait_ge(B_sc, S_CR + half + 1)
                            dve.wait_ge(B_mm, n + 1)
                            dve.scalar_tensor_tensor(two(hB, half), as_tokens(th[:])[:, 2 * half:2 * half + 2, :], 1.0,
                                                     banks(n), ALU.add, ALU.mult).then_inc(B_cv, 1)
                        dve.wait_ge(B_cv, 2)
                        link(dve.scalar_tensor_tensor(z[:], hB[:], 0.5, z[:], ALU.mult, ALU.add))
                        link(norm(hB, z))
                        dve.tensor_tensor(x3[:], x3[:], hB[:], ALU.add).then_inc(B_x6, 1)
                        dve.wait_ge(B_x6, 1)

                    def route_start():
                        dve.scalar_tensor_tensor(a0, lg[:], -1.0, lg[:], ALU.mult, ALU.max).then_inc(C_abs, 1)
                        linkC(dve.memset(before[:, 0, :], 0.0))
                        linkC(dve.memset(sel[:, :, E:E + 2], BIG))

                    def route_root():
                        dve.wait_ge(C_s, 1)
                        dve.tensor_scalar(a2, a1, 1.0, None, ALU.add).then_inc(C_log, 1)
                        dve.wait_ge(C_log, 1)
                        linkC(dve.tensor_scalar(a3, a2, -1.0, None, ALU.add))
                        linkC(dve.tensor_scalar(mask, a3, 0.0, None, ALU.is_equal))
                        linkC(dve.tensor_scalar(a3, a3, 1e-30, None, ALU.max))
                        linkC(dve.reciprocal(a3, a3))
                        dve.wait_ge(C_s, 2)
                        linkC(dve.tensor_tensor(a0, a0, a1, ALU.mult))
                        linkC(dve.tensor_tensor(a0, a0, a3, ALU.mult))
                        linkC(dve.tensor_tensor(a1, a1, mask, ALU.mult))
                        linkC(dve.tensor_tensor(a0, a0, a1, ALU.add))
                        dve.scalar_tensor_tensor(a0, lg[:], 0.0, a0, ALU.max, ALU.add).then_inc(C_plus, 1)

                    def route_choose():
                        dve.wait_ge(C_s, 3)
                        linkC(dve.tensor_tensor(sel[:, :, 0:E], score, biasr[:].rearrange("p (o e) -> p o e", o=1)
                                                .broadcast_to(TE), ALU.add))
                        for i in range(NT):
                            ins = dve.max(top[:, i, :], sel[:, i, :])
                        linkC(ins)
                        for i in range(NT):
                            ins = dve.match_replace(out=rep[:, i, :], in_to_replace=top[:, i, :], in_values=sel[:, i, :],
                                                    imm_value=-BIG)
                        linkC(ins)
                        linkC(dve.tensor_scalar(mask, rep[:, :, 0:E], -0.5 * BIG, None, ALU.is_le))
                        linkC(dve.tensor_copy(mask_b[:], mask))
                        for i in range(NT):
                            ins = dve.tensor_tensor(before[:, i + 1, :], before[:, i, :], mask[:, i, :], ALU.add)
                            if i + 1 < NT:
                                linkC(ins)
                        ins.then_inc(C_mask, 1)
                        linkC(dve.tensor_tensor(weight, mask, score, ALU.mult))
                        linkC(dve.tensor_reduce(total, weight, AX.X, ALU.add))
                        linkC(dve.reciprocal(total, total))
                        linkC(dve.scalar_tensor_tensor(weight, weight, 1.5, total.rearrange("p (i o) -> p i o", o=1)
                                                       .broadcast_to(TE), ALU.mult, ALU.mult))

                    def route_slots():
                        dve.wait_ge(C_pos, 1)
                        ranks = psum[:, 0, 2 * P:2 * P + NT * E].rearrange("p (i e) -> p i e", e=E)
                        dve.tensor_tensor(a1, ranks, seen[:].rearrange("p (o e) -> p o e", o=1).broadcast_to(TE), ALU.add)\
                            .then_inc(C_read, 1)
                        dve.wait_ge(C_read, 1)
                        dve.tensor_tensor(seen[:], seen[:], psum[:, 0, 2 * P + NT * E:2 * P + (NT + 1) * E], ALU.add).then_inc(C_read, 1)
                        linkC(dve.scalar_tensor_tensor(valid, a1, float(CAP), mask, ALU.is_lt, ALU.mult))
                        linkC(dve.tensor_tensor(a1, a1, slotb[:].rearrange("p (o e) -> p o e", o=1).broadcast_to(TE), ALU.add))
                        linkC(dve.tensor_tensor(slot, a1, valid, ALU.mult))
                        linkC(dve.tensor_tensor(routed[:, :, C + 1:ROW], weight, valid, ALU.mult))
                        for i in range(NT):
                            ins = dve.max(slot8[:, i, :], slot[:, i, :])
                        linkC(ins)
                        linkC(dve.tensor_scalar(s8, slot8, 0.0, OOB, ALU.is_equal, ALU.mult))
                        linkC(dve.scalar_tensor_tensor(s8, slot8, -1.0, s8, ALU.add, ALU.add))
                        dve.tensor_copy(idx[:], s8.rearrange("p i k -> p (i k)")).then_inc(C_idx, 1)
                        dve.wait_ge(C_idx, 1)

                    def shared_hidden():
                        dve.wait_ge(B_sc, S_SG + 1)
                        si = wkv[3][:, 0, :]
                        dve.scalar_tensor_tensor(si, th[:, 0, :], 1.0, bank(F_SG), ALU.add, ALU.mult).then_inc(B_sg, 1)
                        dve.wait_ge(B_sg, 1)
                        dve.wait_ge(B_mm, F_SU + 1)
                        dve.scalar_tensor_tensor(si, si, 0.5, bank(F_SU), ALU.mult, ALU.mult).then_inc(B_su, 1)
                        dve.wait_ge(B_su, 1)
                        dve.tensor_scalar(si, si, 10.0, -10.0, ALU.min, ALU.max).then_inc(B_si, 1)
                        for half in range(2):
                            n = F_LG + half
                            dve.wait_ge(B_mm, n + 1)
                            dve.tensor_copy(two(lg, half), bank(n)[:, 0:2 * E].rearrange("p (j c) -> p j c", c=E))\
                                .then_inc(B_lg, 1)

                    if doC:
                        route_start()
                    for s in range(STEPS):
                        if doA:
                            maximum(s)
                        for at, step in ((1, route_root), (5, route_choose), (RANKS, route_slots)) if doC else ():
                            if s == at:
                                step()
                        if doB and s % 4 == 2 and s // 4 < NI:
                            gate(s // 4)
                    if doA:
                        dve.wait_ge(nm_t, 1)
                        linkA(dve.tensor_copy(nmparts[:, 0, :], psum[:, 4, 0:P]))
                        dve.tensor_tensor(nmparts[:, 1, :], psum[:, 4, 0:P], nmparts[:, 0, :], ALU.subtract).then_inc(nm_s, 1)
                    if doB:
                        swiglu_out()
                        link(norm(z, x3))
                        norm(hB, z).then_inc(B_h, 1)
                    if doP:
                        if project:
                            dve.wait_ge(A_in, 16)
                        norm_stats(dve, linkA, hA, stP, mvP, veP, P_var)
                        dve.wait_ge(P_rs, 1)
                        norm_apply(dve, hA, hA, mvP, rsP).then_inc(A_h, 1)
                    if doB:
                        time_mixing()
                        norm(hB, z).then_inc(B_h, 1)
                    if doP:
                        rotate_queries()
                    if doB:
                        dve.wait_ge(B_hT, 6)
                        mixtures(aa[:, :, 1:T + 1], ((wkv[4], CMK), (wkv[5], CMR)))
                    if doP:
                        rotate_keys()
                        split()
                    if doA:
                        dve.wait_ge(den_in, 16 * HKV)
                        dve.reciprocal(den, den).then_inc(A_rden, 1)
                        dve.wait_ge(att_in, 16 * HKV)
                        dve.wait_ge(rden_in, 16 * NC)
                        dve.tensor_tensor(attT, attT, rdenb[:], ALU.mult).then_inc(A_att, 1)
                    if doB:
                        mixing_out()
                        if doC:
                            dve.wait_ge(C_put, 16 * NT * TOPK)
                        link(dve.tensor_copy(routed[:, :, C], tok[:]))
                        link(dve.tensor_scalar(tok[:], tok[:], float(T), None, ALU.add))
                        norm(routed[:, :, 0:C], x3).then_inc(B_h, 1)
                    if doA:
                        dve.wait_ge(A_wo, 1)
                        out = psum[:, 0:2, :].rearrange("p a (j c) -> p (a j) c", c=C)
                        norm_stats(dve, linkA, out, stA, mvA, veA, A_var)
                        dve.wait_ge(A_rs, 1)
                        att = as_tokens(attT)
                        linkA(norm_apply(dve, att, out, mvA, rsA))
                        dve.wait_ge(A_again, 16)
                        linkA(dve.tensor_tensor(x2[:], x2[:], att, ALU.add))
                    if doB:
                        shared_hidden()
                    if doA:
                        norm(hB, x2)
            nc.multi_engine_barrier(mybir.ALL_ENGINES, sems_to_clear=range(sems[0].num, sems[-1].num + 1))

        iteration(project=0)
        iteration(project=1, attend=0)
        iteration(project=2, attend=1, bB=0)
        iteration(project=3, attend=2, bB=1, doC=True)
        iteration(attend=3, bB=2, doC=True)
        iteration(bB=3, doC=True)
        iteration(doC=True)


def experts(nc, a, d, x6):
    AHEAD, WIDE = 8, 4
    with ExitStack() as ctx:
        def sb(name, shape, dt=F32):
            return ctx.enter_context(nc.sbuf_tensor(name, shape, dt))

        def each(name, n=AHEAD):
            return [ctx.enter_context(nc.semaphore(f"{name}{q}")) for q in range(n)]

        xs = sb("xs", [CAP, AHEAD, C + 1])
        wt = sb("wt", [CAP, AHEAD])
        we = sb("we", [P, AHEAD, NC * 2 * EI + C])
        xT = sb("xT", [P, AHEAD, NC * CAP])
        the = sb("the", [CAP, AHEAD, EI])
        hid = sb("hid", [CAP, AHEAD, EI])
        hidT = sb("hidT", [P, AHEAD, CAP])
        ye = sb("ye", [CAP, AHEAD, C])
        idx = sb("idx_e", [CAP, AHEAD], U32)
        ident = sb("ident_e", [P, P])
        ps = ctx.enter_context(nc.psum_tensor("ps_e", [P, 8, 512], F32))
        id_in = ctx.enter_context(nc.semaphore("id_in"))
        x6_in = ctx.enter_context(nc.semaphore("x6_in"))
        e_in, e_xt, e_xTs, e_gu, e_th, e_g, e_hid, e_ht, e_hTs, e_y, e_ys, e_idx = (each(n) for n in (
            "e_in", "e_xt", "e_xTs", "e_gu", "e_th", "e_g", "e_hid", "e_ht", "e_hTs", "e_y", "e_ys", "e_idx"))
        e_put = each("e_put", NACC)
        ye_free = ctx.enter_context(nc.semaphore("ye_free"))
        block = ctx.enter_context(nc.Block())

        def groups():
            return [range(g, g + WIDE) for g in range(0, AHEAD, WIDE)]

        def at(q):
            return 2 * (q % WIDE), 2 * (q % WIDE) + 1

        @block.sync
        def _(sp):
            sp.dma_start(ident[:], a["ident"]).then_inc(id_in, 16)
            with sp.Fori(0, E // AHEAD) as p:
                for q in range(AHEAD):
                    e = p * AHEAD + q
                    table = d["slots"].rearrange("(e s) c -> e s c", s=CAP)
                    sp.wait_ge(e_ys[q], p + 1)
                    sp.dma_start(xs[:, q, :], table[bass.ds(e, 1), :, 0:C + 1].rearrange("o s c -> (o s) c")).then_inc(e_in[q], 16)
                    sp.dma_start(wt[:, q:q + 1], table[bass.ds(e, 1), :, bass.ds(e + C + 1, 1)]
                                 .rearrange("o s c -> (o s) c"), allow_slow_non_contiguous=True).then_inc(e_in[q], 16)
                    sp.dma_start(we[:, q, :], a["we"][bass.ds(e, 1)].rearrange("o p n -> (o p) n")).then_inc(e_in[q], 16)
            sp.dma_start(x6[:], d["x6"].rearrange("i p c -> p i c")).then_inc(x6_in, 16)
            sp.wait_ge(x6_in, 16)

        @block.tensor
        def _(pe):
            pe.wait_ge(id_in, 16)
            with pe.Fori(0, E // AHEAD) as p:
                for group in groups():
                    for q in group:
                        pe.wait_ge(e_in[q], p * 48 + 48)
                        before = q - WIDE if q >= WIDE else q - WIDE + AHEAD
                        pe.wait_ge(e_hTs[before], p + (2 if q >= WIDE else 1))
                        for k in range(NC):
                            ins = pe.transpose(ps[:, at(q)[0], k * CAP:(k + 1) * CAP], xs[:, q, k * P:(k + 1) * P],
                                               ident[0:CAP, 0:CAP])
                        ins.then_inc(e_xt[q], 1)
                    for q in group:
                        before = q - WIDE if q >= WIDE else q - WIDE + AHEAD
                        pe.wait_ge(e_ys[before], p + (2 if q >= WIDE else 1))
                        pe.wait_ge(e_xTs[q], p + 1)
                        for k in range(NC):
                            ins = pe.matmul(ps[0:CAP, at(q)[1], 0:2 * EI], xT[:, q, k * CAP:(k + 1) * CAP],
                                            we[:, q, k * 2 * EI:(k + 1) * 2 * EI], start=(k == 0), stop=(k == NC - 1))
                        ins.then_inc(e_gu[q], 1)
                    for q in group:
                        pe.wait_ge(e_hid[q], p + 1)
                        pe.transpose(ps[:, at(q)[0], NC * CAP:(NC + 1) * CAP], hid[:, q, :], ident[0:CAP, 0:CAP]).then_inc(e_ht[q], 1)
                    for q in group:
                        pe.wait_ge(e_hTs[q], p + 2)
                        pe.matmul(ps[0:CAP, at(q)[1], 2 * EI:2 * EI + C], hidT[:, q, :], we[:, q, NC * 2 * EI:], start=True, stop=True)\
                            .then_inc(e_y[q], 1)

        @block.scalar
        def _(act):
            for q in range(AHEAD):
                act.sem_inc(e_ys[q], 1)
            act.sem_inc(ye_free, AHEAD)
            with act.Fori(0, E // AHEAD) as p:
                for group in groups():
                    for q in group:
                        act.wait_ge(e_xt[q], p + 1)
                        act.activation(xT[:, q, :], ps[:, at(q)[0], 0:NC * CAP], ACT.Copy).then_inc(e_xTs[q], 1)
                    for q in group:
                        act.wait_ge(e_gu[q], p + 1)
                        act.activation(the[:, q, :], ps[0:CAP, at(q)[1], 0:EI], ACT.Tanh, scale=0.5).then_inc(e_th[q], 1)
                    for q in group:
                        act.wait_ge(e_y[q], p + 1)
                        act.wait_ge(ye_free, p * AHEAD + q + 1)
                        act.activation(ye[:, q, :], ps[0:CAP, at(q)[1], 2 * EI:2 * EI + C], ACT.Copy, scale=wt[:, q:q + 1])\
                            .then_inc(e_ys[q], 1)

        @block.vector
        def _(dve):
            for q in range(AHEAD):
                dve.sem_inc(e_hTs[q], 1)
            with dve.Fori(0, E // AHEAD) as p:
                for group in groups():
                    for q in group:
                        dve.wait_ge(e_in[q], p * 48 + 48)
                        dve.wait_ge(ye_free, p * AHEAD + q + 1)
                        dve.tensor_copy(idx[:, q:q + 1], xs[:, q, C:C + 1]).then_inc(e_idx[q], 1)
                        dve.wait_ge(e_th[q], p + 1)
                        dve.scalar_tensor_tensor(hid[:, q, :], the[:, q, :], 1.0, ps[0:CAP, at(q)[1], 0:EI], ALU.add, ALU.mult)\
                            .then_inc(e_g[q], 1)
                        dve.wait_ge(e_g[q], p + 1)
                        dve.scalar_tensor_tensor(hid[:, q, :], hid[:, q, :], 0.5, ps[0:CAP, at(q)[1], EI:2 * EI], ALU.mult, ALU.mult)\
                            .then_inc(e_hid[q], 1)
                    for q in group:
                        dve.wait_ge(e_ht[q], p + 1)
                        dve.tensor_copy(hidT[:, q, :], ps[:, at(q)[0], NC * CAP:(NC + 1) * CAP]).then_inc(e_hTs[q], 1)

        @block.gpsimd
        def _(pool):
            for e in range(E + NACC):
                if e >= NACC:
                    n = e - NACC
                    pool.wait_ge(e_put[n % NACC], 16 * (n // NACC + 1))
                    pool.sem_inc(ye_free, 1)
                if e < E:
                    q = e % AHEAD
                    pool.wait_ge(e_idx[q], e // AHEAD + 1)
                    pool.wait_ge(e_ys[q], e // AHEAD + 2)
                    pool.indirect_dma_start(
                        out=d["acc"][e % NACC], out_offset=bass.IndirectOffsetOnAxis(ap=idx[:, q:q + 1], axis=0),
                        in_=ye[:, q, :], in_offset=None, bounds_check=(TILES + 1) * P - 1, oob_is_err=True,
                        compute_op=ALU.add).then_inc(e_put[e % NACC], 16)


def combine(nc, d, out, x6):
    with ExitStack() as ctx:
        def sb(name, shape, dt=F32):
            return ctx.enter_context(nc.sbuf_tensor(name, shape, dt))

        def sem(name):
            return ctx.enter_context(nc.semaphore(name))

        acc = sb("acc", [P, NACC, TILES, C])
        st = sb("st", [P, TILES, 6])
        mv = sb("mv", [P, TILES, 2])
        ve = sb("ve", [P, TILES])
        rs = sb("rs", [P, TILES])
        mh = sb("mh", [P, NT])
        c_in = [sem(f"c_in{g}") for g in range(B)]
        c_mh, c_v, c_var, c_rs = sem("c_mh"), sem("c_v"), sem("c_var"), sem("c_rs")
        c_norm, c_done, c_out = sem("c_norm"), sem("c_done"), sem("c_out")
        block = ctx.enter_context(nc.Block())

        def tiles(g):
            return slice(g * NT, (g + 1) * NT)

        @block.sync
        def _(sp):
            for g in range(B):
                for i in range(NACC):
                    sp.dma_start(acc[:, i, tiles(g), :], d["acc"][i][g * T:(g + 1) * T].rearrange("(j p) c -> p j c", p=P))\
                        .then_inc(c_in[g], 16)

        @block.vector
        def _(dve):
            link = linked(dve, c_v)

            def sums(g):
                dve.wait_ge(c_in[g], 16 * NACC)
                link(dve.tensor_tensor(acc[:, 0, tiles(g), :], acc[:, 0, tiles(g), :], acc[:, 1, tiles(g), :], ALU.add))
                for i in range(g * NT, (g + 1) * NT):
                    ins = dve.bn_stats(st[:, i, :], acc[:, 0, i, :])
                link(ins)
                for i in range(g * NT, (g + 1) * NT):
                    ins = dve.bn_aggr(mv[:, i, :], st[:, i, :])
                link(ins)
                dve.tensor_scalar(ve[:, tiles(g)], mv[:, tiles(g), 1], EPS, None, ALU.add).then_inc(c_var, 1)

            def norms(g):
                dve.wait_ge(c_rs, g + 1)
                for i in range(g * NT, (g + 1) * NT):
                    ins = dve.tensor_scalar(acc[:, 0, i, :], acc[:, 0, i, :], mv[:, i, 0:1], rs[:, i:i + 1],
                                            ALU.subtract, ALU.mult)
                ins.then_inc(c_norm, 1)
                dve.wait_ge(c_norm, g + 1)
                dve.tensor_tensor(acc[:, 0, tiles(g), :], acc[:, 0, tiles(g), :], x6[:, tiles(g), :], ALU.add).then_inc(c_done, 1)

            sums(0)
            for g in range(B):
                if g + 1 < B:
                    sums(g + 1)
                norms(g)

        @block.gpsimd
        def _(pool):
            pool.memset(mh[:], -0.5).then_inc(c_mh, 1)
            pool.wait_ge(c_mh, 1)
            for g in range(B):
                pool.wait_ge(c_var, g + 1)
                pool.tensor_tensor(rs[:, tiles(g)], ve[:, tiles(g)], mh[:], ALU.pow).then_inc(c_rs, 1)

        @block.scalar
        def _(act):
            for g in range(B):
                act.wait_ge(c_done, g + 1)
                act.dma_start(out[:, tiles(g), :], acc[:, 0, tiles(g), :]).then_inc(c_out, 16)
            act.wait_ge(c_out, 16 * B)


def build(nc, a, out):
    def dram(name, shape, dt=F32):
        return nc.dram_tensor(name, shape, dt).ap()

    d = {
        "qparts": dram("qparts_d", [3, C, T], BF16), "kparts": dram("kparts_d", [3, HKV * D, T], BF16),
        "negmax": dram("negmax_d", [2, NT, HQ, P], BF16), "heads": dram("heads_d", [HKV, P, T]), "rden": dram("rden_d", [HQ, T]),
        "x6": dram("x6_d", [TILES, P, C]), "slots": dram("slots_d", [SLOTS, ROW]),
        "acc": [dram(f"acc{i}_d", [(TILES + 1) * P, C]) for i in range(NACC)],
    }
    with ExitStack() as ctx:
        later = ctx.enter_context(nc.semaphore("later"))
        batch_phase(nc, a, d, later)
        x6 = ctx.enter_context(nc.sbuf_tensor("x6t", [P, TILES, C], F32))
        experts(nc, a, d, x6)
        combine(nc, d, out.rearrange("b (j p) c -> p (b j) c", p=P), x6)


def kernel(**inputs):
    import concourse.bacc as bacc
    from concourse.bass_utils import run_bass_kernel_spmd

    g = {k: np.asarray(v) for k, v in inputs.items()}
    swap = np.arange(C) ^ 1

    def turned(w):
        return np.ascontiguousarray(np.swapaxes(w, -1, -2))

    def by_channel(v, n):
        full = np.zeros(n * P, v.dtype)
        full[:v.size] = v.reshape(-1)
        return full.reshape(n, P).T

    wq, wk = g["L0_attn_Wq"], g["L0_attn_Wk"]
    pair = (np.arange(P) % D) // 2
    inv = (np.float32(1.0) / np.float32(10000.0) ** (np.arange(D // 2, dtype=np.float32) / np.float32(D // 2))).astype(np.float32)
    angle = (np.arange(T, dtype=np.float32)[None, :] * inv[pair][:, None]).astype(np.float32)
    sign = np.where(np.arange(P) % 2 == 0, -1.0, 1.0)[:, None]
    rope = np.stack([np.cos(angle), np.sin(angle) * sign], axis=1).astype(np.float32)
    p, t = np.arange(P)[:, None], np.arange(P)[None, :]
    arrays = {
        "x": g["L0_attn_x"],
        "wq": np.concatenate([turned(wq), turned(wq[swap]), turned(wk), turned(wk[swap[:HKV * D]])], axis=1),
        "wv0": turned(g["L0_attn_Wv"]), "wo0": turned(g["L0_attn_Wo"]),
        "wgate": turned(g["L0_ffn_gate_w"]), "wup": turned(g["L0_ffn_up_w"]), "wdown": turned(g["L0_ffn_down_w"]),
        "gs": by_channel(g["L0_ffn_gate_s"], NI), "us": by_channel(g["L0_ffn_up_s"], NI), "ds": g["L0_ffn_down_s"],
        "wk1": turned(g["L1_attn_Wk"]), "wv1": turned(g["L1_attn_Wv"]), "wr1": turned(g["L1_attn_Wr"]),
        "wo1": turned(g["L1_attn_Wo"]), "wck": turned(g["L1_attn_Wck"]), "wcv": turned(g["L1_attn_Wcv"]),
        "wcr": turned(g["L1_attn_Wcr"]), "wrt": turned(g["L1_ffn_gate_w"]), "wsg": turned(g["L1_ffn_sg"]),
        "wsu": turned(g["L1_ffn_su"]), "wsd": turned(g["L1_ffn_sd"]), "bias": g["L1_ffn_bias"],
        "vecs": np.stack([by_channel(g["L1_attn_" + n], NC) for n in (
            "ln1_w", "ln1_b", "ln2_w", "ln2_b", "tm_k", "tm_v", "tm_r", "time_decay", "time_first", "cm_k", "cm_r")], axis=1),
        "we": np.concatenate([np.concatenate([turned(g["L1_ffn_w_gate"]), turned(g["L1_ffn_w_up"])], axis=2)
                              .reshape(E, NC, P, 2 * EI).transpose(0, 2, 1, 3).reshape(E, P, NC * 2 * EI),
                              turned(g["L1_ffn_w_down"])], axis=2),
        "rope": rope,
        "ident": np.eye(P, dtype=np.float32),
        "causal": np.where(t > p, NEG, 0.0).astype(np.float32),
        "tri": np.stack([(p < t), np.ones((P, P))], axis=1).astype(np.float32),
        "slotb": np.broadcast_to((np.arange(E) * CAP + 1.0)[None, :], (P, E)).astype(np.float32),
        "tok": (np.arange(NT)[None, :] * P + np.arange(P)[:, None]).astype(np.float32),
    }
    arrays = {f"in_{k}": np.ascontiguousarray(v) for k, v in arrays.items()}
    nc = bacc.Bacc("TRN2", target_bir_lowering=False, num_devices=1)
    a = {k[3:]: nc.dram_tensor(k, v.shape, mybir.dt.from_np(v.dtype), kind="ExternalInput").ap() for k, v in arrays.items()}
    out = nc.dram_tensor("out", (B, T, C), F32, kind="ExternalOutput").ap()
    build(nc, a, out)
    r = run_bass_kernel_spmd(nc, [arrays], core_ids=[0])
    return r.results[0]["out"]
```

```python
from contextlib import ExitStack

import numpy as np

import concourse.bass as bass
from concourse import mybir

ALU = mybir.AluOpType
ACT = mybir.ActivationFunctionType
AX = mybir.AxisListType
F32 = mybir.dt.float32
BF16 = mybir.dt.bfloat16
U32 = mybir.dt.uint32

P = 128
B, T, C = 4, 512, 256
NT = T // P
NC = C // P
HQ, HKV, D = 32, 8, 8
GROUP = HQ // HKV
INTER = 704
NI = (INTER + P - 1) // P
ILAST = INTER - (NI - 1) * P
FFN = 1024
NF = FFN // P
E, TOPK, CAP, EI = 32, 6, 96, 128
SLOTS = E * CAP
TILES = B * NT
EPS = 1e-5
SCALE = D ** -0.5
NEG = -1e30
BIG = 3e38
N_LOADS = 11
AHEAD, WIDE = 8, 4
OOB = float(1 << 20)
ROW = C + 1 + E
NACC = 2

Q_PARTS = (0, 0, 0, 1, 1, 2)
K_PARTS = (0, 1, 2, 0, 1, 0)
ROWS = len(Q_PARTS) * D

REGION = T + 384 + 256 + 128
OFFSETS = {0: 0, 1: 512, 3: 896, 2: 1024}
OWN = 1024



def linked(eng, sem):
    done = [0]

    def link(ins):
        done[0] += 1
        ins.then_inc(sem, 1)
        eng.wait_ge(sem, done[0])
    return link


def flat(t):
    return t.rearrange("p a n -> p (a n)")


def as_tokens(t):
    return flat(t).rearrange("p (j c) -> p j c", c=C)


class Scratch:

    def __init__(self, tensor):
        self.t, self.at = tensor, 0

    def cut(self, shape, dt=F32):
        n = int(np.prod(shape[1:])) // (1 if dt == F32 else 2)
        v = self.t[:, self.at:self.at + n]
        self.at += n
        if dt != F32:
            v = v.bitcast(dt)
        dims = " ".join("abcd"[:len(shape) - 1])
        return v.rearrange(f"p ({dims}) -> p {dims}", **dict(zip("abcd", shape[1:]))) if len(shape) > 2 else v


def transformer(nc, a, d, out, later):
    with ExitStack() as ctx:
        def sb(name, shape, dt=F32):
            return ctx.enter_context(nc.sbuf_tensor(name, shape, dt))

        sems = []

        def sem(name):
            sems.append(ctx.enter_context(nc.semaphore(name)))
            return sems[-1]

        WQK = HKV * D
        wq = sb("wq", [P, NC, 2 * C + 2 * WQK])
        wv0 = sb("wv0", [P, NC, HKV * D])
        wo0 = sb("wo0", [P, NC, C])
        wgate = sb("wgate", [P, NC, INTER])
        wup = sb("wup", [P, NC, INTER])
        wdown = sb("wdown", [P, NI, C])
        gs = sb("gs", [P, NI])
        us = sb("us", [P, NI])
        ghalf = sb("ghalf", [P, NI])
        gus = sb("gus", [P, NI])
        ds = sb("ds", [P, C])
        wk1 = sb("wk1", [P, NC, C])
        wv1 = sb("wv1", [P, NC, C])
        wr1 = sb("wr1", [P, NC, C])
        wo1 = sb("wo1", [P, NC, C])
        wck = sb("wck", [P, NC, FFN])
        wcv = sb("wcv", [P, NF, C])
        wcr = sb("wcr", [P, NC, C])
        wrt = sb("wrt", [P, NC, E])
        wsg = sb("wsg", [P, NC, EI])
        wsu = sb("wsu", [P, NC, EI])
        wsd = sb("wsd", [P, C])
        NVEC = 11
        vecs = sb("vecs", [P, NVEC, NC])
        LN1W, LN1B, LN2W, LN2B, TMK, TMV, TMR, TDEC, TFIRST, CMK, CMR = range(NVEC)
        decay = sb("decay", [P, NC])
        rope = sb("rope", [P, 2, T])
        ident = sb("ident", [P, P])
        identb = sb("identb", [P, P], BF16)
        causal = sb("causal", [P, P], BF16)
        mhalf = sb("mhalf", [P, NT])

        NPB = 6
        probs = sb("probs", [P, NPB, REGION])
        early = Scratch(flat(probs[:]))
        attT = early.cut([P, NC, T])
        hAT = early.cut([P, NC, T])
        qparts = early.cut([P, 3, NC, T], BF16)
        kparts = early.cut([P, 3, T], BF16)[0:WQK]
        kr1 = early.cut([P, T])[0:WQK]
        kr2 = early.cut([P, T])[0:WQK]
        qst = sb("qst", [P, HQ // 2, T], BF16)
        kst = sb("kst", [P, 2, HKV, T], BF16)
        vaug = sb("vaug", [P, NT, HKV, 32])
        negmax = sb("negmax", [P, NT, HQ])
        nmparts = sb("nmparts", [P, 2, P], BF16)
        hout = sb("hout", [P, 2, T])
        r1 = sb("r1", [P, NC, T])
        r2 = sb("r2", [P, NC, T])
        hA = sb("hA", [P, NT, C])
        rdenb = hout
        den = sb("den", [P, P])[:]
        stA = sb("stA", [P, NT, 6])
        mvA = sb("mvA", [P, NT, 2])
        veA = sb("veA", [P, NT])
        rsA = sb("rsA", [P, NT])
        stP = sb("stP", [P, NT, 6])
        mvP = sb("mvP", [P, NT, 2])
        veP = sb("veP", [P, NT])
        rsP = sb("rsP", [P, NT])

        x2 = sb("x2", [P, NT, C])
        x3 = sb("x3", [P, NT, C])
        z = sb("z", [P, NT, C])
        hB = sb("hB", [P, NT, C])
        hBT = sb("hBT", [P, NC, T + 1])
        th = flat(hB[:]).rearrange("p (k t) -> p k t", t=T)
        big = sb("big", [P, NF, T])
        ones = flat(big[:])[0:2, 0:HKV * T // 2].bitcast(BF16)
        ut = flat(z[:]).rearrange("p (k t) -> p k t", t=T)
        wkv = [big[:, 2 * i:2 * i + 2, :] for i in range(4)] + [sb(f"wkv{i}", [P, NC, T])[:] for i in (4, 5)]
        pp = sb("pp", [P, NC, T + 1])
        aa = sb("aa", [P, NC, T + 1])
        bb = sb("bb", [P, NC, T + 1])
        stB = sb("stB", [P, NT, 6])
        mvB = sb("mvB", [P, NT, 2])
        veB = sb("veB", [P, NT])
        rsB = sb("rsB", [P, NT])
        ve2 = sb("ve2", [P, NT])
        rs2 = sb("rs2", [P, NT])
        lg = sb("lg", [P, NT, E])

        routed = sb("routed", [P, NT, ROW])
        tok = sb("tok", [P, NT])
        seen = sb("seen", [P, E])
        biasr = sb("biasr", [P, E])
        slotb = sb("slotb", [P, E])
        trib = sb("trib", [P, 2, P], BF16)
        idx = sb("idx", [P, NT * 8], U32)
        mask_b = sb("mask_b", [P, NT, E], BF16)
        before = sb("before", [P, NT + 1, E], BF16)
        free4, free5 = Scratch(flat(wkv[4])), Scratch(flat(wkv[5]))
        TE = [P, NT, E]
        a0, a1, a2, a3, score, mask, valid = (free4.cut(TE) for _ in range(7))
        sel, rep, weight, total, slot, top, slot8, s8 = (free5.cut(shape) for shape in (
            [P, NT, E + 2], [P, NT, E + 2], TE, [P, NT], TE, [P, NT, 8], [P, NT, 8], [P, NT, 8]))

        psum = ctx.enter_context(nc.psum_tensor("psum", [P, 8, 512], F32))
        pflat = flat(psum[:])

        tiles = {"we": probs, "xs": qst, "hid": kst, "small": x2, "ye": wck, "x6": big, "last": r1, "norm": hBT}
        tiles = {name: Scratch(t[:].rearrange("p a b c -> p (a b c)").bitcast(F32) if t is kst else
                               flat(t[:]).bitcast(F32) if t is qst else flat(t[:])) for name, t in tiles.items()}
        tiles = {
            "xs": tiles["xs"].cut([P, AHEAD, C + 1])[0:CAP],
            "xT": tiles["xs"].cut([P, AHEAD, NC * CAP]),
            "the": tiles["hid"].cut([P, AHEAD, EI])[0:CAP],
            "hid": tiles["hid"].cut([P, AHEAD, EI])[0:CAP],
            "hidT": tiles["small"].cut([P, AHEAD, CAP]),
            "wt": tiles["small"].cut([P, AHEAD])[0:CAP],
            "idx": tiles["small"].cut([P, AHEAD])[0:CAP].bitcast(U32),
            "ye": tiles["ye"].cut([P, AHEAD, C])[0:CAP],
            "x6": tiles["x6"].cut([P, TILES, C]),
            "we": tiles["we"].cut([P, AHEAD, NC * 2 * EI + C]),
            "tiles": tiles,
        }
        experts_in = [ctx.enter_context(nc.semaphore(f"experts_in{q}")) for q in range(AHEAD)]

        def load_experts(sp, done, p):
            for q in range(AHEAD):
                sp.dma_start(tiles["we"][:, q, :], a["we"][AHEAD * p + q]).then_inc(done[q], 16)

        N_LATER = 19 + 1 + NACC
        with ExitStack() as once:
            w_in = sem("w_in")
            ones_set = sem("ones_set")
            stacks_set = sem("stacks_set")
            ones_in = sem("ones_in")
            exp_set = sem("exp_set")
            empty_set = sem("empty_set")
            block = once.enter_context(nc.Block())

            @block.sync
            def _(sp):
                loads = [(hA[:], a["x"][0].rearrange("(j p) c -> p j c", p=P)),
                         (wq[:], a["wq"].rearrange("(k p) n -> p k n", p=P)), (rope[:], a["rope"]), (ident[:], a["ident"]),
                         (wv0[:], a["wv0"].rearrange("(k p) n -> p k n", p=P)),
                         (gs[:], a["gs"]), (us[:], a["us"]), (vecs[:], a["vecs"]), (r1[:, 0, 0:P], a["causal"]),
                         (r2[:, 0, 0:2 * P], a["tri"].rearrange("p a n -> p (a n)")), (tok[:], a["tok"])]
                assert len(loads) == N_LOADS
                for to, src in loads:
                    sp.dma_start(to, src).then_inc(w_in, 16)
                sp.wait_ge(ones_set, 1)
                sp.wait_ge(stacks_set, 2)
                for par in range(2):
                    row = 64 * par + ROWS
                    sp.dma_start(flat(kst[row:row + 2, par, :, :]), ones).then_inc(ones_in, 16)
                sp.wait_ge(ones_in, 32)

            @block.gpsimd
            def _(pool):
                pool.memset(ones, 1.0).then_inc(ones_set, 1)
                pool.memset(mhalf[:], -0.5)
                pool.memset(hBT[:, :, 0:1], 0.0)
                pool.memset(pp[:, :, 0:1], -1e38)
                pool.memset(aa[:, :, 0:1], 0.0)
                pool.memset(bb[:, :, 0:1], 0.0)
                pool.memset(vaug[:], 1.0)
                pool.memset(seen[:], 0.0)

            @block.vector
            def _(dve):
                dve.memset(kst[:].bitcast(F32), 0.0).then_inc(stacks_set, 1)
                dve.memset(qst[:].bitcast(F32), 0.0).then_inc(stacks_set, 1)
                dve.wait_ge(w_in, 16 * N_LOADS)
                dve.tensor_copy(identb[:], ident[:])
                dve.tensor_copy(causal[:], r1[:, 0, 0:P])
                dve.tensor_copy(flat(trib[:]), r2[:, 0, 0:2 * P])
                dve.memset(x2[:], 0.0).then_inc(stacks_set, 1)
                dve.wait_ge(stacks_set, 3)
                dve.tensor_scalar(flat(x2[:])[:, C:C + 1], tok[:, 0:1], float(TILES * P), None, ALU.add).then_inc(empty_set, 1)
                dve.tensor_scalar(ghalf[:], gs[:], 0.5, None, ALU.mult)
                dve.scalar_tensor_tensor(gus[:], gs[:], 0.5, us[:], ALU.mult, ALU.mult)
                dve.wait_ge(exp_set, 1)
                dve.tensor_scalar(decay[:], decay[:], -1.0, None, ALU.mult)

            @block.scalar
            def _(act):
                act.wait_ge(w_in, 16 * N_LOADS)
                act.activation(decay[:], vecs[:, TDEC, :], ACT.Exp).then_inc(exp_set, 1)

        def load_later(sp):
            full = (NI - 1) * P
            loads = [(tile[:], a[name].rearrange("(k p) n -> p k n", p=P)) for tile, name in (
                (wo0, "wo0"), (wgate, "wgate"), (wup, "wup"), (wk1, "wk1"), (wv1, "wv1"), (wr1, "wr1"), (wo1, "wo1"),
                (wck, "wck"), (wcv, "wcv"), (wcr, "wcr"), (wrt, "wrt"), (wsg, "wsg"), (wsu, "wsu"))]
            loads += [(wdown[:, 0:NI - 1, :], a["wdown"][0:full].rearrange("(k p) n -> p k n", p=P)),
                      (wdown[0:ILAST, NI - 1, :], a["wdown"][full:INTER]), (wsd[:], a["wsd"]),
                      (ds[:], a["ds"].partition_broadcast(P)), (biasr[:], a["bias"].partition_broadcast(P)),
                      (slotb[:], a["slotb"])]
            for to, src in loads:
                sp.dma_start(to, src).then_inc(later, 16)
            assert len(loads) + 1 + NACC == N_LATER

        def empty_tables(sp):
            def repeated(src, n):
                return src.rearrange("p (o c) -> p o c", o=1).broadcast_to([P, n, src.shape[1]])
            sp.dma_start(d["slots"].rearrange("(k p) c -> p k c", p=P), repeated(flat(x2[:])[:, 0:ROW], SLOTS // P))\
                .then_inc(later, 16)
            sp.dma_start(d["acc"][0][TILES * P:], x2[:, 2, :]).then_inc(later, 16)
            for i in range(1, NACC):
                sp.dma_start(d["acc"][i].rearrange("(k p) c -> p k c", p=P), repeated(x2[:, 2, :], TILES + 1)).then_inc(later, 16)

        A_link, B_link = sem("A_link"), sem("B_link")
        A_in = sem("A_in")
        A_again = sem("A_again")
        B_x3 = sem("B_x3")
        P_var, P_rs = sem("P_var"), sem("P_rs")
        A_var, A_rs = sem("A_var"), sem("A_rs")
        A_h = sem("A_h")
        A_mm = sem("A_mm")
        A_hT = sem("A_hT")
        A_qk = sem("A_qk")
        A_vaug = sem("A_vaug")
        A_rest = sem("A_rest")
        A_cast = sem("A_cast")
        A_parts = sem("A_parts")
        parts_out = sem("parts_out")
        stack_in = sem("stack_in")
        mx_mm, mx_rd = sem("mx_mm"), sem("mx_rd")
        nm_t, nm_s = sem("nm_t"), sem("nm_s")
        nm_out, nm_in = sem("nm_out"), sem("nm_in")
        sc_mm, sc_exp, sc_msk = sem("sc_mm"), sem("sc_exp"), sem("sc_msk")
        pv_mm, pv_rd = sem("pv_mm"), sem("pv_rd")
        ho_out = [sem(f"ho_out{i}") for i in range(2)]
        att_in = sem("att_in")
        den_in, A_rden = sem("den_in"), sem("A_rden")
        rden_out, rden_in = sem("rden_out"), sem("rden_in")
        A_att = sem("A_att")
        A_wo = sem("A_wo")

        B_var, B_rs = sem("B_var"), sem("B_rs")
        B_h = sem("B_h")
        B_mm = sem("B_mm")
        B_gate, B_hid = sem("B_gate"), sem("B_hid")
        B_down, B_wo, B_cv = sem("B_down"), sem("B_wo"), sem("B_cv")
        B_sg, B_su = sem("B_sg"), sem("B_su")
        B_sc = sem("B_sc")
        B_hT = sem("B_hT")
        B_xs = sem("B_xs")
        B_arg = sem("B_arg")
        B_kv, B_ev = sem("B_kv"), sem("B_ev")
        B_rwkv = sem("B_rwkv")
        B_kf = sem("B_kf")
        B_si = sem("B_si")
        B_x6 = sem("B_x6")
        B_lg = sem("B_lg")
        B_sh = sem("B_sh")
        B_out = sem("B_out")

        C_v = sem("C_v")
        C_s = sem("C_s")
        C_abs, C_log, C_plus = sem("C_abs"), sem("C_log"), sem("C_plus")
        C_mask, C_pos = sem("C_mask"), sem("C_pos")
        C_read = sem("C_read")
        C_idx, C_put = sem("C_idx"), sem("C_put")

        def bank(n):
            return psum[:, 6 + n % 2, :]

        S_GU, S_K, S_V, S_R, S_EXP, S_KF, S_CR, S_SG = 0, 12, 14, 16, 18, 22, 30, 32
        F_T1, F_GU, F_DOWN, F_T2, F_K, F_V, F_R, F_WO, F_T3, F_CK, F_CR, F_CV, F_T4, F_SG, F_SU, F_LG, F_SD = \
            0, 2, 14, 16, 18, 20, 22, 24, 26, 28, 36, 38, 40, 42, 43, 44, 46

        read_off = {}
        for k in range(2):
            for n, (f, at) in enumerate(((F_T1, 0), (F_T2, 2), (F_T3, 4), (F_T4, 6))):
                read_off[f + k] = (B_hT, at + k + 1)
            for f, at in ((F_K, S_K), (F_V, S_V), (F_R, S_R), (F_CR, S_CR)):
                read_off[f + k] = (B_sc, at + k + 1)
            for f, by in ((F_DOWN, B_down), (F_WO, B_wo), (F_CV, B_cv), (F_LG, B_lg), (F_SD, B_sh)):
                read_off[f + k] = (by, k + 1)
        for m in range(NI):
            read_off[F_GU + 2 * m] = (B_gate, m + 1)
            read_off[F_GU + 2 * m + 1] = (B_sc, S_GU + 2 * m + 2)
        for f in range(NF):
            read_off[F_CK + f] = (B_sc, S_KF + f + 1)
        read_off[F_SG], read_off[F_SU] = (B_sg, 1), (B_su, 1)

        def norm_sums(dve, link, src, st, tiles=range(NT)):
            for j in tiles:
                ins = dve.bn_stats(st[:, j, :], src[:, j, :])
            link(ins)

        def norm_stats(dve, link, src, st, mv, ve, var, summed=False, tiles=range(NT)):
            if not summed:
                norm_sums(dve, link, src, st, tiles)
            for j in tiles:
                ins = dve.bn_aggr(mv[:, j, :], st[:, j, :])
            link(ins)
            at = slice(tiles[0], tiles[-1] + 1)
            dve.tensor_scalar(ve[:, at], mv[:, at, 1], EPS, None, ALU.add).then_inc(var, 1)

        def norm_apply(dve, out, src, mv, rs, tiles=range(NT)):
            for j in tiles:
                ins = dve.tensor_scalar(out[:, j, :], src[:, j, :], mv[:, j, 0:1], rs[:, j:j + 1],
                                        ALU.subtract, ALU.mult)
            return ins

        def iteration(project=None, attend=None, bB=None, doC=False, last=False):
            doP, doA, doB = project is not None, attend is not None, bB is not None
            delay = bB == B - 1
            shared = last or doB and not delay
            f_sg, s_sg = (0, 0) if last else (F_SG, S_SG)
            f_su, f_lg, f_sd = f_sg + 1, F_SG if delay else F_LG, 2 if last else F_SD
            free = dict(read_off)
            free.update({f_sg: (B_sg, 1), f_su: (B_su, 1)})
            STEPS, PAIRS = NT * HQ // 2, HQ // 2
            N_DOWN = NT * NI
            DOWN_FROM, DOWN_AFTER = 28, 12
            V_LAG = 12
            RANKS = 12
            LAGS = {"t2": 3, "k": 5, "v": 7, "r": 9, "args": (8, 8, 10, 11)}
            with nc.Block() as block:
                @block.sync
                def _(sp):
                    if last:
                        load_experts(sp, experts_in, 0)
                    if project == 0:
                        load_later(sp)
                    elif doP:
                        sp.dma_start(hA[:], a["x"][bass.ds(project, 1)].rearrange("o (j p) c -> p (o j) c", p=P)).then_inc(A_in, 16)
                    if attend == 0:
                        empty_tables(sp)
                    if doA:
                        sp.wait_ge(nm_s, 1)
                        sp.dma_start(d["negmax"].rearrange("s i h t -> (i h) s t"), nmparts[:]).then_inc(nm_out, 16)
                        sp.wait_ge(nm_out, 16)
                        for par in range(2):
                            for s in range(2):
                                row = 64 * par + ROWS + s
                                src = d["negmax"][s].rearrange("i (j two) t -> two j i t", two=2)[par:par + 1]
                                sp.dma_start(qst[row:row + 1, :, :].rearrange("p j (i t) -> p j i t", t=P), src)\
                                    .then_inc(nm_in, 16)
                        for g in range(HKV):
                            sp.wait_ge(pv_rd, g + 1)
                            sp.dma_start(d["heads"][g], hout[:, g % 2, :]).then_inc(ho_out[g % 2], 16)
                        if doB:
                            sp.wait_ge(B_x3, 1)
                        else:
                            sp.wait_ge(later, 16 * N_LATER)
                        sp.dma_start(x2[:], a["x"][bass.ds(attend, 1)].rearrange("o (j p) c -> p (o j) c", p=P)).then_inc(A_again, 16)
                        for i in range(2):
                            sp.wait_ge(ho_out[i], 16 * HKV // 2)
                        sums = d["heads"].rearrange("g (q r) t -> g q r t", r=32)
                        for g in range(HKV):
                            sp.dma_start(den[16 * g:16 * g + 16, :],
                                         sums[g, :, D, :].rearrange("q (b t) -> q b t", b=4)).then_inc(den_in, 16)
                        for g in range(HKV):
                            rows = slice(32 * (g % 4), 32 * (g % 4) + 32)
                            sp.dma_start(attT[rows, g // 4, :], sums[g, :, 0:D, :]).then_inc(att_in, 16)
                        sp.wait_ge(A_rden, 1)
                        sp.dma_start(d["rden"].rearrange("h (b t) -> (h b) t", b=4), den).then_inc(rden_out, 16)
                        sp.wait_ge(rden_out, 16)
                        for k in range(NC):
                            sp.dma_start(rdenb[:, k, :],
                                         d["rden"].rearrange("(h o) t -> h o t", o=1)[16 * k:16 * k + 16].broadcast_to([16, D, T]))\
                                .then_inc(rden_in, 16)
                    if doP:
                        sp.wait_ge(A_parts, 1)
                        sp.dma_start(d["qparts"].rearrange("s (k p) t -> p (s k) t", p=P),
                                     qparts.rearrange("p s k t -> p (s k) t")).then_inc(parts_out, 16)
                        sp.wait_ge(A_parts, 2)
                        sp.dma_start(d["kparts"].rearrange("s p t -> p s t"), kparts).then_inc(parts_out, 16)
                        sp.wait_ge(parts_out, 32)
                        for par in range(2):
                            for r in range(len(Q_PARTS)):
                                rows = slice(64 * par + D * r, 64 * par + D * r + D)
                                src = d["qparts"][Q_PARTS[r]].rearrange("(j two d) t -> two d j t", two=2, d=D)[par]
                                sp.dma_start(qst[rows, :, :], src).then_inc(stack_in, 16)
                                src = d["kparts"][K_PARTS[r]].rearrange("(g d) t -> d g t", d=D)
                                sp.dma_start(kst[rows, par, :, :], src).then_inc(stack_in, 16)
                        sp.wait_ge(stack_in, 16 * 24)
                    if doB:
                        sp.wait_ge(B_x6, 2)
                        sp.dma_start(d["x6"][bass.ds(bB * NT, NT)].rearrange("j p c -> p j c"), x3[:]).then_inc(B_out, 16)
                    if shared:
                        sp.wait_ge(B_sh, 2)
                        sp.dma_start(d["acc"][0][(B - 1 if last else bB) * T:((B - 1 if last else bB) + 1) * T]
                                     .rearrange("(j p) c -> p j c", p=P), as_tokens(wkv[0])).then_inc(B_out, 16)
                    if doB or last:
                        sp.wait_ge(B_out, 16 * (doB + shared))

                @block.tensor
                def _(pe):
                    def fill(n):
                        if n >= 2:
                            pe.wait_ge(*free[n - 2])
                        return bank(n)

                    def transposed(n, m, src=hB):
                        if m:
                            pe.wait_ge(B_h, m)
                        for k in range(NC):
                            to = fill(n + k)
                            for j in range(NT):
                                ins = pe.transpose(to[:, j * P:(j + 1) * P], src[:, j, k * P:(k + 1) * P], ident[:])
                            ins.then_inc(B_mm, 1)

                    def channels(n, w, rows, cols, src, kt=NC):
                        to = fill(n)
                        for k in range(kt):
                            ins = pe.matmul(to[0:rows, :], w[:, k, cols:cols + rows], src[:, k, :],
                                            start=(k == 0), stop=(k == kt - 1))
                        ins.then_inc(B_mm, 1)

                    def gate_up_product(m, part):
                        cols = P if m < NI - 1 else ILAST
                        up, k = divmod(part, 2)
                        n, w = F_GU + 2 * m + up, (wgate, wup)[up]
                        to = fill(n) if k == 0 else bank(n)
                        ins = pe.matmul(to[0:cols, :], w[:, k, m * P:m * P + cols], hT[:, k, :], start=(k == 0), stop=(k == 1))
                        if k == 1:
                            ins.then_inc(B_mm, 1)

                    def down_product(i):
                        j, k = divmod(i, NI)
                        n = F_DOWN + j // 2
                        if i == 0:
                            pe.wait_ge(B_hid, NI)
                        to = fill(n) if j % 2 == 0 and k == 0 else bank(n)
                        end = P if k < NI - 1 else ILAST
                        ins = pe.matmul(to[:, (j % 2) * C:(j % 2 + 1) * C], big[0:end, k, j * P:(j + 1) * P], wdown[0:end, k, :],
                                        start=(k == 0), stop=(k == NI - 1))
                        if j % 2 and k == NI - 1:
                            ins.then_inc(B_mm, 1)

                    def tokens(n, src, w, kt, width=C, last=P):
                        for half in range(2):
                            to = fill(n + half)
                            for j in range(2):
                                at = (2 * half + j) * P
                                for k in range(kt):
                                    rows = last if k == kt - 1 else P
                                    ins = pe.matmul(to[:, j * width:(j + 1) * width], src[0:rows, k, at:at + P],
                                                    w[0:rows, k, :], start=(k == 0), stop=(k == kt - 1))
                            ins.then_inc(B_mm, 1)

                    def project_to(to, w0, m):
                        for k in range(NC):
                            ins = pe.matmul(psum[0:m, to, :], wq[:, k, w0:w0 + m], hAT[:, k, :],
                                            start=(k == 0), stop=(k == NC - 1))
                        return ins

                    def project_queries():
                        pe.wait_ge(A_h, 1)
                        if doA:
                            pe.wait_ge(sc_exp, 3 * PAIRS)
                        for k in range(NC):
                            for j in range(NT):
                                ins = pe.transpose(psum[:, k, j * P:(j + 1) * P], hA[:, j, k * P:(k + 1) * P], ident[:])
                            ins.then_inc(A_mm, 1)
                        pe.wait_ge(A_hT, 2)
                        for i in range(NC):
                            ins = project_to(2 + i, i * P, P)
                        ins.then_inc(A_mm, 1)
                        for i in range(NC):
                            ins = project_to(i, C + i * P, P)
                        ins.then_inc(A_mm, 1)

                    def project_keys():
                        project_to(4, 2 * C, WQK).then_inc(A_mm, 1)
                        if doA:
                            pe.wait_ge(pv_rd, HKV)
                        project_to(5, 2 * C + WQK, WQK).then_inc(A_mm, 1)
                        pe.wait_ge(A_qk, 1)
                        for j in range(NT):
                            for k in range(NC):
                                ins = pe.matmul(psum[:, 2, j * WQK:(j + 1) * WQK], hAT[:, k, j * P:(j + 1) * P],
                                                wv0[:, k, :], start=(k == 0), stop=(k == NC - 1))
                        ins.then_inc(A_mm, 1)

                    def ranks():
                        pe.wait_ge(C_mask, 1)
                        pe.matmul(psum[:, 0, 2 * P:2 * P + (NT + 1) * E], trib[:, 1, :], flat(before[:]), start=True, stop=True)
                        pe.matmul(psum[:, 0, 2 * P:2 * P + NT * E], trib[:, 0, :], flat(mask_b[:]), start=False, stop=True,
                                  skip_group_check=True).then_inc(C_pos, 1)

                    def scores_for_max(s):
                        j, i = s // NT, s % NT
                        if s >= 3:
                            pe.wait_ge(mx_rd, s - 2)
                        if s == RANKS and doC:
                            ranks()
                        if s == RANKS + 3 and doC:
                            pe.wait_ge(C_read, 2)
                        for par in range(2):
                            to = 2 * (s % 3) + par
                            pe.matmul(psum[:, to, 0:(i + 1) * P], qst[:, j, i * P:(i + 1) * P],
                                      kst[:, par, j // 2, 0:(i + 1) * P], start=True, stop=True)
                            ins = pe.matmul(psum[:, to, i * P:(i + 1) * P], identb[:], causal[:], start=False, stop=True,
                                            skip_group_check=True)
                        ins.then_inc(mx_mm, 1)

                    def scores(m):
                        for par in range(2):
                            if m:
                                pe.wait_ge(sc_exp, 3 * (m - 1) + par + 1)
                            for i in (0, 1, 3):
                                at = 1024 * par + OFFSETS[i]
                                ins = pe.matmul(pflat[:, at:at + T - i * P], kst[:, par, m // 2, i * P:(i + 1) * P],
                                                qst[:, m, i * P:T], start=True, stop=True)
                            ins.then_inc(sc_mm, 1)
                        if m:
                            pe.wait_ge(sc_exp, 3 * m)
                        for par in range(2):
                            ins = pe.matmul(psum[:, 4, 2 * P * par:2 * P * (par + 1)], kst[:, par, m // 2, 2 * P:3 * P],
                                            qst[:, m, 2 * P:T], start=True, stop=True)
                        ins.then_inc(sc_mm, 1)

                    def values(g):
                        if g:
                            pe.wait_ge(pv_rd, g)
                        for i in range(NT):
                            if i in (0, 2):
                                pe.wait_ge(sc_msk, 8 * g + 6 + i)
                            for q in range(GROUP):
                                h = g * GROUP + q
                                at = OFFSETS[i]
                                ins = pe.matmul(psum[32 * q:32 * q + 32, 5, i * P:T], vaug[:, i, g, :],
                                                probs[:, h % NPB, at:at + T - i * P], start=(i == 0), stop=True,
                                                skip_group_check=True)
                        ins.then_inc(pv_mm, 1)

                    hT = hBT[:, :, 1:T + 1]

                    def shared_gate_up():
                        channels(f_sg, wsg, P, 0, hT)
                        channels(f_su, wsu, P, 0, hT)

                    if last:
                        shared_gate_up()
                    if doB:
                        transposed(F_T1, 0)
                        pe.wait_ge(B_hT, 2)
                    for s in range(STEPS):
                        if doA:
                            scores_for_max(s)
                        elif doC and s == RANKS:
                            ranks()
                        if doB and s < 4 * NI:
                            gate_up_product(s // 4, s % 4)
                        elif doB and s >= DOWN_FROM:
                            n = N_DOWN - DOWN_AFTER
                            for i in range(n):
                                if s == DOWN_FROM + i * (STEPS - DOWN_FROM) // n:
                                    down_product(i)
                    if doA:
                        pe.wait_ge(mx_rd, STEPS)
                        pe.transpose(psum[:, 4, 0:P], negmax[:].rearrange("p i h -> p (i h)"), ident[:]).then_inc(nm_t, 1)
                    if doB:
                        for i in range(N_DOWN - DOWN_AFTER, N_DOWN):
                            down_product(i)
                    if doA:
                        pe.wait_ge(nm_in, 64)
                    for m in range(PAIRS):
                        if doA:
                            scores(m)
                            if m % 2 == 0 and m:
                                values(m // 2 - 1)
                        if doB:
                            if m == LAGS["t2"]:
                                transposed(F_T2, 1)
                            for i, (n, w, at) in enumerate(((F_K, wk1, "k"), (F_V, wv1, "v"), (F_R, wr1, "r"))):
                                if m == LAGS[at]:
                                    pe.wait_ge(B_xs, i + 1)
                                    for k in range(NC):
                                        channels(n + k, w, P, k * P, wkv[1 + i])
                    if doA:
                        values(HKV - 1)
                    if doB:
                        pe.wait_ge(B_rwkv, 1)
                        tokens(F_WO, wkv[0], wo1, NC)
                    if doP:
                        project_queries()
                    if doB:
                        transposed(F_T3, 2)
                    if doP:
                        project_keys()
                    if doB:
                        pe.wait_ge(B_xs, 4)
                        for f in range(NF):
                            channels(F_CK + f, wck, P, f * P, wkv[4])
                        pe.wait_ge(B_xs, 5)
                        tokens(F_CR, wkv[5], wcr, NC)
                    if doB:
                        pe.wait_ge(B_kf, NF)
                        tokens(F_CV, big, wcv, NF)
                    if doA:
                        pe.wait_ge(A_att, 1)
                        if not doB:
                            pe.wait_ge(later, 16 * N_LATER)
                        if doP:
                            pe.wait_ge(A_qk, 2)
                        for j in range(NT):
                            for k in range(NC):
                                ins = pe.matmul(psum[:, j // 2, (j % 2) * C:(j % 2 + 1) * C], attT[:, k, j * P:(j + 1) * P],
                                                wo0[:, k, :], start=(k == 0), stop=(k == NC - 1))
                        ins.then_inc(A_wo, 1)
                    if doB:
                        transposed(F_T4, 3, routed)
                        pe.wait_ge(B_hT, 8)
                        if shared:
                            shared_gate_up()
                        tokens(f_lg, hT, wrt, NC, width=E)
                    if shared:
                        pe.wait_ge(B_si, 1)
                        tokens(f_sd, wkv[3][:, 0:1, :], wsd[:].rearrange("p (o c) -> p o c", o=1), 1)

                @block.scalar
                def _(act):
                    def transposed(n, w=None, b=None):
                        for k in range(NC):
                            act.wait_ge(B_mm, n + k + 1)
                            if w is None:
                                act.activation(hBT[:, k, 1:T + 1], bank(n + k), ACT.Copy).then_inc(B_hT, 1)
                            else:
                                act.activation(hBT[:, k, 1:T + 1], bank(n + k), ACT.Identity, scale=vecs[:, w, k:k + 1],
                                               bias=vecs[:, b, k:k + 1]).then_inc(B_hT, 1)

                    def read(n, out, func=ACT.Copy, scale=1.0, rows=P):
                        act.wait_ge(B_mm, n + 1)
                        act.activation(out, bank(n)[0:rows, :], func, scale=scale).then_inc(B_sc, 1)

                    def read_values(g):
                        act.wait_ge(pv_mm, g + 1)
                        if g >= 2:
                            act.wait_ge(ho_out[g % 2], 16 * (g // 2))
                        act.activation(hout[:, g % 2, :], psum[:, 5, :], ACT.Copy).then_inc(pv_rd, 1)

                    def pair_exps(m):
                        at = 2 * m % NPB
                        if 2 * m >= NPB:
                            act.wait_ge(pv_mm, (2 * m - NPB) // GROUP + 1)
                        for par in range(2):
                            act.wait_ge(sc_mm, 3 * m + par + 1)
                            act.activation(probs[:, at + par, 0:OWN], pflat[:, 1024 * par:1024 * par + OWN], ACT.Exp,
                                           scale=SCALE).then_inc(sc_exp, 1)
                        act.wait_ge(sc_mm, 3 * m + 3)
                        act.activation(probs[:, at:at + 2, OWN:REGION], psum[:, 4, :].rearrange("p (h t) -> p h t", h=2),
                                       ACT.Exp, scale=SCALE).then_inc(sc_exp, 1)

                    def cast(n, out, src):
                        act.wait_ge(A_rest, n)
                        act.activation(out, src, ACT.Copy).then_inc(A_cast, 1)

                    if doB:
                        transposed(F_T1)
                    if doC:
                        act.wait_ge(C_abs, 1)
                        act.activation(a1, a0, ACT.Exp, scale=-1.0).then_inc(C_s, 1)
                        act.wait_ge(C_log, 1)
                        act.activation(a0, a2, ACT.Ln).then_inc(C_s, 1)
                    for m in range(NI):
                        if m == 1 and doC:
                            act.wait_ge(C_plus, 1)
                            act.activation(score, a0, ACT.Sqrt).then_inc(C_s, 1)
                        if doB:
                            rows = P if m < NI - 1 else ILAST
                            g, u = F_GU + 2 * m, F_GU + 2 * m + 1
                            if m >= 2:
                                act.wait_ge(B_gate, m - 1)
                            else:
                                act.wait_ge(B_hT, 2)
                            read(g, th[0:rows, m % 2, :], ACT.Tanh, ghalf[0:rows, m:m + 1], rows)
                            if m >= 2:
                                act.wait_ge(B_hid, m - 1)
                            read(u, ut[0:rows, m % 2, :], scale=gus[0:rows, m:m + 1], rows=rows)
                    for m in range(PAIRS):
                        if doA:
                            pair_exps(m)
                            if m % 2 and m > 1:
                                read_values(m // 2 - 1)
                        if doB:
                            if m == LAGS["t2"]:
                                transposed(F_T2, LN1W, LN1B)
                            if m == LAGS["k"]:
                                for k in range(NC):
                                    read(F_K + k, wkv[4][:, k, :])
                            if m == LAGS["v"]:
                                for k in range(NC):
                                    read(F_V + k, wkv[5][:, k, :])
                            if m == LAGS["r"]:
                                for k in range(NC):
                                    read(F_R + k, th[:, k, :], ACT.Tanh, 0.5)
                            for i, t in enumerate((0, 1, 3, 2)):
                                if m == LAGS["args"][i]:
                                    act.wait_ge(B_arg, i + 1)
                                    act.activation(wkv[t], wkv[t], ACT.Exp).then_inc(B_sc, 1)
                    if doA:
                        read_values(HKV - 1)
                    if doP:
                        for k in range(NC):
                            act.wait_ge(A_mm, k + 1)
                            act.activation(hAT[:, k, :], psum[:, k, :], ACT.Copy).then_inc(A_hT, 1)
                    if doB:
                        transposed(F_T3, LN2W, LN2B)
                    if doP:
                        cast(1, qparts[:, 0], r1[:])
                        cast(2, kparts[:, 0], kr1)
                        act.wait_ge(A_mm, 7)
                        act.activation(vaug[:, :, :, 0:D], psum[:, 2, 0:NT * WQK].rearrange("p (j g d) -> p j g d", g=HKV, d=D),
                                       ACT.Copy).then_inc(A_vaug, 1)
                    for f in range(NF):
                        if doB:
                            read(F_CK + f, big[:, f, :], ACT.Relu)
                        if doP and f in (1, 2):
                            cast(2 + f, (qparts[:, 1], kparts[:, 1])[f - 1], (r2[:], kr2)[f - 1])
                    if doB:
                        for k in range(2):
                            read(F_CR + k, th[:, k, :], ACT.Tanh, 0.5)
                        transposed(F_T4)
                    if shared:
                        read(f_sg, th[:, 0, :], ACT.Tanh, 0.5)
                        for k in range(2):
                            act.wait_ge(B_mm, f_sd + k + 1)
                            act.activation(wkv[0][:, k, :], bank(f_sd + k), ACT.Copy).then_inc(B_sh, 1)

                @block.gpsimd
                def _(pool):
                    def deviations(var, n, rs_sem, ve, rs, at=slice(0, NT)):
                        pool.wait_ge(var, n)
                        pool.tensor_tensor(rs[:, at], ve[:, at], mhalf[:, at], ALU.pow).then_inc(rs_sem, 1)

                    def devB(*ns):
                        for n in ns if doB else ():
                            deviations(B_var, n, B_rs, ve2 if n == 3 else veB, rs2 if n == 3 else rsB)

                    def mask(m):
                        for part in range(2):
                            for par in range(2):
                                h = 2 * m % NPB + par
                                if part == 0:
                                    pool.wait_ge(sc_exp, 3 * m + par + 1)
                                    blocks = probs[:, h, 0:1024].rearrange("p (a t) -> p a t", t=512)[:, :, 0:P]
                                else:
                                    pool.wait_ge(sc_exp, 3 * m + 3)
                                    blocks = probs[:, h, 896:1152].rearrange("p (a t) -> p a t", t=P)
                                pool.affine_select(out=blocks, in_=blocks, compare_op=ALU.is_ge, fill=0.0, base=0,
                                                   pattern=[[0, 2], [1, P]], channel_multiplier=-1).then_inc(sc_msk, 1)

                    def hidden(m):
                        rows = P if m < NI - 1 else ILAST
                        pool.wait_ge(B_gate, m + 1)
                        pool.wait_ge(B_sc, S_GU + 2 * m + 2)
                        pool.tensor_tensor(big[0:rows, m, :], big[0:rows, m, :], ut[0:rows, m % 2, :], ALU.mult).then_inc(B_hid, 1)

                    def put_rows(first, last):
                        if first == 0:
                            pool.wait_ge(C_idx, 1)
                        for n in range(first, last):
                            i, k = divmod(n, TOPK)
                            pool.indirect_dma_start(
                                out=d["slots"], out_offset=bass.IndirectOffsetOnAxis(ap=idx[:, i * 8 + k:i * 8 + k + 1], axis=0),
                                in_=routed[:, i, :], in_offset=None, bounds_check=SLOTS - 1, oob_is_err=False)\
                                .then_inc(C_put, 16)

                    for m in range(NI):
                        if doB:
                            hidden(m)
                        if doC and m >= 3:
                            put_rows(4 * (m - 3), 4 * (m - 2) if m < NI - 1 else NT * TOPK)
                    devB(1)
                    for m in range(PAIRS):
                        if m == 2:
                            devB(2, 3)
                        if m == V_LAG and doB:
                            pool.wait_ge(B_sc, S_EXP + 4)
                            pool.wait_ge(B_kv, 1)
                            pool.tensor_tensor(wkv[5], wkv[2], wkv[5], ALU.mult).then_inc(B_ev, 1)
                        if m == 6 and doP:
                            deviations(P_var, 1, P_rs, veP, rsP)
                        if doA:
                            mask(m)
                    devB(4)
                    if doB:
                        for f in range(NF):
                            pool.wait_ge(B_sc, S_KF + f + 1)
                            pool.tensor_tensor(big[:, f, :], big[:, f, :], big[:, f, :], ALU.mult).then_inc(B_kf, 1)
                    for i in range(4 if doB else 0):
                        deviations(B_var, 5 + i, B_rs, veB, rsB, slice(i // 2 * 2, i // 2 * 2 + 2))
                    if doA:
                        deviations(A_var, 1, A_rs, veA, rsA)
                        deviations(B_var, 9 if doB else 1, B_rs, veB, rsB)
                    if doC:
                        pool.wait_ge(C_put, 16 * NT * TOPK)
                        pool.dma_reset(range(C_put.num, C_put.num + 1))

                @block.vector
                def _(dve):
                    linkA, link, linkC = linked(dve, A_link), linked(dve, B_link), linked(dve, C_v)
                    norms = [0]

                    def half_sums(src, half):
                        norm_sums(dve, link, src, stB, range(2 * half, 2 * half + 2))

                    def norm_twice(once, twice, src):
                        norms[0] += 2
                        norm_stats(dve, link, src, stB, mvB, veB, B_var)
                        dve.wait_ge(B_var, norms[0] - 1)
                        link(dve.reciprocal(ve2[:], veB[:]))
                        link(dve.tensor_tensor(ve2[:], ve2[:], mvB[:, :, 1], ALU.mult))
                        dve.tensor_scalar(ve2[:], ve2[:], EPS, None, ALU.add).then_inc(B_var, 1)
                        dve.wait_ge(B_rs, norms[0] - 1)
                        norm_apply(dve, once, src, mvB, rsB)
                        dve.wait_ge(B_rs, norms[0])
                        link(dve.tensor_tensor(rs2[:], rs2[:], rsB[:], ALU.mult))
                        return norm_apply(dve, twice, src, mvB, rs2)

                    def norm(out, src, summed=False, tiles=range(NT)):
                        norms[0] += 1
                        norm_stats(dve, link, src, stB, mvB, veB, B_var, summed, tiles)
                        dve.wait_ge(B_rs, norms[0])
                        return norm_apply(dve, out, src, mvB, rsB, tiles)

                    def two(t, half):
                        return t[:, 2 * half:2 * half + 2, :]

                    def banks(n):
                        return bank(n).rearrange("p (j c) -> p j c", c=C)

                    def rotate_queries():
                        cos = rope[:, 0:1, :].broadcast_to([P, NC, T])
                        sin = rope[:, 1:2, :].broadcast_to([P, NC, T])
                        dve.wait_ge(A_mm, 3)
                        dve.tensor_tensor(r1[:], psum[:, 2:4, :], cos, ALU.mult).then_inc(A_qk, 1)
                        dve.wait_ge(A_mm, 4)
                        dve.tensor_tensor(r2[:], psum[:, 0:2, :], sin, ALU.mult).then_inc(A_qk, 1)
                        dve.wait_ge(A_qk, 2)
                        dve.tensor_tensor(r1[:], r1[:], r2[:], ALU.add).then_inc(A_rest, 1)

                    def rotate_keys():
                        dve.wait_ge(A_mm, 5)
                        dve.tensor_tensor(kr1, psum[0:WQK, 4, :], rope[0:WQK, 0, :], ALU.mult).then_inc(A_qk, 1)
                        dve.wait_ge(A_mm, 6)
                        dve.tensor_tensor(kr2, psum[0:WQK, 5, :], rope[0:WQK, 1, :], ALU.mult).then_inc(A_qk, 1)
                        dve.wait_ge(A_qk, 4)
                        dve.tensor_tensor(kr1, kr1, kr2, ALU.add).then_inc(A_rest, 1)

                    def split():
                        dve.wait_ge(A_cast, 1)
                        dve.tensor_tensor(r2[:], r1[:], qparts[:, 0], ALU.subtract).then_inc(A_rest, 1)
                        dve.wait_ge(A_cast, 2)
                        dve.wait_ge(A_rest, 2)
                        dve.tensor_tensor(kr2, kr1, kparts[:, 0], ALU.subtract).then_inc(A_rest, 1)
                        dve.wait_ge(A_cast, 3)
                        dve.wait_ge(A_rest, 3)
                        dve.tensor_tensor(qparts[:, 2], r2[:], qparts[:, 1], ALU.subtract).then_inc(A_parts, 1)
                        dve.wait_ge(A_cast, 4)
                        dve.wait_ge(A_rest, 4)
                        dve.tensor_tensor(kparts[:, 2], kr2, kparts[:, 1], ALU.subtract).then_inc(A_parts, 1)

                    def invert_sums():
                        dve.wait_ge(den_in, 16 * HKV)
                        dve.reciprocal(den, den).then_inc(A_rden, 1)

                    def maximum(s):
                        j, i = s // NT, s % NT
                        dve.wait_ge(mx_mm, s + 1)
                        to = 2 * (s % 3)
                        dve.tensor_reduce(negmax[:, i, 2 * j:2 * j + 2], psum[:, to:to + 2, 0:(i + 1) * P], AX.X,
                                          ALU.max, negate=True).then_inc(mx_rd, 1)

                    def gate(m):
                        rows = P if m < NI - 1 else ILAST
                        dve.wait_ge(B_sc, S_GU + 2 * m + 1)
                        dve.scalar_tensor_tensor(big[0:rows, m, :], th[0:rows, m % 2, :], 1.0, bank(F_GU + 2 * m)[0:rows, :],
                                                 ALU.add, ALU.mult).then_inc(B_gate, 1)

                    def mixtures(diff, outs):
                        link(dve.tensor_tensor(diff, hBT[:, :, 1:T + 1], hBT[:, :, 0:T], ALU.subtract))
                        for out, vec in outs:
                            for k in range(NC):
                                ins = dve.scalar_tensor_tensor(out[:, k, :], diff[:, k, :], vecs[:, vec, k:k + 1],
                                                               hBT[:, k, 0:T], ALU.mult, ALU.add)
                            ins.then_inc(B_xs, 1)

                    def swiglu_out():
                        for half in range(2):
                            n = F_DOWN + half
                            dve.wait_ge(B_mm, n + 1)
                            dve.tensor_tensor(two(hB, half), banks(n), ds[:].rearrange("p (o c) -> p o c", o=1)
                                              .broadcast_to([P, 2, C]), ALU.mult).then_inc(B_down, 1)
                            dve.wait_ge(B_down, half + 1)
                            half_sums(hB, half)
                        link(norm(hB, hB, summed=True))
                        dve.tensor_tensor(x3[:], x2[:], hB[:], ALU.add).then_inc(B_x3, 1)
                        dve.wait_ge(B_x3, 1)

                    def project_norm():
                        if project:
                            dve.wait_ge(A_in, 16)
                        norm_stats(dve, linkA, hA, stP, mvP, veP, P_var)
                        dve.wait_ge(P_rs, 1)
                        norm_apply(dve, hA, hA, mvP, rsP).then_inc(A_h, 1)

                    def time_mixing():
                        dve.wait_ge(B_hT, 4)
                        mixtures(wkv[0], ((wkv[1], TMK), (wkv[2], TMV), (wkv[3], TMR)))
                        if doP:
                            project_norm()
                        k_, v_ = wkv[4], wkv[5]
                        dve.wait_ge(B_sc, S_K + 2)
                        for k in range(NC):
                            ins = dve.tensor_tensor_scan(pp[:, k, 1:T + 1], decay[:, k:k + 1].broadcast_to([P, T]), k_[:, k, :],
                                                         -1e38, ALU.add, ALU.max)
                        link(ins)
                        old, new = pp[:, :, 0:T], pp[:, :, 1:T + 1]
                        for k in range(NC):
                            ins = dve.scalar_tensor_tensor(wkv[0][:, k, :], old[:, k, :], decay[:, k:k + 1], new[:, k, :],
                                                           ALU.add, ALU.subtract)
                        ins.then_inc(B_arg, 1)
                        dve.tensor_tensor(wkv[1], k_, new, ALU.subtract).then_inc(B_arg, 1)
                        dve.wait_ge(B_mm, F_V + 2)
                        for k in range(NC):
                            ins = dve.scalar_tensor_tensor(wkv[2][:, k, :], k_[:, k, :], vecs[:, TFIRST, k:k + 1], old[:, k, :],
                                                           ALU.add, ALU.max)
                        link(ins)
                        dve.wait_ge(B_mm, F_R + 2)
                        dve.tensor_tensor(wkv[3], old, wkv[2], ALU.subtract).then_inc(B_arg, 1)
                        dve.wait_ge(B_arg, 3)
                        for k in range(NC):
                            ins = dve.scalar_tensor_tensor(wkv[2][:, k, :], k_[:, k, :], vecs[:, TFIRST, k:k + 1],
                                                           wkv[2][:, k, :], ALU.add, ALU.subtract)
                        ins.then_inc(B_arg, 1)
                        dve.wait_ge(B_arg, 4)
                        dve.wait_ge(B_sc, S_EXP + 2)
                        dve.tensor_tensor(k_, wkv[1], v_, ALU.mult).then_inc(B_kv, 1)
                        dve.wait_ge(B_kv, 1)
                        for k in range(NC):
                            dve.tensor_tensor_scan(aa[:, k, 1:T + 1], wkv[0][:, k, :], k_[:, k, :], 0.0, ALU.mult, ALU.add)
                            ins = dve.tensor_tensor_scan(bb[:, k, 1:T + 1], wkv[0][:, k, :], wkv[1][:, k, :], 0.0,
                                                         ALU.mult, ALU.add)
                        link(ins)
                        dve.wait_ge(B_sc, S_EXP + 4)
                        dve.tensor_tensor(wkv[0], wkv[3], aa[:, :, 0:T], ALU.mult)
                        link(dve.tensor_tensor(k_, wkv[3], bb[:, :, 0:T], ALU.mult))
                        dve.wait_ge(B_ev, 1)
                        dve.tensor_tensor(wkv[0], wkv[0], v_, ALU.add)
                        link(dve.tensor_tensor(k_, k_, wkv[2], ALU.add))
                        link(dve.reciprocal(k_, k_))
                        link(dve.scalar_tensor_tensor(k_, th[:], 1.0, k_, ALU.add, ALU.mult))
                        dve.scalar_tensor_tensor(wkv[0], wkv[0], 0.5, k_, ALU.mult, ALU.mult).then_inc(B_rwkv, 1)
                        for half in range(2):
                            n = F_WO + half
                            dve.wait_ge(B_mm, n + 1)
                            dve.tensor_tensor(two(z, half), two(z, half), banks(n), ALU.add).then_inc(B_wo, 1)
                            dve.wait_ge(B_wo, half + 1)
                            half_sums(z, half)

                    def mixing_out():
                        if doC:
                            dve.wait_ge(C_put, 16 * NT * TOPK)
                        link(dve.tensor_copy(routed[:, :, C], tok[:]))
                        link(dve.tensor_scalar(tok[:], tok[:], float(T), None, ALU.add))
                        for half in range(2):
                            n, tiles = F_CV + half, range(2 * half, 2 * half + 2)
                            dve.wait_ge(B_sc, S_CR + half + 1)
                            dve.wait_ge(B_mm, n + 1)
                            dve.scalar_tensor_tensor(two(hB, half), as_tokens(th[:])[:, 2 * half:2 * half + 2, :], 1.0,
                                                     banks(n), ALU.add, ALU.mult).then_inc(B_cv, 1)
                            dve.wait_ge(B_cv, half + 1)
                            link(dve.scalar_tensor_tensor(two(z, half), two(hB, half), 0.5, two(z, half), ALU.mult, ALU.add))
                            link(norm(hB, z, tiles=tiles))
                            dve.tensor_tensor(two(x3, half), two(x3, half), two(hB, half), ALU.add).then_inc(B_x6, 1)
                            dve.wait_ge(B_x6, half + 1)
                            ins = norm(routed[:, :, 0:C], x3, tiles=tiles)
                        ins.then_inc(B_h, 1)

                    def route_start():
                        dve.scalar_tensor_tensor(a0, lg[:], -1.0, lg[:], ALU.mult, ALU.max).then_inc(C_abs, 1)
                        linkC(dve.memset(before[:, 0, :], 0.0))
                        linkC(dve.memset(sel[:, :, E:E + 2], BIG))

                    def route_root():
                        dve.wait_ge(C_s, 1)
                        dve.tensor_scalar(a2, a1, 1.0, None, ALU.add).then_inc(C_log, 1)
                        dve.wait_ge(C_log, 1)
                        linkC(dve.tensor_scalar(a3, a2, -1.0, None, ALU.add))
                        linkC(dve.tensor_scalar(mask, a3, 0.0, None, ALU.is_equal))
                        linkC(dve.tensor_scalar(a3, a3, 1e-30, None, ALU.max))
                        linkC(dve.reciprocal(a3, a3))
                        dve.wait_ge(C_s, 2)
                        linkC(dve.tensor_tensor(a0, a0, a1, ALU.mult))
                        linkC(dve.tensor_tensor(a0, a0, a3, ALU.mult))
                        linkC(dve.tensor_tensor(a1, a1, mask, ALU.mult))
                        linkC(dve.tensor_tensor(a0, a0, a1, ALU.add))
                        dve.scalar_tensor_tensor(a0, lg[:], 0.0, a0, ALU.max, ALU.add).then_inc(C_plus, 1)

                    def route_choose():
                        dve.wait_ge(C_s, 3)
                        linkC(dve.tensor_tensor(sel[:, :, 0:E], score, biasr[:].rearrange("p (o e) -> p o e", o=1)
                                                .broadcast_to(TE), ALU.add))
                        for i in range(NT):
                            ins = dve.max(top[:, i, :], sel[:, i, :])
                        linkC(ins)
                        for i in range(NT):
                            ins = dve.match_replace(out=rep[:, i, :], in_to_replace=top[:, i, :], in_values=sel[:, i, :],
                                                    imm_value=-BIG)
                        linkC(ins)
                        linkC(dve.tensor_scalar(mask, rep[:, :, 0:E], -0.5 * BIG, None, ALU.is_le))
                        linkC(dve.tensor_copy(mask_b[:], mask))
                        for i in range(NT):
                            ins = dve.tensor_tensor(before[:, i + 1, :], before[:, i, :], mask[:, i, :], ALU.add)
                            if i + 1 < NT:
                                linkC(ins)
                        ins.then_inc(C_mask, 1)
                        linkC(dve.tensor_tensor(weight, mask, score, ALU.mult))
                        linkC(dve.tensor_reduce(total, weight, AX.X, ALU.add))
                        linkC(dve.reciprocal(total, total))
                        linkC(dve.scalar_tensor_tensor(weight, weight, 1.5, total.rearrange("p (i o) -> p i o", o=1)
                                                       .broadcast_to(TE), ALU.mult, ALU.mult))

                    def route_slots():
                        dve.wait_ge(C_pos, 1)
                        ranks = psum[:, 0, 2 * P:2 * P + NT * E].rearrange("p (i e) -> p i e", e=E)
                        dve.tensor_tensor(a1, ranks, seen[:].rearrange("p (o e) -> p o e", o=1).broadcast_to(TE), ALU.add)\
                            .then_inc(C_read, 1)
                        dve.wait_ge(C_read, 1)
                        dve.tensor_tensor(seen[:], seen[:], psum[:, 0, 2 * P + NT * E:2 * P + (NT + 1) * E], ALU.add).then_inc(C_read, 1)
                        linkC(dve.scalar_tensor_tensor(valid, a1, float(CAP), mask, ALU.is_lt, ALU.mult))
                        linkC(dve.tensor_tensor(a1, a1, slotb[:].rearrange("p (o e) -> p o e", o=1).broadcast_to(TE), ALU.add))
                        linkC(dve.tensor_tensor(slot, a1, valid, ALU.mult))
                        linkC(dve.tensor_tensor(routed[:, :, C + 1:ROW], weight, valid, ALU.mult))
                        for i in range(NT):
                            ins = dve.max(slot8[:, i, :], slot[:, i, :])
                        linkC(ins)
                        linkC(dve.tensor_scalar(s8, slot8, 0.0, OOB, ALU.is_equal, ALU.mult))
                        linkC(dve.scalar_tensor_tensor(s8, slot8, -1.0, s8, ALU.add, ALU.add))
                        dve.tensor_copy(idx[:], s8.rearrange("p i k -> p (i k)")).then_inc(C_idx, 1)
                        dve.wait_ge(C_idx, 1)

                    def shared_hidden():
                        dve.wait_ge(B_sc, s_sg + 1)
                        si = wkv[3][:, 0, :]
                        dve.scalar_tensor_tensor(si, th[:, 0, :], 1.0, bank(f_sg), ALU.add, ALU.mult).then_inc(B_sg, 1)
                        dve.wait_ge(B_sg, 1)
                        dve.wait_ge(B_mm, f_su + 1)
                        dve.scalar_tensor_tensor(si, si, 0.5, bank(f_su), ALU.mult, ALU.mult).then_inc(B_su, 1)
                        dve.wait_ge(B_su, 1)
                        dve.tensor_scalar(si, si, 10.0, -10.0, ALU.min, ALU.max).then_inc(B_si, 1)

                    def logits():
                        for half in range(2):
                            n = f_lg + half
                            dve.wait_ge(B_mm, n + 1)
                            dve.tensor_copy(two(lg, half), bank(n)[:, 0:2 * E].rearrange("p (j c) -> p j c", c=E))\
                                .then_inc(B_lg, 1)

                    if doC:
                        route_start()
                    for s in range(STEPS):
                        if doA:
                            maximum(s)
                        for at, step in ((1, route_root), (5, route_choose), (RANKS, route_slots)) if doC else ():
                            if s == at:
                                step()
                        if doB and s % 4 == 2 and s // 4 < NI:
                            gate(s // 4)
                    if doA:
                        dve.wait_ge(nm_t, 1)
                        linkA(dve.tensor_copy(nmparts[:, 0, :], psum[:, 4, 0:P]))
                        dve.tensor_tensor(nmparts[:, 1, :], psum[:, 4, 0:P], nmparts[:, 0, :], ALU.subtract).then_inc(nm_s, 1)
                    if doB:
                        swiglu_out()
                        norm_twice(z, hB, x3).then_inc(B_h, 1)
                    if doP and not doB:
                        project_norm()
                    if doB:
                        time_mixing()
                        norm(hB, z, summed=True).then_inc(B_h, 1)
                    if doP:
                        rotate_queries()
                    if doB:
                        dve.wait_ge(B_hT, 6)
                        mixtures(aa[:, :, 1:T + 1], ((wkv[4], CMK), (wkv[5], CMR)))
                    if doA and not doB:
                        invert_sums()
                    if doP:
                        rotate_keys()
                        split()
                    if doA and doB:
                        invert_sums()
                    if doA:
                        dve.wait_ge(att_in, 16 * HKV)
                        dve.wait_ge(rden_in, 16 * NC)
                        dve.tensor_tensor(attT, attT, rdenb[:], ALU.mult).then_inc(A_att, 1)
                    if doB:
                        mixing_out()
                    if doA:
                        dve.wait_ge(A_wo, 1)
                        out = psum[:, 0:2, :].rearrange("p a (j c) -> p (a j) c", c=C)
                        norm_stats(dve, linkA, out, stA, mvA, veA, A_var)
                        dve.wait_ge(A_rs, 1)
                        att = as_tokens(attT)
                        linkA(norm_apply(dve, att, out, mvA, rsA))
                        dve.wait_ge(A_again, 16)
                        linkA(dve.tensor_tensor(x2[:], x2[:], att, ALU.add))
                    if shared:
                        shared_hidden()
                    if doB:
                        logits()
                    if doA:
                        norm(hB, x2)
            nc.multi_engine_barrier(mybir.ALL_ENGINES, sems_to_clear=range(sems[0].num, sems[-1].num + 1))

        iteration(project=0)
        iteration(project=1, attend=0)
        iteration(project=2, attend=1, bB=0)
        iteration(project=3, attend=2, bB=1, doC=True)
        iteration(attend=3, bB=2, doC=True)
        iteration(bB=3, doC=True)
        iteration(doC=True, last=True)
        experts_and_sum(nc, a, d, out, ident, psum, tiles, experts_in)


def experts_and_sum(nc, a, d, out, ident, ps, tiles, e_in):
    xs, xT, the, hid, hidT, wt, idx, ye, x6, we = (tiles[n] for n in (
        "xs", "xT", "the", "hid", "hidT", "wt", "idx", "ye", "x6", "we"))
    scratch = tiles["tiles"]
    with ExitStack() as ctx:
        def sem(name):
            return ctx.enter_context(nc.semaphore(name))

        e_xt, e_xTs, e_gu, e_th, e_g, e_hid, e_ht, e_hTs, e_y, e_ys, e_idx = (sem(n) for n in (
            "e_xt", "e_xTs", "e_gu", "e_th", "e_g", "e_hid", "e_ht", "e_hTs", "e_y", "e_ys", "e_idx"))
        e_put = [sem(f"e_put{i}") for i in range(NACC)]
        ye_free = sem("ye_free")
        x6_in = sem("x6_in")
        x_in = [sem(f"x_in{q}") for q in range(AHEAD)]
        c_in = [sem(f"c_in{g}") for g in range(B)]
        c_v, c_var, c_rs, c_mr = sem("c_v"), sem("c_var"), sem("c_rs"), sem("c_mr")
        c_mh, c_norm, c_out = sem("c_mh"), sem("c_norm"), sem("c_out")
        c_done = [sem("c_done0"), sem("c_done1")]

        place = Scratch(scratch["we"].t)
        cuts = [place.cut([P, NT, C]) for _ in range(NACC * B - 1)] + [scratch["last"].cut([P, NT, C])]
        acc = [[cuts[NACC * g + i] for i in range(NACC)] for g in range(B)]
        small = scratch["norm"]
        st, mv, ve, rs, mr, mh = (small.cut(shape) for shape in (
            [P, TILES, 6], [P, TILES, 2], [P, TILES], [P, TILES], [P, TILES], [P, NT]))
        block = ctx.enter_context(nc.Block())

        def groups():
            return [range(g, g + WIDE) for g in range(0, AHEAD, WIDE)]

        def banks(q):
            return 2 * (q % WIDE), 2 * (q % WIDE) + 1

        def batch(g):
            return slice(g * NT, (g + 1) * NT)

        @block.sync
        def _(sp):
            table = d["slots"].rearrange("(e s) c -> e s c", s=CAP)

            def load_rows(e, q):
                sp.dma_start(xs[:, q, :], table[bass.ds(e, 1), :, 0:C + 1].rearrange("o s c -> (o s) c")).then_inc(x_in[q], 16)

            def load_weights(e, q, weights=True):
                sp.dma_start(wt[:, q:q + 1], table[bass.ds(e, 1), :, bass.ds(e + C + 1, 1)]
                             .rearrange("o s c -> (o s) c"), allow_slow_non_contiguous=True).then_inc(e_in[q], 16)
                if weights:
                    sp.dma_start(we[:, q, :], a["we"][bass.ds(e, 1)].rearrange("o p n -> (o p) n")).then_inc(e_in[q], 16)
            for q in range(AHEAD):
                load_rows(q, q)
            for q in range(AHEAD):
                load_weights(q, q, False)
            with sp.Fori(0, E // AHEAD - 1) as p:
                for group in groups():
                    for q in group:
                        sp.wait_ge(e_xt, p * AHEAD + q + 1)
                        sp.wait_ge(e_idx, p * AHEAD + q + 1)
                        load_rows((p + 1) * AHEAD + q, q)
                    for q in group:
                        sp.wait_ge(e_ys, p * AHEAD + q + 1 + AHEAD)
                        load_weights((p + 1) * AHEAD + q, q)
            sp.dma_start(x6, d["x6"].rearrange("i p c -> p i c")).then_inc(x6_in, 16)
            for i in range(NACC):
                sp.wait_ge(e_put[i], 16 * E // NACC)
            for g in range(B):
                for i in range(NACC):
                    sp.dma_start(acc[g][i], d["acc"][i][g * T:(g + 1) * T].rearrange("(j p) c -> p j c", p=P)).then_inc(c_in[g], 16)
            for g in range(B):
                sp.wait_ge(c_done[g % 2], g // 2 + 1)
                sp.dma_start(out[:, batch(g), :], acc[g][1]).then_inc(c_out, 16)
            sp.wait_ge(c_out, 16 * B)

        @block.tensor
        def _(pe):
            def transpose_rows(n0, loads, group):
                for q in group:
                    pe.wait_ge(x_in[q], loads)
                    pe.wait_ge(e_hTs, n0 + q + 1)
                    for k in range(NC):
                        ins = pe.transpose(ps[:, banks(q)[0], k * CAP:(k + 1) * CAP], xs[:, q, k * P:(k + 1) * P],
                                           ident[0:CAP, 0:CAP])
                    ins.then_inc(e_xt, 1)

            def work(p, following):
                n0 = p * AHEAD
                for group in groups():
                    for q in group:
                        pe.wait_ge(e_ys, n0 + q + 1 + AHEAD - WIDE)
                        pe.wait_ge(e_xTs, n0 + q + 1)
                        pe.wait_ge(e_in[q], n0 * (32 // AHEAD) + 32)
                        for k in range(NC):
                            ins = pe.matmul(ps[0:CAP, banks(q)[1], 0:2 * EI], xT[:, q, k * CAP:(k + 1) * CAP],
                                            we[:, q, k * 2 * EI:(k + 1) * 2 * EI], start=(k == 0), stop=(k == NC - 1))
                        ins.then_inc(e_gu, 1)
                    for q in group:
                        pe.wait_ge(e_hid, n0 + q + 1)
                        pe.transpose(ps[:, banks(q)[0], NC * CAP:(NC + 1) * CAP], hid[:, q, :], ident[0:CAP, 0:CAP]).then_inc(e_ht, 1)
                    if group[0] + WIDE < AHEAD:
                        transpose_rows(n0, n0 * (16 // AHEAD) + 16, range(group[0] + WIDE, group[0] + 2 * WIDE))
                    elif following:
                        transpose_rows(n0 + AHEAD, n0 * (16 // AHEAD) + 32, range(WIDE))
                    for q in group:
                        pe.wait_ge(e_hTs, n0 + q + 1 + WIDE)
                        pe.matmul(ps[0:CAP, banks(q)[1], 2 * EI:2 * EI + C], hidT[:, q, :], we[:, q, NC * 2 * EI:], start=True, stop=True)\
                            .then_inc(e_y, 1)

            transpose_rows(0, 16, range(WIDE))
            with pe.Fori(0, E // AHEAD - 1) as p:
                work(p, True)
            work(E // AHEAD - 1, False)

        @block.scalar
        def _(act):
            act.sem_inc(e_ys, AHEAD)
            act.sem_inc(ye_free, AHEAD)

            def copy_rows(n0, group):
                for q in group:
                    act.wait_ge(e_xt, n0 + q + 1)
                    act.activation(xT[:, q, :], ps[:, banks(q)[0], 0:NC * CAP], ACT.Copy).then_inc(e_xTs, 1)

            def work(p, following):
                n0 = p * AHEAD
                for group in groups():
                    for q in group:
                        act.wait_ge(e_gu, n0 + q + 1)
                        act.activation(the[:, q, :], ps[0:CAP, banks(q)[1], 0:EI], ACT.Tanh, scale=0.5).then_inc(e_th, 1)
                    if group[0] + WIDE < AHEAD:
                        copy_rows(n0, range(group[0] + WIDE, group[0] + 2 * WIDE))
                    elif following:
                        copy_rows(n0 + AHEAD, range(WIDE))
                    for q in group:
                        act.wait_ge(e_y, n0 + q + 1)
                        act.wait_ge(e_in[q], n0 * (32 // AHEAD) + 32)
                        act.wait_ge(ye_free, n0 + q + 1)
                        act.activation(ye[:, q, :], ps[0:CAP, banks(q)[1], 2 * EI:2 * EI + C], ACT.Copy, scale=wt[:, q:q + 1])\
                            .then_inc(e_ys, 1)

            copy_rows(0, range(WIDE))
            with act.Fori(0, E // AHEAD - 1) as p:
                work(p, True)
            work(E // AHEAD - 1, False)
            for g in range(B):
                act.wait_ge(c_mr, g + 1)
                for j in range(NT):
                    i = g * NT + j
                    ins = act.activation(acc[g][1][:, j, :], acc[g][0][:, j, :], ACT.Identity, scale=rs[:, i:i + 1], bias=mr[:, i:i + 1])
                ins.then_inc(c_norm, 1)

        @block.vector
        def _(dve):
            dve.sem_inc(e_hTs, WIDE)
            with dve.Fori(0, E // AHEAD) as p:
                for group in groups():
                    for q in group:
                        dve.wait_ge(x_in[q], p * 16 + 16)
                        dve.wait_ge(ye_free, p * AHEAD + q + 1)
                        dve.tensor_copy(idx[:, q:q + 1], xs[:, q, C:C + 1]).then_inc(e_idx, 1)
                        dve.wait_ge(e_th, p * AHEAD + q + 1)
                        dve.scalar_tensor_tensor(hid[:, q, :], the[:, q, :], 1.0, ps[0:CAP, banks(q)[1], 0:EI], ALU.add, ALU.mult)\
                            .then_inc(e_g, 1)
                        dve.wait_ge(e_g, p * AHEAD + q + 1)
                        dve.scalar_tensor_tensor(hid[:, q, :], hid[:, q, :], 0.5, ps[0:CAP, banks(q)[1], EI:2 * EI], ALU.mult, ALU.mult)\
                            .then_inc(e_hid, 1)
                    for q in group:
                        dve.wait_ge(e_ht, p * AHEAD + q + 1)
                        dve.tensor_copy(hidT[:, q, :], ps[:, banks(q)[0], NC * CAP:(NC + 1) * CAP]).then_inc(e_hTs, 1)
            link = linked(dve, c_v)

            def sums(g):
                dve.wait_ge(c_in[g], 16 * NACC)
                total = acc[g][0]
                link(dve.tensor_tensor(total, total, acc[g][1], ALU.add))
                for j in range(NT):
                    ins = dve.bn_stats(st[:, g * NT + j, :], total[:, j, :])
                link(ins)
                for j in range(NT):
                    ins = dve.bn_aggr(mv[:, g * NT + j, :], st[:, g * NT + j, :])
                link(ins)
                dve.tensor_scalar(ve[:, batch(g)], mv[:, batch(g), 1], EPS, None, ALU.add).then_inc(c_var, 1)

            def shift(g):
                dve.wait_ge(c_rs, g + 1)
                dve.scalar_tensor_tensor(mr[:, batch(g)], mv[:, batch(g), 0], -1.0, rs[:, batch(g)], ALU.mult, ALU.mult).then_inc(c_mr, 1)

            sums(0)
            for g in range(1, B):
                sums(g)
                shift(g - 1)
            shift(B - 1)
            dve.wait_ge(x6_in, 16)
            for g in range(1, B, 2):
                dve.wait_ge(c_norm, g + 1)
                dve.tensor_tensor(acc[g][1], acc[g][1], x6[:, batch(g), :], ALU.add).then_inc(c_done[1], 1)

        @block.gpsimd
        def _(pool):
            pool.memset(mh, -0.5).then_inc(c_mh, 1)
            for e in range(E + NACC):
                if e >= NACC:
                    n = e - NACC
                    pool.wait_ge(e_put[n % NACC], 16 * (n // NACC + 1))
                    pool.sem_inc(ye_free, 1)
                if e < E:
                    q = e % AHEAD
                    pool.wait_ge(e_idx, e + 1)
                    pool.wait_ge(e_ys, e + 1 + AHEAD)
                    pool.indirect_dma_start(
                        out=d["acc"][e % NACC], out_offset=bass.IndirectOffsetOnAxis(ap=idx[:, q:q + 1], axis=0),
                        in_=ye[:, q, :], in_offset=None, bounds_check=(TILES + 1) * P - 1, oob_is_err=True,
                        compute_op=ALU.add).then_inc(e_put[e % NACC], 16)
            pool.wait_ge(c_mh, 1)
            for g in range(B):
                pool.wait_ge(c_var, g + 1)
                pool.tensor_tensor(rs[:, batch(g)], ve[:, batch(g)], mh, ALU.pow).then_inc(c_rs, 1)
                if g == 0:
                    pool.wait_ge(x6_in, 16)
                if g == 1 or g == B - 1:
                    h = g // 2 * 2
                    pool.wait_ge(c_norm, h + 1)
                    pool.tensor_tensor(acc[h][1], acc[h][1], x6[:, batch(h), :], ALU.add).then_inc(c_done[0], 1)

def build(nc, a, out):
    def dram(name, shape, dt=F32):
        return nc.dram_tensor(name, shape, dt).ap()

    d = {
        "qparts": dram("qparts_d", [3, C, T], BF16), "kparts": dram("kparts_d", [3, HKV * D, T], BF16),
        "negmax": dram("negmax_d", [2, NT, HQ, P], BF16), "heads": dram("heads_d", [HKV, P, T]), "rden": dram("rden_d", [HQ, T]),
        "x6": dram("x6_d", [TILES, P, C]), "slots": dram("slots_d", [SLOTS, ROW]),
        "acc": [dram(f"acc{i}_d", [(TILES + 1) * P, C]) for i in range(NACC)],
    }
    with ExitStack() as ctx:
        later = ctx.enter_context(nc.semaphore("later"))
        transformer(nc, a, d, out.rearrange("b (j p) c -> p (b j) c", p=P), later)


def kernel(**inputs):
    import concourse.bacc as bacc
    from concourse.bass_utils import run_bass_kernel_spmd

    g = {k: np.asarray(v) for k, v in inputs.items()}
    swap = np.arange(C) ^ 1

    def turned(w):
        return np.ascontiguousarray(np.swapaxes(w, -1, -2))

    def by_channel(v, n):
        full = np.zeros(n * P, v.dtype)
        full[:v.size] = v.reshape(-1)
        return full.reshape(n, P).T

    wq, wk = g["L0_attn_Wq"], g["L0_attn_Wk"]
    pair = (np.arange(P) % D) // 2
    inv = (np.float32(1.0) / np.float32(10000.0) ** (np.arange(D // 2, dtype=np.float32) / np.float32(D // 2))).astype(np.float32)
    angle = (np.arange(T, dtype=np.float32)[None, :] * inv[pair][:, None]).astype(np.float32)
    sign = np.where(np.arange(P) % 2 == 0, -1.0, 1.0)[:, None]
    rope = np.stack([np.cos(angle), np.sin(angle) * sign], axis=1).astype(np.float32)
    p, t = np.arange(P)[:, None], np.arange(P)[None, :]
    arrays = {
        "x": g["L0_attn_x"],
        "wq": np.concatenate([turned(wq), turned(wq[swap]), turned(wk), turned(wk[swap[:HKV * D]])], axis=1),
        "wv0": turned(g["L0_attn_Wv"]), "wo0": turned(g["L0_attn_Wo"]),
        "wgate": turned(g["L0_ffn_gate_w"]), "wup": turned(g["L0_ffn_up_w"]), "wdown": turned(g["L0_ffn_down_w"]),
        "gs": by_channel(g["L0_ffn_gate_s"], NI), "us": by_channel(g["L0_ffn_up_s"], NI), "ds": g["L0_ffn_down_s"],
        "wk1": turned(g["L1_attn_Wk"]), "wv1": turned(g["L1_attn_Wv"]), "wr1": turned(g["L1_attn_Wr"]),
        "wo1": turned(g["L1_attn_Wo"]), "wck": turned(g["L1_attn_Wck"]), "wcv": turned(g["L1_attn_Wcv"]),
        "wcr": turned(g["L1_attn_Wcr"]), "wrt": turned(g["L1_ffn_gate_w"]), "wsg": turned(g["L1_ffn_sg"]),
        "wsu": turned(g["L1_ffn_su"]), "wsd": turned(g["L1_ffn_sd"]), "bias": g["L1_ffn_bias"],
        "vecs": np.stack([by_channel(g["L1_attn_" + n], NC) for n in (
            "ln1_w", "ln1_b", "ln2_w", "ln2_b", "tm_k", "tm_v", "tm_r", "time_decay", "time_first", "cm_k", "cm_r")], axis=1),
        "we": np.concatenate([np.concatenate([turned(g["L1_ffn_w_gate"]), turned(g["L1_ffn_w_up"])], axis=2)
                              .reshape(E, NC, P, 2 * EI).transpose(0, 2, 1, 3).reshape(E, P, NC * 2 * EI),
                              turned(g["L1_ffn_w_down"])], axis=2),
        "rope": rope,
        "ident": np.eye(P, dtype=np.float32),
        "causal": np.where(t > p, NEG, 0.0).astype(np.float32),
        "tri": np.stack([(p < t), np.ones((P, P))], axis=1).astype(np.float32),
        "slotb": np.broadcast_to((np.arange(E) * CAP + 1.0)[None, :], (P, E)).astype(np.float32),
        "tok": (np.arange(NT)[None, :] * P + np.arange(P)[:, None]).astype(np.float32),
    }
    arrays = {f"in_{k}": np.ascontiguousarray(v) for k, v in arrays.items()}
    nc = bacc.Bacc("TRN2", target_bir_lowering=False, num_devices=1)
    a = {k[3:]: nc.dram_tensor(k, v.shape, mybir.dt.from_np(v.dtype), kind="ExternalInput").ap() for k, v in arrays.items()}
    out = nc.dram_tensor("out", (B, T, C), F32, kind="ExternalOutput").ap()
    build(nc, a, out)
    r = run_bass_kernel_spmd(nc, [arrays], core_ids=[0])
    return r.results[0]["out"]
```
